# Optimizing a Trainium2 kernel written in Bass

```python
import numpy as np
import jax
import jax.numpy as jnp

def _softmax(x, axis=-1):
    return jax.nn.softmax(x, axis=axis)

def _gelu(x):
    return jax.nn.gelu(x, approximate=True)

def _silu(x):
    return jax.nn.silu(x)

def _sigmoid(x):
    return jax.nn.sigmoid(x)

def _layernorm(x, axis=-1, eps=1e-05):
    m = jnp.mean(x, axis=axis, keepdims=True)
    v = jnp.var(x, axis=axis, keepdims=True)
    return (x - m) / jnp.sqrt(v + eps)

def _scatter_add(tgt, idx, src, axis=0):
    return tgt.at[idx].add(src)

def _segment_sum(src, seg, n):
    return jax.ops.segment_sum(src, seg, n)
kernel_name = 'mk_flamingo_gated_d2_seqx_r4_200a46'

def setup_inputs(seed: int=0):
    np.random.seed(seed)
    _w = jnp.asarray

    def _rec_inputs():
        import jax
        import jax.numpy as jnp
        _rk = jax.random.key(seed)
        x = 7.22e-05 + 1 * jax.random.normal(jax.random.fold_in(_rk, 1), (32, 256, 256), jnp.float32)
        _lenS = 256 - jax.random.randint(jax.random.fold_in(_rk, 7), (32,), 0, max(1, 256 // 4) + 1, jnp.int32)
        _lenS2 = 256 - jax.random.randint(jax.random.fold_in(_rk, 8), (32,), 0, max(1, 256 // 4) + 1, jnp.int32)
        _ctx_1024P = jax.random.normal(jax.random.fold_in(_rk, 11), (32, 16, 256), jnp.float32)
        _ctx_1024c = jax.random.dirichlet(jax.random.fold_in(_rk, 511), 0.3 * jnp.ones((16,), jnp.float32), (32, 256))
        _ctx_1024t = jnp.einsum('bsk,bkd->bsd', _ctx_1024c, _ctx_1024P)
        _ctx_1024t = _ctx_1024t * jax.lax.rsqrt(jnp.mean(jnp.square(_ctx_1024t)) + 1e-12) * 0.953939
        ctx_1024 = 4.13588e-05 + 0.999923 * (_ctx_1024t + 0.3 * jax.random.normal(jax.random.fold_in(_rk, 611), (32, 256, 256), jnp.float32))
        _validS = jnp.arange(256)[None, :] < _lenS[:, None]
        _validS2 = jnp.arange(256)[None, :] < _lenS2[:, None]
        _causal = jnp.tril(jnp.ones((256, 256), dtype=bool))
        mask_Bx1xSxS2_if1 = jnp.where(jnp.ones((32, 1, 256, 256), dtype=bool), 1, 0).astype(jnp.int32)
        _g = jax.random.normal(jax.random.fold_in(_rk, 9001), (2, 2), jnp.float32)
        _g = jnp.sign(_g) * jnp.maximum(jnp.abs(_g), 1.0) + (_g == 0) * 1.0
        g_xattn = _g[0]
        g_ffn = _g[1]
        return (x, ctx_1024, mask_Bx1xSxS2_if1, g_xattn, g_ffn)
    x, ctx_1024, mask_Bx1xSxS2_if1, g_xattn, g_ffn = _rec_inputs()

    def _L0_xattn_setup():
        import jax, jax.numpy as jnp
        import numpy as np
        D_MODEL = 256
        HEADS = 16
        D_K = D_MODEL // HEADS
        BS, SEQ = (4, 512)
        key = jax.random.key(seed)
        ks = jax.random.split(key, 12)
        s = 1.0 / np.sqrt(D_MODEL)
        inp = {'q': jax.random.normal(ks[0], (BS, SEQ, D_MODEL), jnp.float32), 'k': jax.random.normal(ks[1], (BS, SEQ, D_MODEL), jnp.float32), 'v': jax.random.normal(ks[2], (BS, SEQ, D_MODEL), jnp.float32), 'mask': jnp.ones((BS, 1, SEQ, SEQ), jnp.int32), 'Wq': jax.random.normal(ks[3], (D_MODEL, D_MODEL), jnp.float32) * s, 'bq': jnp.zeros((D_MODEL,), jnp.float32), 'Wk': jax.random.normal(ks[4], (D_MODEL, D_MODEL), jnp.float32) * s, 'bk': jnp.zeros((D_MODEL,), jnp.float32), 'Wv': jax.random.normal(ks[5], (D_MODEL, D_MODEL), jnp.float32) * s, 'bv': jnp.zeros((D_MODEL,), jnp.float32), 'Wo': jax.random.normal(ks[6], (D_MODEL, D_MODEL), jnp.float32) * s, 'bo': jnp.zeros((D_MODEL,), jnp.float32)}
        return inp
    _L0_xattn_all = _L0_xattn_setup()
    _L0_xattn_in = {k: v for k, v in _L0_xattn_all.items() if k in ('Wq', 'bq', 'Wk', 'bk', 'Wv', 'bv', 'Wo', 'bo')}
    del _L0_xattn_all

    def _L0_ffn_setup():
        import jax, jax.numpy as jnp
        import numpy as np
        EPS = 1e-05

        def rmsnorm(x):
            var = jnp.mean(jnp.square(x), axis=-1, keepdims=True)
            return x * jax.lax.rsqrt(var + 1e-06)

        def activation_quant(x):
            scale = 127.0 / jnp.clip(jnp.max(jnp.abs(x), axis=-1, keepdims=True), EPS, None)
            return jnp.clip(jnp.round(x * scale), -128, 127) / scale

        def weight_quant(w):
            scale = 1.0 / jnp.clip(jnp.mean(jnp.abs(w)), EPS, None)
            return jnp.clip(jnp.round(w * scale), -1, 1) / scale

        def bitlinear(x, w, b):
            xn = rmsnorm(x)
            xq = xn + jax.lax.stop_gradient(activation_quant(xn) - xn)
            wq = w + jax.lax.stop_gradient(weight_quant(w) - w)
            return jnp.einsum('bsi,oi->bso', xq, wq) + b
        key = jax.random.key(seed)
        k1, k2, k3 = jax.random.split(key, 3)
        B, S, D, H = (4, 512, 256, 1024)
        x = jax.random.normal(k1, (B, S, D), dtype=jnp.float32)
        w1 = jax.random.normal(k2, (H, D), dtype=jnp.float32) * D ** (-0.5)
        b1 = jnp.zeros((H,), dtype=jnp.float32)
        w2 = jax.random.normal(k3, (D, H), dtype=jnp.float32) * H ** (-0.5)
        b2 = jnp.zeros((D,), dtype=jnp.float32)
        return {'x': x, 'w1': w1, 'b1': b1, 'w2': w2, 'b2': b2}
    _L0_ffn_all = _L0_ffn_setup()
    _L0_ffn_in = {k: v for k, v in _L0_ffn_all.items() if k in ('w1', 'b1', 'w2', 'b2')}
    del _L0_ffn_all

    def _L1_xattn_setup():
        import jax, jax.numpy as jnp
        import numpy as np
        B, T, D = (8, 512, 256)
        key = jax.random.key(seed)
        kq, kk, kv = jax.random.split(key, 3)
        return {'query': jax.random.normal(kq, (B, T, D), dtype=jnp.float32), 'key': jax.random.normal(kk, (B, T, D), dtype=jnp.float32), 'value': jax.random.normal(kv, (B, T, D), dtype=jnp.float32)}
    _L1_xattn_all = _L1_xattn_setup()
    _L1_xattn_in = {k: v for k, v in _L1_xattn_all.items() if k in ()}
    del _L1_xattn_all

    def _L1_ffn_setup():
        import jax, jax.numpy as jnp
        import numpy as np
        TOP_K = 8
        NUM_EXPERTS = 32
        CAPACITY = 256
        key = jax.random.key(seed)
        k1, k2, k3, k4 = jax.random.split(key, 4)
        B, S, H, E, F = (2, 256, 256, NUM_EXPERTS, 192)
        return {'hidden_states': jax.random.normal(k1, (B, S, H), dtype=jnp.float32), 'gate_weight': jax.random.normal(k2, (E, H), dtype=jnp.float32) * 0.02, 'gate_up_proj': jax.random.normal(k3, (E, 2 * F, H), dtype=jnp.float32) * 0.02, 'down_proj': jax.random.normal(k4, (E, H, F), dtype=jnp.float32) * 0.02}
    _L1_ffn_all = _L1_ffn_setup()
    _L1_ffn_in = {k: v for k, v in _L1_ffn_all.items() if k in ('gate_weight', 'gate_up_proj', 'down_proj')}
    del _L1_ffn_all
    return {'x': x, 'ctx_1024': ctx_1024, 'mask_Bx1xSxS2_if1': mask_Bx1xSxS2_if1, 'g_xattn': g_xattn, 'g_ffn': g_ffn, 'L0_xattn_Wq': _L0_xattn_in['Wq'], 'L0_xattn_bq': _L0_xattn_in['bq'], 'L0_xattn_Wk': _L0_xattn_in['Wk'], 'L0_xattn_bk': _L0_xattn_in['bk'], 'L0_xattn_Wv': _L0_xattn_in['Wv'], 'L0_xattn_bv': _L0_xattn_in['bv'], 'L0_xattn_Wo': _L0_xattn_in['Wo'], 'L0_xattn_bo': _L0_xattn_in['bo'], 'L0_ffn_w1': _L0_ffn_in['w1'], 'L0_ffn_b1': _L0_ffn_in['b1'], 'L0_ffn_w2': _L0_ffn_in['w2'], 'L0_ffn_b2': _L0_ffn_in['b2'], 'L1_ffn_gate_weight': _L1_ffn_in['gate_weight'], 'L1_ffn_gate_up_proj': _L1_ffn_in['gate_up_proj'], 'L1_ffn_down_proj': _L1_ffn_in['down_proj']}

def reference(x, ctx_1024, mask_Bx1xSxS2_if1, g_xattn, g_ffn, L0_xattn_Wq, L0_xattn_bq, L0_xattn_Wk, L0_xattn_bk, L0_xattn_Wv, L0_xattn_bv, L0_xattn_Wo, L0_xattn_bo, L0_ffn_w1, L0_ffn_b1, L0_ffn_w2, L0_ffn_b2, L1_ffn_gate_weight, L1_ffn_gate_up_proj, L1_ffn_down_proj):
    import jax
    import jax.numpy as jnp

    def _L0_xattn_ref(q, k, v, mask, Wq, bq, Wk, bk, Wv, bv, Wo, bo):
        import jax, jax.numpy as jnp
        import numpy as np
        D_MODEL = 256
        HEADS = 16
        D_K = D_MODEL // HEADS
        BS, SEQ = (4, 512)
        bs = q.shape[0]

        def proj(x, W, b):
            y = jnp.einsum('bsd,ed->bse', x, W) + b
            return y.reshape(bs, -1, HEADS, D_K).transpose(0, 2, 1, 3)
        qh, kh, vh = (proj(q, Wq, bq), proj(k, Wk, bk), proj(v, Wv, bv))
        scores = jnp.einsum('bhqd,bhkd->bhqk', qh, kh) / jnp.sqrt(jnp.float32(D_K))
        scores = jnp.where(mask == 0, jnp.float32(-1000000000.0), scores)
        attn = jax.nn.softmax(scores, axis=-1)
        out = jnp.einsum('bhqk,bhkd->bhqd', attn, vh)
        concat = out.transpose(0, 2, 1, 3).reshape(bs, -1, D_MODEL)
        return jnp.einsum('bsd,ed->bse', concat, Wo) + bo

    def _L0_ffn_ref(x, w1, b1, w2, b2):
        import jax, jax.numpy as jnp
        import numpy as np
        EPS = 1e-05

        def rmsnorm(x):
            var = jnp.mean(jnp.square(x), axis=-1, keepdims=True)
            return x * jax.lax.rsqrt(var + 1e-06)

        def activation_quant(x):
            scale = 127.0 / jnp.clip(jnp.max(jnp.abs(x), axis=-1, keepdims=True), EPS, None)
            return jnp.clip(jnp.round(x * scale), -128, 127) / scale

        def weight_quant(w):
            scale = 1.0 / jnp.clip(jnp.mean(jnp.abs(w)), EPS, None)
            return jnp.clip(jnp.round(w * scale), -1, 1) / scale

        def bitlinear(x, w, b):
            xn = rmsnorm(x)
            xq = xn + jax.lax.stop_gradient(activation_quant(xn) - xn)
            wq = w + jax.lax.stop_gradient(weight_quant(w) - w)
            return jnp.einsum('bsi,oi->bso', xq, wq) + b
        h = bitlinear(x, w1, b1)
        h = jax.nn.gelu(h, approximate=False)
        return bitlinear(h, w2, b2)

    def _L1_xattn_ref(query, key, value):
        import jax, jax.numpy as jnp
        import numpy as np
        B, T, D = (8, 512, 256)
        d = query.shape[-1]
        scores = jnp.einsum('bqd,bkd->bqk', query, key) * d ** (-0.5)
        tril = jnp.tril(jnp.ones((query.shape[1], key.shape[1]), dtype=bool))
        scores = jnp.where(tril, scores, -jnp.inf)
        attn = jax.nn.softmax(scores, axis=-1)
        return jnp.einsum('bqk,bkd->bqd', attn, value)

    def _L1_ffn_ref(hidden_states, gate_weight, gate_up_proj, down_proj):
        import jax, jax.numpy as jnp
        import numpy as np
        TOP_K = 8
        NUM_EXPERTS = 32
        CAPACITY = 256
        B, S, H = hidden_states.shape
        E = gate_weight.shape[0]
        N = B * S
        x = hidden_states.reshape(N, H)
        logits = x @ gate_weight.T
        probs = jax.nn.softmax(logits.astype(jnp.float32), axis=-1)
        topw, topi = jax.lax.top_k(probs, TOP_K)
        topw = topw / topw.sum(-1, keepdims=True)
        topw = topw.astype(x.dtype)
        flat_e = topi.reshape(-1)
        flat_w = topw.reshape(-1)
        flat_x = jnp.repeat(x, TOP_K, axis=0)
        oh = jax.nn.one_hot(flat_e, E, dtype=jnp.int32)
        pos = (jnp.cumsum(oh, axis=0) * oh).sum(-1) - 1
        buf = jnp.zeros((E, CAPACITY, H), x.dtype).at[flat_e, pos].set(flat_x, mode='drop')
        gu = jnp.einsum('ech,efh->ecf', buf, gate_up_proj)
        gate, up = jnp.split(gu, 2, axis=-1)
        h = jax.nn.silu(gate) * up
        eo = jnp.einsum('ecf,ehf->ech', h, down_proj)
        tok_out = eo.at[flat_e, pos].get(mode='fill', fill_value=0)
        out = (tok_out * flat_w[:, None]).reshape(N, TOP_K, H).sum(1)
        return out.reshape(B, S, H)
    x = x + jnp.tanh(g_xattn[0]) * _L0_xattn_ref(_layernorm(x, axis=-1), ctx_1024, ctx_1024, mask_Bx1xSxS2_if1, L0_xattn_Wq, L0_xattn_bq, L0_xattn_Wk, L0_xattn_bk, L0_xattn_Wv, L0_xattn_bv, L0_xattn_Wo, L0_xattn_bo)
    x = x + jnp.tanh(g_ffn[0]) * _L0_ffn_ref(_layernorm(x, axis=-1), L0_ffn_w1, L0_ffn_b1, L0_ffn_w2, L0_ffn_b2)
    x = x + jnp.tanh(g_xattn[1]) * _L1_xattn_ref(_layernorm(x, axis=-1), ctx_1024, ctx_1024)
    x = x + jnp.tanh(g_ffn[1]) * _L1_ffn_ref(_layernorm(x, axis=-1), L1_ffn_gate_weight, L1_ffn_gate_up_proj, L1_ffn_down_proj)
    return x

_drawn_inputs = setup_inputs


def setup_inputs(seed=0):
    import zlib

    import numpy as np

    out = dict(_drawn_inputs(seed))
    spreads = {'g_ffn': (-1.0, 0.6),
     'L0_xattn_bq': (0.0, 0.463),
     'L0_xattn_bk': (0.0, 0.8),
     'L0_xattn_bv': (0.0, 0.1),
     'L0_xattn_bo': (0.0, 0.1),
     'L0_ffn_b1': (0.0, 0.1),
     'L0_ffn_b2': (0.0, 0.1)}
    factors = {'L1_ffn_gate_weight': 8.0, 'L1_ffn_gate_up_proj': 8.0, 'L1_ffn_down_proj': 8.0}
    for name, (base, spread) in spreads.items():
        noise = np.random.default_rng([zlib.crc32(name.encode()), seed]).standard_normal(out[name].shape)
        drawn = base * np.exp(spread * noise) if base else spread * noise
        out[name] = jnp.asarray(drawn.astype(out[name].dtype))
    for name, factor in factors.items():
        out[name] = (out[name] * factor).astype(out[name].dtype)
    return out
```

```python
from contextlib import ExitStack

import concourse.bass as bass
from concourse import mybir

F32 = mybir.dt.float32
BF16 = mybir.dt.bfloat16
I32 = mybir.dt.int32
U32 = mybir.dt.uint32
ALU = mybir.AluOpType
ACT = mybir.ActivationFunctionType
AX_X = mybir.AxisListType.X

P = 128
BATCHES = 32
SEQ = 256
D = 256
TILES = SEQ // P
ROW = TILES * D
HEADS = 16
DK = D // HEADS
PAIRS = 6
KROWS = PAIRS * DK
SHIFT = 3
HIDDEN = 1024
EXPERTS = 32
TOPK = 8
CAPACITY = 256
FFN = 192
TOKENS = BATCHES * SEQ
ALL_TILES = TOKENS // P
LN_EPS = 1e-5
RMS_EPS = 1e-6
QUANT_EPS = 1e-5
MASKED = -1e30
ROUND = 12582912.0
Q_PARTS = [0, 0, 1, 1, 0, 2]
K_PARTS = [0, 1, 0, 1, 2, 0]


class Seq:

    def __init__(self, turns, slot, known, count):
        self.turns, self.slot, self.known, self.count = turns, slot, known, count

    def shift(self, k):
        s = self.slot + k
        known = None if self.known is None else self.known + k
        return Seq(self.turns + s // 3, s % 3, known, self.count)

    @property
    def number(self):
        return self.turns * 3 + self.slot

    def exists(self):
        return self.known is None or 0 <= self.known < self.count


def pipeline(eng, step, first, last, steady_first, steady_last, count=BATCHES):
    for n in range(first, steady_first):
        step(Seq(n // 3, n % 3, n, count))
    turns = (steady_last - steady_first + 1) // 3
    with eng.Fori(0, turns, 1) as it:
        for s in range(steady_first, steady_first + 3):
            step(Seq(it + s // 3, s % 3, None, count))
    for n in range(steady_first + 3 * turns, last + 1):
        step(Seq(n // 3, n % 3, n, count))


def phase_semaphores(nc, ctx, prefix):
    made = []

    def clear():
        nc.clear_and_free_semaphores(made)
        nc.all_engine_barrier()

    ctx.callback(clear)

    def sem(name):
        made.append(nc.alloc_semaphore(name=f"{prefix}_{name}"))
        return made[-1]

    return sem


def cross_attention(nc, dram, passed, x_res, gates):
    with ExitStack() as ctx:
        def sb(name, shape, dt=F32):
            return ctx.enter_context(nc.sbuf_tensor(name, shape, dt))

        sem = phase_semaphores(nc, ctx, "x")

        q_stack = [sb(f"q_stack{r}", [KROWS + SHIFT, HEADS, SEQ], BF16) for r in range(3)]
        k_stack = [sb(f"k_stack{r}", [KROWS + SHIFT, HEADS, SEQ], BF16) for r in range(3)]
        ctx_t = [sb(f"ctx_t{r}", [P, 2, SEQ]) for r in range(3)]
        mask_raw = [sb(f"mask_raw{r}", [P, TILES, SEQ], I32) for r in range(3)]
        masked = [sb(f"masked{r}", [P, TILES, SEQ], BF16) for r in range(3)]
        values = [sb(f"values{r}", [P, TILES, HEADS, 32]) for r in range(3)]
        any_masked = [sb(f"any_masked{r}", [1, 1], I32) for r in range(3)]
        masked_cols = sb("masked_cols", [P, 1])
        wq, wk, wv = (sb(n, [P, 2, D]) for n in ("wq", "wk", "wv"))
        wo = sb("wo", [P, 2, D])
        o_bias = sb("o_bias", [P, D])
        qk_bias = sb("qk_bias", [P, 4])
        v_bias = sb("v_bias", [P, D])
        stats = sb("stats", [P, TILES, 6])
        mean_var = sb("mean_var", [P, TILES, 2])
        rstd = sb("rstd", [P, TILES])
        neg_half = sb("neg_half", [P, TILES])
        xn = sb("xn", [P, TILES, D])
        xn_t = sb("xn_t", [P, 2, SEQ])
        full = sb("full", [P, 4, SEQ])
        rest = sb("rest", [P, 4, SEQ])
        parts = sb("parts", [P, 4, 3, SEQ], BF16)
        row_max = sb("row_max", [P, TILES, HEADS])
        max_rest = sb("max_rest", [P, TILES, HEADS])
        max_parts = sb("max_parts", [P, TILES, 3, HEADS], BF16)
        max_rows = sb("max_rows", [3 * HEADS, SEQ], BF16)
        probs = [sb(f"probs{u}", [P, 4, SEQ]) for u in range(2)]
        out_raw = sb("out_raw", [P, 4, SEQ])
        inv_sum = sb("inv_sum", [P, TILES, HEADS])
        heads_out = sb("heads_out", [P, TILES, D])
        heads_t = sb("heads_t", [P, 2, SEQ])
        ident = sb("ident", [P, P])
        ident_b = sb("ident_b", [P, P], BF16)
        ident_mask = sb("ident_mask", [P, 3 * P], BF16)
        ones_col = sb("ones_col", [P, 1])
        ones_b = sb("ones_b", [P, 1], BF16)

        def ps(name, shape, dt=F32):
            return ctx.enter_context(nc.psum_tensor(name, shape, dt))

        ps_max = [ps(f"ps_max{u}", [P, TILES, SEQ]) for u in range(2)]
        ps_exp = [ps(f"ps_exp{u}", [P, 4, SEQ]) for u in range(2)]
        ps_out = ps("ps_out", [P, 2, SEQ])
        ps_misc = ps("ps_misc", [P, 2, SEQ])
        ps_bits = ps_misc[0:3 * HEADS, 0, :].bitcast(BF16)[:, 0:SEQ]

        weights_in = sem("weights_in")
        x_in = [sem(f"x_in{r}") for r in range(3)]
        ctx_in = [sem(f"ctx_in{r}") for r in range(3)]
        mask_in = [sem(f"mask_in{r}") for r in range(3)]
        consts_dve = sem("consts_dve")
        consts_pool = sem("consts_pool")
        stats_done, aggr_done, var_eps, rstd_done, xn_done = (
            sem(n) for n in ("stats_done", "aggr_done", "var_eps", "rstd_done", "xn_done"))
        xnt_ready, xnt_out = sem("xnt_ready"), sem("xnt_out")
        q_ready, q_out, k_ready, k_out = (sem(n) for n in ("q_ready", "q_out", "k_ready", "k_out"))
        rest1, mid, rest_low = sem("rest1"), sem("mid"), sem("rest_low")
        parts_out = [sem(f"parts_out{r}") for r in range(3)]
        stack_in = [sem(f"stack_in{r}") for r in range(3)]
        v_ready, v_out = sem("v_ready"), sem("v_out")
        scores_max, max_done = sem("scores_max"), sem("max_done")
        max_hi, max_mid_rest, max_mid, max_low_rest, max_split = (
            sem(n) for n in ("max_hi", "max_mid_rest", "max_mid", "max_low_rest", "max_split"))
        max_t, max_t_out = sem("max_t"), sem("max_t_out")
        shift_in = [sem(f"shift_in{r}") for r in range(3)]
        scores_exp, exp_done, pv_done = sem("scores_exp"), sem("exp_done"), sem("pv_done")
        out_copied = sem("out_copied")
        nat_ready, inv_done, nat_done = sem("nat_ready"), sem("inv_done"), sem("nat_done")
        heads_ready, heads_out_t = sem("heads_ready"), sem("heads_out_t")
        bias_done = sem("bias_done")
        wo_ready, res_done = sem("wo_ready"), sem("res_done")
        mask_done = sem("mask_done")
        cols_ready, cols_out, count_ready, count_out = (
            sem(n) for n in ("cols_ready", "cols_out", "count_ready", "count_out"))

        FIRST, LAST = -4, BATCHES
        STEADY = (2, BATCHES - 6)
        HEADS_AT = [3, 3, 3, 3, 2, 2, 0, 0]
        HEAD0 = [sum(HEADS_AT[:s]) for s in range(8)]

        def stages(s):
            return s, s.shift(1), s.shift(2), s.shift(3), s.shift(4)

        block = ctx.enter_context(nc.Block())

        @block.sync
        def _(sp):
            for t, name in ((wq, "wq"), (wk, "wk"), (wv, "wv"), (wo, "wo"), (qk_bias, "qk_bias")):
                sp.dma_start(t[:], dram[name]).then_inc(weights_in, 16)
            sp.dma_start(v_bias[:], dram["bv"].partition_broadcast(P)).then_inc(weights_in, 16)
            sp.dma_start(o_bias[:], dram["bo"].partition_broadcast(P)).then_inc(weights_in, 16)

            def load_x(n):
                sp.dma_start(x_res[:, bass.ds(n.number * ROW, ROW)].rearrange("p (t d) -> p t d", t=TILES),
                             dram["x"][bass.ds(n.number, 1)].rearrange("b (t p) d -> p (b t) d", p=P)
                             ).then_inc(x_in[n.slot], 16)

            def load_ctx(n):
                sp.dma_start(ctx_t[n.slot][:], dram["ctx_t"][bass.ds(n.number, 1)].rearrange(
                    "b (c p) k -> p (b c) k", p=P)).then_inc(ctx_in[n.slot], 16)

            def load_mask(n):
                sp.dma_start(mask_raw[n.slot][:], dram["mask"][bass.ds(n.number, 1)].rearrange(
                    "b (t p) k -> p (b t) k", p=P)).then_inc(mask_in[n.slot], 16)

            def step(s):
                a, b, d, c, e = stages(s)
                f = s.shift(5)
                if f.exists():
                    if d.exists():
                        sp.wait_ge(aggr_done, 2 * d.number + 2)
                    load_x(f)
                if e.exists():
                    if b.exists():
                        sp.wait_ge(v_out, 2 * b.number + 2)
                    load_ctx(e)
                if c.exists():
                    if a.exists():
                        sp.wait_ge(mask_done, a.number + 1)
                    load_mask(c)
                    sp.wait_ge(rest_low, 2 * c.number + 2)
                    sp.sem_inc(passed, 1)
                    if a.exists():
                        sp.wait_ge(stack_in[c.slot], 192 * c.turns)
                    for m in range(4):
                        sp.dma_start(dram["parts"][c.slot, m // 2, :, (m % 2) * P:(m % 2 + 1) * P, :]
                                     .rearrange("i p t -> p i t"), parts[:, m]
                                     ).then_inc(parts_out[c.slot], 16)
                if b.exists():
                    sp.wait_ge(max_t_out, b.number + 1)
                    for part in range(SHIFT):
                        sp.dma_start(q_stack[b.slot][KROWS + part:KROWS + part + 1, :, :],
                                     max_rows[part * HEADS:(part + 1) * HEADS, :]
                                     ).then_inc(shift_in[b.slot], 16)
                if c.exists():
                    sp.wait_ge(parts_out[c.slot], 64 * (c.turns + 1))
                    if a.exists():
                        sp.wait_ge(scores_exp, 8 * a.number + 8)
                    for which, stack, order in ((0, q_stack, Q_PARTS), (1, k_stack, K_PARTS)):
                        for group, part in enumerate(order):
                            sp.dma_start(stack[c.slot][group * DK:(group + 1) * DK, :, :],
                                         dram["parts"][c.slot, which, part]
                                         .rearrange("(h d) t -> d h t", d=DK)
                                         ).then_inc(stack_in[c.slot], 16)

            pipeline(sp, step, FIRST - 1, LAST, *STEADY)

        @block.gpsimd
        def _(pool):
            g = nc.gpsimd
            pool.wait_ge(consts_dve, 17)
            for m, fill in ((ident[:], 1.0), (ident_b[:], 1.0), (ident_mask[:, P:2 * P], MASKED)):
                g.affine_select(out=m, in_=m, compare_op=ALU.not_equal, fill=fill, base=0,
                                pattern=[[-1, P]], channel_multiplier=1).then_inc(consts_pool, 1)

            def step(s):
                a, b, d, c, e = stages(s)
                if e.exists():
                    pool.wait_ge(aggr_done, 2 * e.number + 2)
                    pool.sem_inc(passed, 1)
                    g.tensor_scalar(rstd[:], mean_var[:, :, 1], LN_EPS, None, ALU.add
                                    ).then_inc(var_eps, 1)
                    pool.wait_ge(var_eps, e.number + 1)
                    g.tensor_tensor(rstd[:], rstd[:], neg_half[:], ALU.pow).then_inc(rstd_done, 1)
                if d.exists():
                    pool.wait_ge(mask_in[d.slot], 16 * (d.turns + 1))
                    if s.shift(-1).exists():
                        pool.wait_ge(scores_exp, 8 * s.number)
                    pool.sem_inc(passed, 1)
                    g.tensor_scalar(masked[d.slot][:], mask_raw[d.slot][:], 0, None, ALU.is_equal
                                    ).then_inc(mask_done, 1)
                if c.exists():
                    for which, out in ((0, q_out), (1, k_out)):
                        sl = slice(2 * which, 2 * which + 2)
                        pool.wait_ge(out, 4 * c.number + 4)
                        if which == 0 and c.shift(-1).exists():
                            pool.wait_ge(rest_low, 2 * c.number)
                        g.tensor_tensor(rest[:, sl], full[:, sl], parts[:, sl, 0], ALU.subtract
                                        ).then_inc(rest1, 1)
                        pool.wait_ge(mid, 2 * c.number + which + 1)
                        g.tensor_tensor(parts[:, sl, 2], rest[:, sl], parts[:, sl, 1], ALU.subtract
                                        ).then_inc(rest_low, 1)
                if b.exists():
                    pool.wait_ge(max_done, HEADS * b.number + HEADS)
                    if s.exists():
                        pool.wait_ge(max_t, s.number + 1)
                    pool.sem_inc(passed, 1)
                    g.tensor_copy(max_parts[:, :, 0], row_max[:]).then_inc(max_hi, 1)
                    pool.wait_ge(max_hi, b.number + 1)
                    g.tensor_tensor(max_rest[:], row_max[:], max_parts[:, :, 0], ALU.subtract
                                    ).then_inc(max_mid_rest, 1)
                    pool.wait_ge(max_mid_rest, b.number + 1)
                    pool.sem_inc(passed, 1)
                    g.tensor_copy(max_parts[:, :, 1], max_rest[:]).then_inc(max_mid, 1)
                    pool.wait_ge(max_mid, b.number + 1)
                    g.tensor_tensor(max_parts[:, :, 2], max_rest[:], max_parts[:, :, 1], ALU.subtract
                                    ).then_inc(max_split, 1)
                if d.exists():
                    pool.wait_ge(xn_done, 2 * d.number + 2)
                    xs = x_res[:, bass.ds(d.number * ROW, ROW)].rearrange("p (t d) -> p t d", t=TILES)
                    g.tensor_tensor(xs, xs, o_bias[:].unsqueeze(1).to_broadcast([P, TILES, D]), ALU.add
                                    ).then_inc(bias_done, 1)

            pipeline(pool, step, FIRST, LAST, *STEADY)

        @block.vector
        def _(dve):
            v = nc.vector
            v.memset(ident[:], 0.0).then_inc(consts_dve, 1)
            v.memset(ident_b[:], 0.0).then_inc(consts_dve, 1)
            v.memset(ident_mask[:], 0.0).then_inc(consts_dve, 1)
            v.memset(neg_half[:], -0.5).then_inc(consts_dve, 1)
            v.memset(ones_col[:], 1.0).then_inc(consts_dve, 1)
            v.memset(ones_b[:], 1.0).then_inc(consts_dve, 1)
            for r in range(3):
                v.memset(values[r][:], 0.0).then_inc(consts_dve, 1)
            for r in range(3):
                v.memset(k_stack[r][KROWS:KROWS + SHIFT], 1.0).then_inc(consts_dve, 1)
            dve.wait_ge(consts_dve, 12)
            for r in range(3):
                v.memset(values[r][:, :, :, DK:DK + 1], 1.0).then_inc(consts_dve, 1)
            dve.wait_ge(weights_in, 112)
            v.tensor_scalar(qk_bias[:, 0:2], qk_bias[:, 0:2], 0.25, None, ALU.mult).then_inc(consts_dve, 1)

            v.tensor_scalar(o_bias[:], o_bias[:], gates[:, 0:1], None, ALU.mult).then_inc(consts_dve, 1)

            def step(s):
                a, b, d, c, e = stages(s)
                z = s.shift(-1)

                def maxima(slot):
                    if not b.exists():
                        return
                    for h in range(HEAD0[slot], HEAD0[slot] + HEADS_AT[slot]):
                        dve.wait_ge(scores_max, HEADS * b.number + h + 1)
                        if h == 0 and s.exists():
                            dve.wait_ge(max_split, s.number + 1)
                        v.tensor_reduce(row_max[:, :, h], ps_max[h % 2][:], AX_X, ALU.max,
                                        negate=True).then_inc(max_done, 1)

                def normalise(t):
                    if not z.exists():
                        return
                    dve.wait_ge(nat_ready, 2 * z.number + t + 1)
                    if t == 0 and z.shift(-1).exists():
                        dve.wait_ge(heads_ready, z.number)
                    nat = ps_misc[:].rearrange("p g (h k) -> p (g h) k", k=32)
                    v.reciprocal(inv_sum[:, t], nat[:, :, DK]).then_inc(inv_done, 1)
                    dve.wait_ge(inv_done, 2 * z.number + t + 1)
                    v.tensor_tensor(heads_out[:, t].rearrange("p (h k) -> p h k", k=DK),
                                    nat[:, :, 0:DK],
                                    inv_sum[:, t].unsqueeze(2).to_broadcast([P, HEADS, DK]), ALU.mult
                                    ).then_inc(nat_done, 1)

                maxima(0)
                if e.exists():
                    dve.wait_ge(x_in[e.slot], 16 * (e.turns + 1))
                    if c.exists():
                        dve.wait_ge(xn_done, 2 * e.number)
                    dve.sem_inc(passed, 1)
                    for t in range(TILES):
                        v.bn_stats(stats[:, t], x_res[:, bass.ds(e.number * ROW + t * D, D)]
                                   ).then_inc(stats_done, 1)
                    dve.wait_ge(stats_done, 2 * e.number + 2)
                    dve.sem_inc(passed, 1)
                    for t in range(TILES):
                        v.bn_aggr(mean_var[:, t], stats[:, t]).then_inc(aggr_done, 1)
                normalise(0)
                normalise(1)
                maxima(1)
                maxima(2)
                if z.exists():
                    dve.wait_ge(wo_ready, z.number + 1)
                    dve.wait_ge(bias_done, z.number + 1)
                    xs = x_res[:, bass.ds(z.number * ROW, ROW)]
                    v.scalar_tensor_tensor(xs, ps_misc[:].rearrange("p t d -> p (t d)"),
                                           gates[:, 0:1], xs, ALU.mult, ALU.add).then_inc(res_done, 1)
                if e.exists():
                    dve.wait_ge(rstd_done, e.number + 1)
                    if c.exists():
                        dve.wait_ge(xnt_ready, c.number + 1)
                    for t in range(TILES):
                        v.tensor_scalar(xn[:, t], x_res[:, bass.ds(e.number * ROW + t * D, D)],
                                        mean_var[:, t, 0:1], rstd[:, t:t + 1], ALU.subtract, ALU.mult
                                        ).then_inc(xn_done, 1)
                maxima(3)
                if c.exists():
                    dve.wait_ge(rest1, 2 * c.number + 1)
                    v.tensor_copy(parts[:, 0:2, 1], rest[:, 0:2]).then_inc(mid, 1)
                if d.exists():
                    dve.wait_ge(v_ready, d.number + 1)
                    if z.exists():
                        dve.wait_ge(pv_done, 8 * z.number + 8)
                    for t in range(TILES):
                        v.tensor_tensor(values[d.slot][:, t, :, 0:DK],
                                        ps_misc[:, t].rearrange("p (h k) -> p h k", k=DK),
                                        v_bias[:].rearrange("p (h k) -> p h k", k=DK), ALU.add
                                        ).then_inc(v_out, 1)
                maxima(4)
                if c.exists():
                    dve.wait_ge(rest1, 2 * c.number + 2)
                    v.tensor_copy(parts[:, 2:4, 1], rest[:, 2:4]).then_inc(mid, 1)
                if d.exists():
                    dve.wait_ge(cols_ready, d.number + 1)
                    v.tensor_copy(masked_cols[:], ps_misc[:, 0, 0:1]).then_inc(cols_out, 1)
                maxima(5)
                if d.exists():
                    dve.wait_ge(count_ready, d.number + 1)
                    v.tensor_copy(any_masked[d.slot][:], ps_misc[0:1, 0, 0:1]).then_inc(count_out, 1)

            pipeline(dve, step, FIRST, LAST, *STEADY)

        @block.scalar
        def _(act):
            s_ = nc.scalar
            act.wait_ge(weights_in, 112)
            act.wait_ge(consts_dve, 16)

            def step(s):
                a, b, d, c, e = stages(s)

                def exponentials(u):
                    if not a.exists():
                        return
                    act.wait_ge(scores_exp, 8 * a.number + u + 1)
                    if u >= 2 or a.shift(-1).exists():
                        act.wait_ge(pv_done, 8 * a.number + u - 1)
                    s_.activation(probs[u % 2][:], ps_exp[u % 2][:], ACT.Exp).then_inc(exp_done, 1)

                def copy_out(pair):
                    if not a.exists():
                        return
                    act.wait_ge(pv_done, 8 * a.number + 4 * pair + 4)
                    if pair == 0 and a.shift(-1).exists():
                        act.wait_ge(nat_ready, 2 * a.number)
                    s_.copy(out_raw[:, 2 * pair:2 * pair + 2], ps_out[:]).then_inc(out_copied, 1)

                def parts_of(which, ready, out):
                    if not c.exists():
                        return
                    act.wait_ge(ready, c.number + 1)
                    if c.shift(-1).exists():
                        act.wait_ge(rest_low, 2 * c.number)
                        before = c.shift(-1)
                        act.wait_ge(parts_out[before.slot], 64 * (before.turns + 1))
                    scale = 0.25 if which == 0 else 1.0
                    for m in range(2):
                        bias = qk_bias[:, 2 * which + m:2 * which + m + 1]
                        s_.activation(full[:, 2 * which + m], ps_misc[:, m], ACT.Identity, bias=bias,
                                      scale=scale).then_inc(out, 1)
                        s_.activation(parts[:, 2 * which + m, 0], ps_misc[:, m], ACT.Identity,
                                      bias=bias, scale=scale).then_inc(out, 1)

                exponentials(0)
                if c.exists():
                    act.wait_ge(xnt_ready, c.number + 1)
                    if c.shift(-1).exists():
                        act.wait_ge(q_ready, c.number)
                    s_.copy(xn_t[:], ps_misc[:]).then_inc(xnt_out, 1)
                exponentials(1)
                parts_of(0, q_ready, q_out)
                exponentials(2)
                z = s.shift(-1)
                if z.exists():
                    act.wait_ge(heads_ready, z.number + 1)
                    if z.shift(-1).exists():
                        act.wait_ge(wo_ready, z.number)
                    s_.copy(heads_t[:], ps_misc[:]).then_inc(heads_out_t, 1)
                parts_of(1, k_ready, k_out)
                exponentials(3)
                exponentials(4)
                copy_out(0)
                exponentials(5)
                exponentials(6)
                if b.exists():
                    act.wait_ge(max_t, b.number + 1)
                    if s.exists():
                        act.wait_ge(shift_in[s.slot], 48 * (s.turns + 1))
                    s_.copy(max_rows[:], ps_bits).then_inc(max_t_out, 1)
                exponentials(7)
                copy_out(1)

            pipeline(act, step, FIRST, LAST, *STEADY)

        @block.tensor
        def _(pe):
            t_ = nc.tensor
            flag_a = pe.alloc_register("flag_a")
            flag_b = pe.alloc_register("flag_b")
            pe.wait_ge(weights_in, 112)
            pe.wait_ge(consts_dve, 15)
            pe.wait_ge(consts_pool, 3)

            def step(s):
                a, b, d, c, e = stages(s)
                z = s.shift(-1)

                def exp_scores(u, with_mask):
                    if not a.exists():
                        return
                    group, kt = u // 2, u % 2
                    if u == 0:
                        pe.wait_ge(shift_in[a.slot], 48 * (a.turns + 1))
                    if u >= 2 or a.shift(-1).exists():
                        pe.wait_ge(exp_done, 8 * a.number + u - 1)
                    for i in range(4):
                        h = 4 * group + i
                        out = ps_exp[u % 2][:, i]
                        mm = t_.matmul(out, k_stack[a.slot][:, h, kt * P:(kt + 1) * P],
                                       q_stack[a.slot][:, h, :], start=True, stop=not with_mask)
                        if with_mask:
                            for t in range(TILES):
                                mm = t_.matmul(out, masked[a.slot][:, t, kt * P:(kt + 1) * P],
                                               ident_mask[:, (1 - t) * P:(3 - t) * P],
                                               start=False, stop=t == TILES - 1)
                    mm.then_inc(scores_exp, 1)

                def max_scores(slot, with_mask):
                    if not b.exists():
                        return
                    if slot == 0:
                        pe.wait_ge(stack_in[b.slot], 192 * (b.turns + 1))
                    for h in range(HEAD0[slot], HEAD0[slot] + HEADS_AT[slot]):
                        if h >= 2 or s.exists():
                            pe.wait_ge(max_done, HEADS * b.number + h - 1)
                        for t in range(TILES):
                            out = ps_max[h % 2][:, t]
                            mm = t_.matmul(out, q_stack[b.slot][0:KROWS, h, t * P:(t + 1) * P],
                                           k_stack[b.slot][0:KROWS, h, :], start=True,
                                           stop=not with_mask)
                            if with_mask:
                                mm = t_.matmul(out, ident_mask[:, P:2 * P], masked[b.slot][:, t, :],
                                               start=False, stop=True)
                        mm.then_inc(scores_max, 1)

                def weigh_values(u):
                    if not a.exists():
                        return
                    group, kt = u // 2, u % 2
                    pe.wait_ge(exp_done, 8 * a.number + u + 1)
                    if u % 4 == 0 and (u or a.shift(-1).exists()):
                        pe.wait_ge(out_copied, 2 * a.number + u // 4)
                    for i in range(4):
                        mm = t_.matmul(ps_out[32 * i:32 * i + 32, group % 2, :],
                                       values[a.slot][:, kt, 4 * group + i, :], probs[u % 2][:, i, :],
                                       start=kt == 0, stop=kt == 1, skip_group_check=True)
                    mm.then_inc(pv_done, 1)

                def misc(slot):
                    if slot == 0 and c.exists():
                        pe.wait_ge(xn_done, 2 * c.number + 2)
                        if b.exists():
                            pe.wait_ge(count_out, b.number + 1)
                        elif d.exists():
                            pe.wait_ge(k_out, 4 * d.number + 4)
                        for t in range(TILES):
                            for k in range(2):
                                mm = t_.transpose(ps_misc[:, k, t * P:(t + 1) * P],
                                                  xn[:, t, k * P:(k + 1) * P], ident[:])
                        mm.then_inc(xnt_ready, 1)
                    if slot in (0.5, 1) and z.exists():
                        t = int(slot)
                        if t == 1:
                            pe.wait_ge(nat_done, 2 * z.number + 1)
                        else:
                            pe.wait_ge(out_copied, 2 * z.number + 2)
                            if c.exists():
                                pe.wait_ge(xnt_out, c.number + 1)
                            elif b.exists():
                                pe.wait_ge(count_out, b.number + 1)
                            elif s.exists():
                                pe.wait_ge(max_t_out, s.number + 1)
                            else:
                                pe.wait_ge(res_done, z.number)
                        for k in range(4):
                            mm = t_.transpose(ps_misc[:, k // 2, (k % 2) * P:(k % 2 + 1) * P],
                                              out_raw[:, k, t * P:(t + 1) * P], ident[:])
                        mm.then_inc(nat_ready, 1)
                    if slot in (1.5, 2.5) and c.exists():
                        if slot == 1.5:
                            pe.wait_ge(xnt_out, c.number + 1)
                            if z.exists():
                                pe.wait_ge(nat_done, 2 * z.number + 2)
                            w, moving, ready = wq, xn_t, q_ready
                        else:
                            pe.wait_ge(q_out, 4 * c.number + 4)
                            pe.wait_ge(ctx_in[c.slot], 16 * (c.turns + 1))
                            if z.exists():
                                pe.wait_ge(heads_out_t, z.number + 1)
                            w, moving, ready = wk, ctx_t[c.slot], k_ready
                        for m in range(2):
                            for k in range(2):
                                mm = t_.matmul(ps_misc[:, m], w[:, k, m * P:(m + 1) * P],
                                               moving[:, k, :], start=k == 0, stop=k == 1)
                        mm.then_inc(ready, 1)
                    if slot == 2 and z.exists():
                        pe.wait_ge(nat_done, 2 * z.number + 2)
                        if c.exists():
                            pe.wait_ge(q_out, 4 * c.number + 4)
                        for t in range(TILES):
                            for k in range(2):
                                mm = t_.transpose(ps_misc[:, k, t * P:(t + 1) * P],
                                                  heads_out[:, t, k * P:(k + 1) * P], ident[:])
                        mm.then_inc(heads_ready, 1)
                    if slot == 3 and z.exists():
                        pe.wait_ge(heads_out_t, z.number + 1)
                        if c.exists():
                            pe.wait_ge(k_out, 4 * c.number + 4)
                        for t in range(TILES):
                            for k in range(2):
                                mm = t_.matmul(ps_misc[:, t], heads_t[:, k, t * P:(t + 1) * P],
                                               wo[:, k, :], start=k == 0, stop=k == 1)
                        mm.then_inc(wo_ready, 1)
                    if slot == 3.5 and d.exists():
                        pe.wait_ge(ctx_in[d.slot], 16 * (d.turns + 1))
                        if z.exists():
                            pe.wait_ge(res_done, z.number + 1)
                        else:
                            pe.wait_ge(k_out, 4 * c.number + 4)
                        for t in range(TILES):
                            for k in range(2):
                                mm = t_.matmul(ps_misc[:, t], ctx_t[d.slot][:, k, t * P:(t + 1) * P],
                                               wv[:, k, :], start=k == 0, stop=k == 1)
                        mm.then_inc(v_ready, 1)
                    if slot == 4 and d.exists():
                        pe.wait_ge(v_out, 2 * d.number + 2)
                        pe.wait_ge(mask_done, d.number + 1)
                        for n in range(2 * TILES):
                            mm = t_.matmul(ps_misc[:, 0, 0:1],
                                           masked[d.slot][:, n // 2, (n % 2) * P:(n % 2 + 1) * P],
                                           ones_b[:], start=n == 0, stop=n == 2 * TILES - 1)
                        mm.then_inc(cols_ready, 1)
                    if slot == 6 and b.exists():
                        pe.wait_ge(max_split, b.number + 1)
                        if d.exists():
                            pe.wait_ge(cols_out, d.number + 1)
                        elif z.exists():
                            pe.wait_ge(res_done, z.number + 1)
                        pe.sem_inc(passed, 1)
                        for t in range(TILES):
                            mm = t_.transpose(ps_bits[:, t * P:(t + 1) * P],
                                              max_parts[:, t].rearrange("p i h -> p (i h)"), ident_b[:])
                        mm.then_inc(max_t, 1)
                    if slot == 7 and d.exists():
                        pe.wait_ge(cols_out, d.number + 1)
                        if b.exists():
                            pe.wait_ge(max_t_out, b.number + 1)
                        t_.matmul(ps_misc[0:1, 0, 0:1], masked_cols[:], ones_col[:], start=True,
                                  stop=True).then_inc(count_ready, 1)

                def body(with_mask):
                    for slot in range(8):
                        exp_scores(slot, with_mask)
                        misc(slot)
                        max_scores(slot, with_mask)
                        misc(slot + 0.5)
                        if slot:
                            weigh_values(slot - 1)
                    weigh_values(7)

                if a.exists() or b.exists():
                    if b.exists():
                        pe.wait_ge(count_out, b.number + 1)
                        pe.sem_inc(passed, 1)
                        pe.reg_load(flag_b, any_masked[b.slot][0:1, 0:1])
                    if a.exists():
                        pe.reg_load(flag_a, any_masked[a.slot][0:1, 0:1])
                        if b.exists():
                            pe.reg_add(flag_a, flag_a, flag_b)
                        flag = flag_a
                    else:
                        flag = flag_b
                    with pe.If_ne(flag, 0):
                        body(True)
                    with pe.Else():
                        body(False)
                else:
                    body(False)

            pipeline(pe, step, FIRST, LAST, *STEADY)


def ternary_ffn(nc, dram, passed, x_res, gates):
    with ExitStack() as ctx:
        def sb(name, shape, dt=F32):
            return ctx.enter_context(nc.sbuf_tensor(name, shape, dt))

        sem = phase_semaphores(nc, ctx, "f")

        def ps(name, shape, dt=F32):
            return ctx.enter_context(nc.psum_tensor(name, shape, dt))

        KH = HIDDEN // P
        w1 = sb("f_w1", [P, 2 * HIDDEN])
        w2 = sb("f_w2", [P, KH * D])
        w1_q = sb("f_w1_q", [P, 2, HIDDEN], BF16)
        w2_q = sb("f_w2_q", [P, KH, D], BF16)
        b1 = sb("f_b1", [P, HIDDEN])
        b2 = sb("f_b2", [P, D])
        abs_sum = sb("f_abs_sum", [P, 2])
        w_mean = sb("f_w_mean", [P, 2])
        w_inv = sb("f_w_inv", [P, 2])
        out_scale = sb("f_out_scale", [P, 2])
        ones = sb("f_ones", [P, P])
        ident = sb("f_ident", [P, P])
        neg_half = sb("f_neg_half", [P, TILES])
        neg_one = sb("f_neg_one", [P, TILES])
        stats = sb("f_stats", [P, TILES, 6])
        mean_var = sb("f_mean_var", [P, TILES, 2])
        centred = sb("f_centred", [P, TILES, D])
        x_max = sb("f_x_max", [P, TILES])
        chain = sb("f_chain", [P, 8, TILES])
        x_mul = [sb(f"f_x_mul{r}", [P, TILES]) for r in range(3)]
        x_scale = [sb(f"f_x_scale{r}", [P, TILES]) for r in range(3)]
        x_int = sb("f_x_int", [P, TILES, D])
        x_int_t = sb("f_x_int_t", [P, 2, SEQ], BF16)
        h = [sb(f"f_h{r}", [P, TILES, HIDDEN]) for r in range(3)]
        squares = sb("f_squares", [P, HIDDEN], BF16)
        h_sum = sb("f_h_sum", [P, TILES])
        h_max = sb("f_h_max", [P, TILES])
        h_chain = sb("f_h_chain", [P, 4, TILES])
        h_mul = [sb(f"f_h_mul{r}", [P, TILES]) for r in range(3)]
        h_scale = [sb(f"f_h_scale{r}", [P, TILES]) for r in range(3)]
        h_int_t = [sb(f"f_h_int_t{t}", [P, KH, P], BF16) for t in range(TILES)]
        ps_h = [ps(f"f_ps_h{t}", [P, HIDDEN]) for t in range(TILES)]
        ps_x = ps("f_ps_x", [P, 2, SEQ])
        ps_g = ps("f_ps_g", [P, KH, P])
        ps_o = ps("f_ps_o", [P, TILES, D])

        w_in, consts = sem("f_w_in"), sem("f_consts")
        ident_done = sem("f_ident_done")
        w_abs, w_total, w_done = sem("f_w_abs"), sem("f_w_total"), sem("f_w_done")
        stats_done, aggr_done, centred_done, max_done = (
            sem(f"f_{n}") for n in ("stats_done", "aggr_done", "centred_done", "max_done"))
        chain1, x_scaled, bias_done = sem("f_chain1"), sem("f_x_scaled"), sem("f_bias_done")
        x_int_done, x_turned, x_int_out = (sem(f"f_{n}") for n in ("x_int_done", "x_turned", "x_int_out"))
        h_ready, h_done, gelu_done, sum_done, hmax_done = (
            sem(f"f_{n}") for n in ("h_ready", "h_done", "gelu_done", "sum_done", "hmax_done"))
        chain2, h_scaled = sem("f_chain2"), sem("f_h_scaled")
        h_int_done, h_turned, h_int_out, o_ready, res_done = (
            sem(f"f_{n}") for n in ("h_int_done", "h_turned", "h_int_out", "o_ready", "res_done"))

        FIRST, LAST = -2, BATCHES - 1
        STEADY = (2, BATCHES - 3)

        def stages(s):
            return s, s.shift(1), s.shift(2)

        block = ctx.enter_context(nc.Block())

        @block.sync
        def _(sp):
            sp.dma_start(w1[:], dram["w1"].rearrange("p c h -> p (c h)")).then_inc(w_in, 16)
            sp.dma_start(w2[:], dram["w2"].rearrange("p c d -> p (c d)")).then_inc(w_in, 16)
            sp.dma_start(b1[:], dram["b1"].partition_broadcast(P)).then_inc(w_in, 16)
            sp.dma_start(b2[:], dram["b2"].partition_broadcast(P)).then_inc(w_in, 16)
            sp.wait_ge(w_in, 64)

        @block.gpsimd
        def _(pool):
            g = nc.gpsimd
            pool.wait_ge(consts, 4)
            g.affine_select(out=ident[:], in_=ident[:], compare_op=ALU.not_equal, fill=1.0, base=0,
                            pattern=[[-1, P]], channel_multiplier=1).then_inc(ident_done, 1)
            pool.wait_ge(w_done, 12)

            def step(s):
                a, c, e = stages(s)
                if e.exists():
                    pool.wait_ge(aggr_done, 2 * e.number + 2)
                    pool.wait_ge(max_done, e.number + 1)
                    if s.shift(-1).exists():
                        pool.wait_ge(h_done, 2 * s.number)
                    links = 0

                    def link(ins):
                        nonlocal links
                        links += 1
                        ins.then_inc(chain1, 1)
                        pool.wait_ge(chain1, 8 * e.number + links)

                    var, r1, ms, r2, r12 = mean_var[:, :, 1], chain[:, 1], chain[:, 2], chain[:, 3], chain[:, 4]
                    big, inv = chain[:, 5], chain[:, 6]
                    pool.sem_inc(passed, 1)
                    link(g.tensor_scalar(chain[:, 0], var, LN_EPS, None, ALU.add))
                    link(g.tensor_tensor(r1, chain[:, 0], neg_half[:], ALU.pow))
                    link(g.tensor_tensor(ms, var, r1, ALU.mult))
                    link(g.tensor_tensor(ms, ms, r1, ALU.mult))
                    pool.sem_inc(passed, 1)
                    link(g.tensor_scalar(ms, ms, RMS_EPS, None, ALU.add))
                    link(g.tensor_tensor(r2, ms, neg_half[:], ALU.pow))
                    link(g.tensor_tensor(r12, r1, r2, ALU.mult))
                    link(g.tensor_tensor(big, x_max[:], r12, ALU.mult))
                    pool.sem_inc(passed, 1)
                    g.tensor_scalar(big, big, QUANT_EPS, None, ALU.max).then_inc(x_scaled, 1)
                    pool.wait_ge(x_scaled, 5 * e.number + 1)
                    g.tensor_tensor(inv, big, neg_one[:], ALU.pow).then_inc(x_scaled, 1)
                    g.tensor_scalar(x_scale[e.slot][:], big, out_scale[:, 0:1], None, ALU.mult
                                    ).then_inc(x_scaled, 1)
                    pool.wait_ge(x_scaled, 5 * e.number + 3)
                    g.tensor_tensor(inv, inv, r12, ALU.mult).then_inc(x_scaled, 1)
                    pool.wait_ge(x_scaled, 5 * e.number + 4)
                    pool.sem_inc(passed, 1)
                    g.tensor_scalar(x_mul[e.slot][:], inv, 127.0, None, ALU.mult).then_inc(x_scaled, 1)
                    pool.wait_ge(centred_done, 2 * e.number + 2)
                    xs = x_res[:, bass.ds(e.number * ROW, ROW)].rearrange("p (t d) -> p t d", t=TILES)
                    g.tensor_tensor(xs, xs, b2[:].unsqueeze(1).to_broadcast([P, TILES, D]), ALU.add
                                    ).then_inc(bias_done, 1)
                if c.exists():
                    pool.wait_ge(sum_done, 2 * c.number + 2)
                    pool.wait_ge(hmax_done, 2 * c.number + 2)
                    if s.shift(-1).exists():
                        pool.wait_ge(res_done, 2 * s.number)
                    rms, big, inv = h_chain[:, 0], h_chain[:, 1], h_chain[:, 2]
                    n = 6 * c.number
                    pool.sem_inc(passed, 1)
                    g.tensor_scalar(rms, h_sum[:], 1.0 / HIDDEN, RMS_EPS, ALU.mult, ALU.add
                                    ).then_inc(chain2, 1)
                    pool.wait_ge(chain2, n + 1)
                    g.tensor_tensor(rms, rms, neg_half[:], ALU.pow).then_inc(chain2, 1)
                    pool.wait_ge(chain2, n + 2)
                    g.tensor_tensor(big, h_max[:], rms, ALU.mult).then_inc(chain2, 1)
                    pool.wait_ge(chain2, n + 3)
                    pool.sem_inc(passed, 1)
                    g.tensor_scalar(big, big, QUANT_EPS, None, ALU.max).then_inc(chain2, 1)
                    pool.wait_ge(chain2, n + 4)
                    g.tensor_tensor(inv, big, neg_one[:], ALU.pow).then_inc(chain2, 1)
                    pool.wait_ge(chain2, n + 5)
                    g.tensor_tensor(inv, inv, rms, ALU.mult).then_inc(chain2, 1)
                    pool.wait_ge(chain2, n + 6)
                    pool.sem_inc(passed, 1)
                    g.tensor_scalar(h_mul[c.slot][:], inv, 127.0, None, ALU.mult).then_inc(h_scaled, 1)
                    g.tensor_scalar(h_scale[c.slot][:], big, out_scale[:, 1:2], None, ALU.mult
                                    ).then_inc(h_scaled, 1)

            pipeline(pool, step, FIRST, LAST, *STEADY)

        @block.vector
        def _(dve):
            v = nc.vector
            v.memset(ones[:], 1.0).then_inc(consts, 1)
            v.memset(ident[:], 0.0).then_inc(consts, 1)
            v.memset(neg_half[:], -0.5).then_inc(consts, 1)
            v.memset(neg_one[:], -1.0).then_inc(consts, 1)
            dve.wait_ge(w_in, 64)
            for i, w in ((0, w1), (1, w2)):
                v.tensor_reduce(abs_sum[:, i:i + 1], w[:], AX_X, ALU.add,
                                apply_absolute_value=True).then_inc(w_abs, 1)
            dve.wait_ge(w_total, 1)
            v.tensor_scalar(w_mean[:], ps_o[:, 0, 0:2], 1.0 / (HIDDEN * D), QUANT_EPS, ALU.mult, ALU.max
                            ).then_inc(w_done, 1)
            dve.wait_ge(w_done, 1)
            v.reciprocal(w_inv[:], w_mean[:]).then_inc(w_done, 1)
            v.tensor_scalar(out_scale[:], w_mean[:], 1.0 / 127.0, None, ALU.mult).then_inc(w_done, 1)
            dve.wait_ge(w_done, 3)
            v.tensor_scalar(out_scale[:, 1:2], out_scale[:, 1:2], gates[:, 2:3], None, ALU.mult
                            ).then_inc(w_done, 1)
            v.tensor_scalar(b2[:], b2[:], gates[:, 2:3], None, ALU.mult).then_inc(w_done, 1)
            n = 5
            for i, w, q in ((0, w1, w1_q), (1, w2, w2_q)):
                flat = q[:].rearrange("p c n -> p (c n)")
                v.tensor_scalar(w[:], w[:], w_inv[:, i:i + 1], ROUND, ALU.mult, ALU.add).then_inc(w_done, 1)
                dve.wait_ge(w_done, n + 1)
                v.tensor_scalar(w[:], w[:], ROUND, 1.0, ALU.subtract, ALU.min).then_inc(w_done, 1)
                dve.wait_ge(w_done, n + 2)
                v.tensor_scalar(flat, w[:], -1.0, None, ALU.max).then_inc(w_done, 1)
                n += 3
            v.memset(squares[:], 0.0).then_inc(w_done, 1)
            dve.wait_ge(w_done, 12)

            def step(s):
                a, c, e = stages(s)

                def quantise_h(t):
                    if a.exists():
                        dve.wait_ge(h_scaled, 2 * a.number + 2)
                        hs = h[a.slot][:, t]
                        v.tensor_scalar(hs, hs, h_mul[a.slot][:, t:t + 1], ROUND, ALU.mult, ALU.add
                                        ).then_inc(h_int_done, 1)

                def hidden(t):
                    if c.exists():
                        dve.wait_ge(h_ready, 2 * c.number + t + 1)
                        if s.shift(-2).exists():
                            dve.wait_ge(h_turned, 2 * s.number - 2)
                        v.scalar_tensor_tensor(h[c.slot][:, t], ps_h[t][:], x_scale[c.slot][:, t:t + 1],
                                               b1[:], ALU.mult, ALU.add).then_inc(h_done, 1)

                if c.exists():
                    dve.wait_ge(x_scaled, 5 * c.number + 5)
                    if a.exists():
                        dve.wait_ge(x_turned, a.number + 1)
                    for t in range(TILES):
                        v.tensor_scalar(x_int[:, t], centred[:, t], x_mul[c.slot][:, t:t + 1], ROUND,
                                        ALU.mult, ALU.add).then_inc(x_int_done, 1)
                quantise_h(0)
                hidden(0)
                quantise_h(1)
                hidden(1)
                if e.exists():
                    def x_tile(t):
                        return x_res[:, bass.ds(e.number * ROW + t * D, D)]

                    if c.exists():
                        dve.wait_ge(x_scaled, 5 * e.number)
                        dve.wait_ge(x_int_done, 2 * e.number)
                    dve.sem_inc(passed, 1)
                    for t in range(TILES):
                        v.bn_stats(stats[:, t], x_tile(t)).then_inc(stats_done, 1)
                    dve.wait_ge(stats_done, 2 * e.number + 2)
                    dve.sem_inc(passed, 1)
                    for t in range(TILES):
                        v.bn_aggr(mean_var[:, t], stats[:, t]).then_inc(aggr_done, 1)
                    dve.wait_ge(aggr_done, 2 * e.number + 2)
                    for t in range(TILES):
                        v.tensor_scalar(centred[:, t], x_tile(t), mean_var[:, t, 0:1], None,
                                        ALU.subtract).then_inc(centred_done, 1)
                    dve.wait_ge(centred_done, 2 * e.number + 2)
                    v.tensor_reduce(x_max[:], centred[:], AX_X, ALU.max, apply_absolute_value=True
                                    ).then_inc(max_done, 1)
                if c.exists():
                    for t in range(TILES):
                        dve.wait_ge(gelu_done, 2 * c.number + t + 1)
                        if a.exists():
                            dve.wait_ge(h_scaled, 2 * a.number + 2)
                        v.tensor_reduce(h_max[:, t:t + 1], h[c.slot][:, t], AX_X, ALU.max,
                                        apply_absolute_value=True).then_inc(hmax_done, 1)
                if a.exists():
                    dve.wait_ge(bias_done, a.number + 1)
                    for t in range(TILES):
                        dve.wait_ge(o_ready, 2 * a.number + TILES)
                        xs = x_res[:, bass.ds(a.number * ROW + t * D, D)]
                        v.scalar_tensor_tensor(xs, ps_o[:, t], h_scale[a.slot][:, t:t + 1], xs,
                                               ALU.mult, ALU.add).then_inc(res_done, 1)

            pipeline(dve, step, FIRST, LAST, *STEADY)

        @block.scalar
        def _(act):
            s_ = nc.scalar
            act.wait_ge(w_done, 12)

            def step(s):
                a, c, e = stages(s)

                def turned_h(t):
                    if a.exists():
                        act.wait_ge(h_turned, 2 * a.number + t + 1)
                        if s.shift(-1).exists():
                            act.wait_ge(o_ready, 2 * a.number)
                        s_.activation(h_int_t[t][:], ps_g[:], ACT.Copy, bias=-ROUND).then_inc(h_int_out, 1)

                def gelu(t):
                    if c.exists():
                        hs = h[c.slot][:, t]
                        act.wait_ge(h_done, 2 * c.number + t + 1)
                        s_.activation(hs, hs, ACT.Gelu).then_inc(gelu_done, 1)
                        act.wait_ge(gelu_done, 2 * c.number + t + 1)
                        if a.exists():
                            act.wait_ge(h_scaled, 2 * a.number + 2)
                        if t or a.exists():
                            act.wait_ge(sum_done, 2 * c.number + t)
                        s_.activation(squares[:], hs, ACT.Square, accum_out=h_sum[:, t:t + 1]
                                      ).then_inc(sum_done, 1)

                if c.exists():
                    act.wait_ge(x_turned, c.number + 1)
                    if a.exists():
                        act.wait_ge(h_ready, 2 * c.number)
                    s_.activation(x_int_t[:], ps_x[:], ACT.Copy, bias=-ROUND).then_inc(x_int_out, 1)
                turned_h(0)
                gelu(0)
                turned_h(1)
                gelu(1)

            pipeline(act, step, FIRST, LAST, *STEADY)

        @block.tensor
        def _(pe):
            t_ = nc.tensor
            pe.wait_ge(w_abs, 2)
            pe.wait_ge(consts, 4)
            t_.matmul(ps_o[:, 0, 0:2], ones[:], abs_sum[:], start=True, stop=True).then_inc(w_total, 1)
            pe.wait_ge(ident_done, 1)
            pe.wait_ge(w_done, 12)

            def step(s):
                a, c, e = stages(s)

                def first(t):
                    if c.exists():
                        if t == 0:
                            pe.wait_ge(x_int_out, c.number + 1)
                            if a.exists():
                                pe.wait_ge(h_done, 2 * c.number)
                        for half in range(2):
                            for k in range(2):
                                mm = t_.matmul(ps_h[t][:, half * 512:half * 512 + 512],
                                               x_int_t[:, k, t * P:(t + 1) * P],
                                               w1_q[:, k, half * 512:half * 512 + 512],
                                               start=k == 0, stop=k == 1)
                        mm.then_inc(h_ready, 1)

                def turn(t):
                    if a.exists():
                        pe.wait_ge(h_int_done, 2 * a.number + t + 1)
                        if t or s.shift(-1).exists():
                            pe.wait_ge(h_int_out, 2 * a.number + t)
                        for k in range(KH):
                            mm = t_.transpose(ps_g[:, k], h[a.slot][:, t, k * P:(k + 1) * P], ident[:])
                        mm.then_inc(h_turned, 1)

                def second(t):
                    if a.exists():
                        pe.wait_ge(h_int_out, 2 * a.number + t + 1)
                        if t == 0 and s.shift(-1).exists():
                            pe.wait_ge(res_done, 2 * a.number)
                        for k in range(KH):
                            mm = t_.matmul(ps_o[:, t], h_int_t[t][:, k], w2_q[:, k],
                                           start=k == 0, stop=k == KH - 1)
                        mm.then_inc(o_ready, 1)

                if c.exists():
                    pe.wait_ge(x_int_done, 2 * c.number + 2)
                    for t in range(TILES):
                        for k in range(2):
                            mm = t_.transpose(ps_x[:, k, t * P:(t + 1) * P],
                                              x_int[:, t, k * P:(k + 1) * P], ident[:])
                    mm.then_inc(x_turned, 1)
                first(0)
                turn(0)
                first(1)
                second(0)
                turn(1)
                second(1)

            pipeline(pe, step, FIRST, LAST, *STEADY)


def causal_attention(nc, dram, passed, x_res, gates, logits, out):
    with ExitStack() as ctx:
        def sb(name, shape, dt=F32):
            return ctx.enter_context(nc.sbuf_tensor("c_" + name, shape, dt))

        sem = phase_semaphores(nc, ctx, "c")

        def ps(name, shape, dt=F32):
            return ctx.enter_context(nc.psum_tensor("c_" + name, shape, dt))

        KEYS = P + SEQ
        ctx_t = [sb(f"ctx_t{r}", [P, 2, SEQ]) for r in range(3)]
        ctx_n = [sb(f"ctx_n{r}", [P, TILES, D]) for r in range(3)]
        gate_w = sb("gate_w", [P, 2, EXPERTS])
        ident = sb("ident", [P, P])
        causal = sb("causal", [P, KEYS])
        zero_row = sb("zero_row", [1, D + EXPERTS])
        neg_half = sb("neg_half", [P, TILES])
        stats = sb("stats", [P, 2, TILES, 6])
        mean_var = sb("mean_var", [P, 2, TILES, 2])
        rstd = sb("rstd", [P, 2, TILES])
        xn = sb("xn", [P, TILES, D])
        xn_t = sb("xn_t", [P, 2, SEQ])
        scores = sb("scores", [P, KEYS])
        neg_max = sb("neg_max", [P, TILES])
        probs = [sb(f"probs{r}", [P, KEYS]) for r in range(3)]
        sums = [sb(f"sums{r}", [P, TILES]) for r in range(3)]
        inv = sb("inv", [P, TILES])
        probs_t = sb("probs_t", [P, KEYS])
        y = [sb(f"y{r}", [P, TILES, D]) for r in range(3)]
        y_t = sb("y_t", [P, 2, SEQ])
        ps_x = ps("ps_x", [P, 2, SEQ])
        ps_s = ps("ps_s", [P, 512])
        ps_p = ps("ps_p", [P, 512])
        ps_v = ps("ps_v", [P, TILES, D])
        ps_y = ps("ps_y", [P, 2, SEQ])
        ps_l = ps("ps_l", [P, TILES, EXPERTS])

        w_in, consts, pool_consts = sem("w_in"), sem("consts"), sem("pool_consts")
        ctx_t_in = [sem(f"ctx_t_in{r}") for r in range(3)]
        ctx_n_in = [sem(f"ctx_n_in{r}") for r in range(3)]
        stats1, aggr1, rstd1, xn_done = sem("stats1"), sem("aggr1"), sem("rstd1"), sem("xn_done")
        stats2, aggr2, rstd2, y_done = sem("stats2"), sem("aggr2"), sem("rstd2"), sem("y_done")
        x_turned, x_out, s_ready, s_done = sem("x_turned"), sem("x_out"), sem("s_ready"), sem("s_done")
        max_done, exp_done = sem("max_done"), sem("exp_done")
        p_turned, p_out, v_ready = sem("p_turned"), sem("p_out"), sem("v_ready")
        inv_done, res_done = sem("inv_done"), sem("res_done")
        y_turned, y_out, l_ready, l_out = sem("y_turned"), sem("y_out"), sem("l_ready"), sem("l_out")
        table_out = [sem(f"table_out{r}") for r in range(3)]
        result_out = [sem(f"result_out{r}") for r in range(3)]
        zero_out = sem("zero_out")

        FIRST, LAST = -2, BATCHES
        STEADY = (4, BATCHES - 3)

        def stages(s):
            return s, s.shift(1), s.shift(2), s.shift(-1)

        def tile(n, t):
            return x_res[:, bass.ds(n.number * ROW + t * D, D)]

        block = ctx.enter_context(nc.Block())

        @block.sync
        def _(sp):
            sp.dma_start(gate_w[:], dram["gate_w"]).then_inc(w_in, 16)
            sp.wait_ge(consts, 3)
            sp.dma_start(dram["table"][0:1, :], zero_row[:]).then_inc(zero_out, 16)

            def step(s):
                a, c, e, z = stages(s)
                if e.exists():
                    if z.exists():
                        sp.wait_ge(s_ready, z.number + 1)
                        sp.wait_ge(v_ready, z.number + 1)
                    sp.dma_start(ctx_t[e.slot][:], dram["ctx_t"][bass.ds(e.number, 1)].rearrange(
                        "b (c p) k -> p (b c) k", p=P)).then_inc(ctx_t_in[e.slot], 16)
                    sp.dma_start(ctx_n[e.slot][:], dram["ctx"][bass.ds(e.number, 1)].rearrange(
                        "b (t p) d -> p (b t) d", p=P)).then_inc(ctx_n_in[e.slot], 16)
                if z.exists():
                    sp.wait_ge(y_done, 2 * z.number + 2)
                    rows = dram["table"][bass.ds(z.number * SEQ + 1, SEQ), 0:D]
                    sp.dma_start(rows.rearrange("(t p) d -> p t d", p=P), y[z.slot][:]
                                 ).then_inc(table_out[z.slot], 16)
                    sp.dma_start(out[bass.ds(z.number * SEQ, SEQ), :].rearrange("(t p) d -> p t d", p=P),
                                 x_res[:, bass.ds(z.number * ROW, ROW)].rearrange(
                                     "p (t d) -> p t d", t=TILES)).then_inc(result_out[z.slot], 16)

            pipeline(sp, step, FIRST, LAST, *STEADY)
            sp.wait_ge(zero_out, 16)
            for r in range(3):
                uses = len(range(r, BATCHES, 3))
                sp.wait_ge(table_out[r], 16 * uses)
                sp.wait_ge(result_out[r], 16 * uses)

        @block.gpsimd
        def _(pool):
            g = nc.gpsimd
            pool.wait_ge(consts, 4)
            g.affine_select(out=ident[:], in_=ident[:], compare_op=ALU.not_equal, fill=1.0, base=0,
                            pattern=[[-1, P]], channel_multiplier=1).then_inc(pool_consts, 1)
            for lo, hi, base in ((0, P, 0), (P, KEYS, P)):
                g.affine_select(out=causal[:, lo:hi], in_=causal[:, lo:hi], compare_op=ALU.is_ge,
                                fill=MASKED, base=base, pattern=[[-1, hi - lo]], channel_multiplier=1
                                ).then_inc(pool_consts, 1)

            def step(s):
                a, c, e, z = stages(s)
                for n, i, aggr, done, used in ((a, 1, aggr2, rstd2, y_done), (e, 0, aggr1, rstd1, xn_done)):
                    if n.exists():
                        pool.wait_ge(aggr, 2 * n.number + 2)
                        pool.sem_inc(passed, 1)
                        g.tensor_scalar(rstd[:, i], mean_var[:, i, :, 1], LN_EPS, None, ALU.add
                                        ).then_inc(done, 1)
                        pool.wait_ge(done, 2 * n.number + 1)
                        g.tensor_tensor(rstd[:, i], rstd[:, i], neg_half[:], ALU.pow).then_inc(done, 1)

            pipeline(pool, step, FIRST, LAST, *STEADY)

        @block.vector
        def _(dve):
            v = nc.vector
            v.memset(ident[:], 0.0).then_inc(consts, 1)
            v.memset(causal[:], 0.0).then_inc(consts, 1)
            v.memset(zero_row[:], 0.0).then_inc(consts, 1)
            v.memset(neg_half[:], -0.5).then_inc(consts, 1)
            dve.wait_ge(pool_consts, 3)

            def statistics(n, i, stats_done, aggr, last_used):
                dve.sem_inc(passed, 1)
                for t in range(TILES):
                    v.bn_stats(stats[:, i, t], tile(n, t)).then_inc(stats_done, 1)
                dve.wait_ge(stats_done, 2 * n.number + 2)
                dve.sem_inc(passed, 1)
                for t in range(TILES):
                    v.bn_aggr(mean_var[:, i, t], stats[:, i, t]).then_inc(aggr, 1)

            def step(s):
                a, c, e, z = stages(s)
                if c.exists():
                    dve.wait_ge(rstd1, 2 * c.number + 2)
                    if a.exists():
                        dve.wait_ge(x_turned, a.number + 1)
                    for t in range(TILES):
                        v.tensor_scalar(xn[:, t], tile(c, t), mean_var[:, 0, t, 0:1],
                                        rstd[:, 0, t:t + 1], ALU.subtract, ALU.mult).then_inc(xn_done, 1)
                if z.exists():
                    dve.wait_ge(rstd2, 2 * z.number + 2)
                    if s.shift(-4).exists():
                        dve.wait_ge(table_out[z.slot], 16 * z.turns)
                    for t in range(TILES):
                        v.tensor_scalar(y[z.slot][:, t], tile(z, t), mean_var[:, 1, t, 0:1],
                                        rstd[:, 1, t:t + 1], ALU.subtract, ALU.mult).then_inc(y_done, 1)
                if a.exists():
                    dve.wait_ge(exp_done, 2 * a.number + 2)
                    if z.exists():
                        dve.wait_ge(res_done, 2 * a.number)
                    v.reciprocal(inv[:], sums[a.slot][:]).then_inc(inv_done, 1)
                    dve.wait_ge(inv_done, 2 * a.number + 1)
                    v.tensor_scalar(inv[:], inv[:], gates[:, 1:2], None, ALU.mult).then_inc(inv_done, 1)
                    dve.wait_ge(inv_done, 2 * a.number + 2)
                    dve.wait_ge(v_ready, a.number + 1)
                    for t in range(TILES):
                        v.scalar_tensor_tensor(tile(a, t), ps_v[:, t], inv[:, t:t + 1], tile(a, t),
                                               ALU.mult, ALU.add).then_inc(res_done, 1)
                    dve.wait_ge(res_done, 2 * a.number + 2)
                    if z.exists():
                        dve.wait_ge(y_done, 2 * a.number)
                    statistics(a, 1, stats2, aggr2, y_done)
                if e.exists():
                    if c.exists():
                        dve.wait_ge(xn_done, 2 * e.number)
                    statistics(e, 0, stats1, aggr1, xn_done)
                if c.exists():
                    dve.wait_ge(s_ready, c.number + 1)
                    if a.exists():
                        dve.wait_ge(exp_done, 2 * c.number)
                    v.tensor_tensor(scores[:], ps_s[:, 0:KEYS], causal[:], ALU.add).then_inc(s_done, 1)
                    dve.wait_ge(s_done, c.number + 1)
                    for t, keys in ((0, slice(0, P)), (1, slice(P, KEYS))):
                        v.tensor_reduce(neg_max[:, t:t + 1], scores[:, keys], AX_X, ALU.max, negate=True
                                        ).then_inc(max_done, 1)
                if z.exists():
                    dve.wait_ge(l_ready, z.number + 1)
                    v.tensor_copy(logits[:, :, bass.ds(z.number * TILES, TILES)].rearrange("p e t -> p t e"),
                                  ps_l[:]).then_inc(l_out, 1)

            pipeline(dve, step, FIRST, LAST, *STEADY)

        @block.scalar
        def _(act):
            s_ = nc.scalar

            def step(s):
                a, c, e, z = stages(s)
                if c.exists():
                    act.wait_ge(x_turned, c.number + 1)
                    if a.exists():
                        act.wait_ge(s_ready, c.number)
                    s_.activation(xn_t[:], ps_x[:], ACT.Copy, scale=float(D) ** -0.5).then_inc(x_out, 1)
                if a.exists():
                    act.wait_ge(p_turned, a.number + 1)
                    if z.exists():
                        act.wait_ge(v_ready, a.number)
                    s_.copy(probs_t[:], ps_p[:, 0:KEYS]).then_inc(p_out, 1)
                if z.exists():
                    act.wait_ge(y_turned, z.number + 1)
                    if s.shift(-2).exists():
                        act.wait_ge(l_ready, z.number)
                    s_.copy(y_t[:], ps_y[:]).then_inc(y_out, 1)
                if c.exists():
                    if s.shift(-2).exists():
                        act.wait_ge(p_turned, c.number - 2)
                        act.wait_ge(inv_done, 2 * c.number - 4)
                    for t, keys in ((0, slice(0, P)), (1, slice(P, KEYS))):
                        act.wait_ge(max_done, 2 * c.number + t + 1)
                        s_.activation(probs[c.slot][:, keys], scores[:, keys], ACT.Exp,
                                      bias=neg_max[:, t:t + 1], accum_out=sums[c.slot][:, t:t + 1]
                                      ).then_inc(exp_done, 1)

            pipeline(act, step, FIRST, LAST, *STEADY)

        @block.tensor
        def _(pe):
            t_ = nc.tensor
            pe.wait_ge(pool_consts, 3)
            pe.wait_ge(w_in, 16)

            def turn(dst, src):
                for t in range(TILES):
                    for k in range(2):
                        mm = t_.transpose(dst[:, k, t * P:(t + 1) * P], src[:, t, k * P:(k + 1) * P],
                                          ident[:])
                return mm

            def step(s):
                a, c, e, z = stages(s)
                if c.exists():
                    pe.wait_ge(xn_done, 2 * c.number + 2)
                    if a.exists():
                        pe.wait_ge(x_out, c.number)
                    turn(ps_x, xn).then_inc(x_turned, 1)
                if a.exists():
                    pe.wait_ge(exp_done, 2 * a.number + 2)
                    if z.exists():
                        pe.wait_ge(p_out, a.number)
                    for i in range(3):
                        mm = t_.transpose(ps_p[:, i * P:(i + 1) * P], probs[a.slot][:, i * P:(i + 1) * P],
                                          ident[:])
                    mm.then_inc(p_turned, 1)
                if z.exists():
                    pe.wait_ge(y_done, 2 * z.number + 2)
                    if s.shift(-2).exists():
                        pe.wait_ge(y_out, z.number)
                    turn(ps_y, y[z.slot]).then_inc(y_turned, 1)
                if a.exists():
                    pe.wait_ge(p_out, a.number + 1)
                    pe.wait_ge(ctx_n_in[a.slot], 16 * (a.turns + 1))
                    if z.exists():
                        pe.wait_ge(res_done, 2 * a.number)
                    t_.matmul(ps_v[:, 0], probs_t[:, 0:P], ctx_n[a.slot][:, 0], start=True, stop=True)
                    for k in range(2):
                        mm = t_.matmul(ps_v[:, 1], probs_t[:, (1 + k) * P:(2 + k) * P],
                                       ctx_n[a.slot][:, k], start=k == 0, stop=k == 1)
                    mm.then_inc(v_ready, 1)
                if c.exists():
                    pe.wait_ge(x_out, c.number + 1)
                    pe.wait_ge(ctx_t_in[c.slot], 16 * (c.turns + 1))
                    if a.exists():
                        pe.wait_ge(s_done, c.number)
                    for t, keys in ((0, slice(0, P)), (1, slice(P, KEYS))):
                        for k in range(2):
                            mm = t_.matmul(ps_s[:, keys], xn_t[:, k, t * P:(t + 1) * P],
                                           ctx_t[c.slot][:, k, 0:(t + 1) * P], start=k == 0, stop=k == 1)
                    mm.then_inc(s_ready, 1)
                if z.exists():
                    pe.wait_ge(y_out, z.number + 1)
                    if s.shift(-2).exists():
                        pe.wait_ge(l_out, z.number)
                    for t in range(TILES):
                        for k in range(2):
                            mm = t_.matmul(ps_l[:, t], y_t[:, k, t * P:(t + 1) * P], gate_w[:, k],
                                           start=k == 0, stop=k == 1)
                    mm.then_inc(l_ready, 1)

            pipeline(pe, step, FIRST, LAST, *STEADY)


def routing(nc, dram, passed, gates, logits, gather_rows, scatter_rows):
    with ExitStack() as ctx:
        def sb(name, shape, dt=F32):
            return ctx.enter_context(nc.sbuf_tensor("r_" + name, shape, dt))

        sem = phase_semaphores(nc, ctx, "r")

        N = EXPERTS * ALL_TILES
        DIGIT = 16
        GROUP = P // DIGIT
        GROUPS = EXPERTS // GROUP
        TGROUP = 4
        TGROUPS = ALL_TILES // TGROUP
        NONE = 4096.0
        probs = sb("probs", [P, EXPERTS, ALL_TILES])
        mine = [sb(f"mine{u}", [P, TGROUP, EXPERTS]) for u in range(2)]
        mine_top = [sb(f"mine_top{u}", [P, TGROUP, TOPK]) for u in range(2)]
        mine_rest = [sb(f"mine_rest{u}", [P, TGROUP, EXPERTS]) for u in range(2)]
        top = sb("top", [P, ALL_TILES, TOPK])
        row = sb("row", [P, 2, ALL_TILES])
        chosen = sb("chosen", [P, EXPERTS, ALL_TILES], BF16)
        weights = sb("weights", [P, ALL_TILES, EXPERTS])
        restart = sb("restart", [P, EXPERTS, ALL_TILES], BF16)
        before = sb("before", [P, N])
        place = sb("place", [P, N], I32)
        digit = sb("digit", [P, N], I32)
        high = sb("high", [P, EXPERTS, ALL_TILES], BF16)
        low = sb("low", [P, EXPERTS, ALL_TILES], BF16)
        lower = sb("lower", [P, P], BF16)
        ones = sb("ones", [P, P], BF16)
        zeros = sb("zeros", [P, 512], BF16)
        digits_i = sb("digits_i", [P, EXPERTS, DIGIT], I32)
        digits = sb("digits", [P, EXPERTS, DIGIT], BF16)
        token_i = sb("token_i", [P, 1], I32)
        token = sb("token", [P, 1])
        tile_i = sb("tile_i", [P, ALL_TILES], I32)
        tile_base = sb("tile_base", [P, ALL_TILES])
        is_high = [sb(f"is_high{u}", [P, EXPERTS, DIGIT], BF16) for u in range(2)]
        is_low = [sb(f"is_low{u}", [P, EXPERTS, DIGIT], BF16) for u in range(2)]
        low_token = [sb(f"low_token{u}", [P, EXPERTS, DIGIT], BF16) for u in range(2)]
        low_tile = [sb(f"low_tile{u}", [P, EXPERTS, DIGIT], BF16) for u in range(2)]
        own = sb("own", [P, GROUP, DIGIT])
        crossed = sb("crossed", [P, GROUPS, GROUP, DIGIT])
        found = sb("found", [P, GROUPS, DIGIT])
        by_half = sb("by_half", [2 * EXPERTS, P])
        ident = sb("ident", [P, P])
        empty = sb("empty", [P, 2 * EXPERTS])
        shifted = sb("shifted", [P, 2 * EXPERTS])
        PC = min(N, 512)
        ps_rank = ctx.enter_context(nc.psum_tensor("r_ps_rank", [P, 2048], F32))
        ps_total = ctx.enter_context(nc.psum_tensor("r_ps_total", [P, 2048], F32))
        ps_rows = ps_total[:, 0:512]
        ps_turn = ps_total[:, 512:512 + 2 * EXPERTS]

        steps, consts, pool_consts = sem("steps"), sem("consts"), sem("pool_consts")
        shifted_done, exp_done = sem("shifted_done"), sem("exp_done")
        top_done, replaced, chosen_done = sem("top_done"), sem("replaced"), sem("chosen_done")
        weights_done, weights_out = sem("weights_done"), sem("weights_out")
        ranked, place_read, digits_done = sem("ranked"), sem("place_read"), sem("digits_done")
        cleared, high_done, low_done, spread = sem("cleared"), sem("high_done"), sem("low_done"), sem("spread")
        summed, found_done, found_out = sem("summed"), sem("found_done"), sem("found_out")
        turned, rows_done = sem("turned"), sem("rows_done")
        probs_done, mine_in, top_out = sem("probs_done"), sem("mine_in"), sem("top_out")
        flat = "p e t -> p (e t)"

        def in_groups(eng, work):
            for g in range(2):
                work(g, g, True)
            with eng.Fori(1, TGROUPS // 2, 1) as it:
                for u in range(2):
                    work(it * 2 + u, u, False)

        block = ctx.enter_context(nc.Block())

        @block.gpsimd
        def _(pool):
            g = nc.gpsimd
            g.iota(digits_i[:], pattern=[[0, EXPERTS], [1, DIGIT]], base=0, channel_multiplier=0
                   ).then_inc(pool_consts, 1)
            g.iota(token_i[:], pattern=[[0, 1]], base=1, channel_multiplier=1).then_inc(pool_consts, 1)
            g.iota(tile_i[:], pattern=[[P, ALL_TILES]], base=0, channel_multiplier=0
                   ).then_inc(pool_consts, 1)
            pool.wait_ge(consts, 5)
            g.affine_select(out=lower[:], in_=lower[:], compare_op=ALU.is_gt, fill=0.0, base=0,
                            pattern=[[1, P]], channel_multiplier=-1).then_inc(pool_consts, 1)
            g.affine_select(out=ident[:], in_=ident[:], compare_op=ALU.not_equal, fill=1.0, base=0,
                            pattern=[[-1, P]], channel_multiplier=1).then_inc(pool_consts, 1)
            g.affine_select(out=own[:], in_=own[:], compare_op=ALU.is_ge, fill=0.0, base=0,
                            pattern=[[-DIGIT, GROUP], [0, DIGIT]], channel_multiplier=1
                            ).then_inc(pool_consts, 1)
            pool.wait_ge(pool_consts, 6)
            g.affine_select(out=own[:], in_=own[:], compare_op=ALU.is_ge, fill=0.0, base=DIGIT - 1,
                            pattern=[[DIGIT, GROUP], [0, DIGIT]], channel_multiplier=-1
                            ).then_inc(pool_consts, 1)

        @block.sync
        def _(sp):
            sp.wait_ge(weights_done, 1)
            sp.dma_start(dram["table"][1:TOKENS + 1, D:D + EXPERTS].rearrange("(t p) e -> p t e", p=P),
                         weights[:]).then_inc(weights_out, 16)
            sp.wait_ge(found_done, 1)
            sp.dma_start(dram["places"].rearrange("(g p l) -> p g l", g=GROUPS, l=DIGIT), found[:]
                         ).then_inc(found_out, 16)
            sp.wait_ge(found_out, 16)
            sp.dma_start(by_half[:], dram["places"].rearrange("(h p) -> h p", p=P)).then_inc(found_out, 16)
            sp.wait_ge(weights_out, 16)

        @block.scalar
        def _(act):
            act.wait_ge(shifted_done, 1)
            nc.scalar.activation(probs[:], probs[:], ACT.Exp).then_inc(exp_done, 1)
            act.wait_ge(probs_done, 1)

            def copy_in(g, u, first):
                if not first:
                    act.wait_ge(replaced, TGROUP * (g - 1))
                nc.scalar.copy(mine[u][:], probs[:, :, bass.ds(g * TGROUP, TGROUP)]
                               .rearrange("p e t -> p t e")).then_inc(mine_in, 1)

            def copy_out(g, u):
                act.wait_ge(top_done, TGROUP * (g + 1))
                nc.scalar.copy(top[:, bass.ds(g * TGROUP, TGROUP)], mine_top[u][:]).then_inc(top_out, 1)

            copy_in(0, 0, True)
            copy_in(1, 1, True)
            with act.Fori(0, TGROUPS // 2 - 1, 1) as it:
                for u in range(2):
                    copy_out(it * 2 + u, u)
                    copy_in(it * 2 + u + 2, u, False)
            for u in range(2):
                copy_out(TGROUPS - 2 + u, u)

        @block.vector
        def _(dve):
            v = nc.vector
            links = 0

            def link(ins):
                nonlocal links
                links += 1
                ins.then_inc(steps, 1)
                dve.wait_ge(steps, links)

            v.memset(lower[:], 1.0).then_inc(consts, 1)
            v.memset(ones[:], 1.0).then_inc(consts, 1)
            v.memset(zeros[:], 0.0).then_inc(consts, 1)
            v.memset(ident[:], 0.0).then_inc(consts, 1)
            v.memset(own[:], 1.0).then_inc(consts, 1)
            link(v.memset(restart[:], 1.0))
            link(v.memset(restart[:, :, 0:1], 0.0))
            dve.wait_ge(pool_consts, 7)
            link(v.tensor_copy(digits[:], digits_i[:]))
            link(v.tensor_copy(token[:], token_i[:]))
            link(v.tensor_copy(tile_base[:], tile_i[:]))

            def spread_row(i):
                return row[:, i].unsqueeze(1).to_broadcast([P, EXPERTS, ALL_TILES])

            link(v.tensor_reduce(row[:, 0], logits[:].rearrange("p e t -> p t e"), AX_X, ALU.max))
            v.tensor_tensor(probs[:], logits[:], spread_row(0), ALU.subtract).then_inc(shifted_done, 1)
            dve.wait_ge(exp_done, 1)
            link(v.tensor_reduce(row[:, 0], probs[:].rearrange("p e t -> p t e"), AX_X, ALU.add))
            link(v.reciprocal(row[:, 1], row[:, 0]))
            v.tensor_tensor(probs[:], probs[:], spread_row(1), ALU.mult).then_inc(probs_done, 1)
            dve.wait_ge(probs_done, 1)
            def top_group(g, u, first):
                dve.wait_ge(mine_in, g + 1)
                if not first:
                    dve.wait_ge(top_out, g - 1)
                dve.sem_inc(passed, 1)
                for i in range(TGROUP):
                    v.max(mine_top[u][:, i], mine[u][:, i]).then_inc(top_done, 1)
                for i in range(TGROUP):
                    dve.wait_ge(top_done, TGROUP * g + i + 1)
                    dve.sem_inc(passed, 1)
                    v.match_replace(out=mine_rest[u][:, i], in_to_replace=mine_top[u][:, i],
                                    in_values=mine[u][:, i], imm_value=-1.0).then_inc(replaced, 1)
                dve.wait_ge(replaced, TGROUP * (g + 1))
                v.tensor_scalar(chosen[:, :, bass.ds(g * TGROUP, TGROUP)].rearrange("p e t -> p t e"),
                                mine_rest[u][:], 0.0, None, ALU.is_lt).then_inc(chosen_done, 1)

            in_groups(dve, top_group)
            dve.wait_ge(top_out, TGROUPS)
            link(v.tensor_reduce(row[:, 0], top[:], AX_X, ALU.add))
            link(v.reciprocal(row[:, 1], row[:, 0]))
            link(v.tensor_scalar(row[:, 1], row[:, 1], gates[:, 3:4], None, ALU.mult))
            v.tensor_tensor(weights[:], probs[:].rearrange("p e t -> p t e"),
                            row[:, 1].unsqueeze(2).to_broadcast([P, ALL_TILES, EXPERTS]), ALU.mult
                            ).then_inc(weights_done, 1)
            dve.wait_ge(ranked, 1)
            total = ps_total[:, 0:N]
            link(v.tensor_tensor_scan(before[:], restart[:].rearrange(flat), total, 0.0, ALU.mult, ALU.add))
            link(v.tensor_tensor(before[:], before[:], total, ALU.subtract))
            link(v.tensor_tensor(before[:], before[:], ps_rank[:, 0:N], ALU.add))
            dve.wait_ge(chosen_done, TGROUPS)
            link(v.scalar_tensor_tensor(before[:], chosen[:].rearrange(flat), -NONE, before[:],
                                        ALU.mult, ALU.add))
            link(v.tensor_scalar(place[:], before[:], NONE, None, ALU.add))
            link(v.tensor_single_scalar(digit[:], place[:], 4, ALU.logical_shift_right))
            link(v.tensor_copy(high[:].rearrange(flat), digit[:]))
            link(v.tensor_single_scalar(digit[:], place[:], DIGIT - 1, ALU.bitwise_and))
            v.tensor_copy(low[:].rearrange(flat), digit[:]).then_inc(digits_done, 1)
            dve.wait_ge(digits_done, 1)

            def one_hot(t, u, first):
                if not first:
                    dve.wait_ge(summed, t - 1)
                v.tensor_tensor(is_high[u][:], high[:, :, bass.ds(t, 1)].to_broadcast([P, EXPERTS, DIGIT]),
                                digits[:], ALU.is_equal).then_inc(high_done, 1)
                v.tensor_tensor(is_low[u][:], low[:, :, bass.ds(t, 1)].to_broadcast([P, EXPERTS, DIGIT]),
                                digits[:], ALU.is_equal).then_inc(low_done, 1)
                dve.wait_ge(low_done, t + 1)
                v.tensor_scalar(low_token[u][:], is_low[u][:], token[:, 0:1], None, ALU.mult
                                ).then_inc(spread, 1)
                v.tensor_scalar(low_tile[u][:], is_low[u][:], tile_base[:, bass.ds(t, 1)], None, ALU.mult
                                ).then_inc(spread, 1)

            one_hot(0, 0, True)
            one_hot(1, 1, True)
            with dve.Fori(1, ALL_TILES // 2, 1) as it:
                one_hot(it * 2, 0, False)
                one_hot(it * 2 + 1, 1, False)
            dve.wait_ge(summed, ALL_TILES)
            link(v.tensor_tensor(crossed[:].rearrange("p g e l -> p g (e l)"),
                                 ps_rows.rearrange("p (g n) -> p g n", g=GROUPS),
                                 own[:].rearrange("p e l -> p (e l)").unsqueeze(1).to_broadcast(
                                     [P, GROUPS, P]), ALU.mult))
            v.tensor_reduce(found[:], crossed[:].rearrange("p g e l -> p g l e"), AX_X, ALU.add
                            ).then_inc(found_done, 1)
            dve.wait_ge(turned, 1)
            v.tensor_copy(gather_rows[:], ps_turn).then_inc(rows_done, 1)
            link(v.tensor_scalar(empty[:], ps_turn, 0.0, float(TOKENS + 1), ALU.is_equal, ALU.mult))
            link(v.tensor_tensor(shifted[:], empty[:], ps_turn, ALU.add))
            v.tensor_scalar(scatter_rows[:], shifted[:], -1.0, None, ALU.add).then_inc(rows_done, 1)
            dve.wait_ge(rows_done, 2)

        @block.tensor
        def _(pe):
            t_ = nc.tensor
            pe.wait_ge(pool_consts, 7)
            pe.wait_ge(chosen_done, TGROUPS)
            for i in range(N // PC):
                cols = chosen[:].rearrange(flat)[:, i * PC:(i + 1) * PC]
                t_.matmul(ps_rank[:, i * PC:(i + 1) * PC], lower[:], cols, start=True, stop=True)
                mm = t_.matmul(ps_total[:, i * PC:(i + 1) * PC], ones[:], cols, start=True, stop=True)
            mm.then_inc(ranked, 1)
            pe.wait_ge(digits_done, 1)
            t_.matmul(ps_rows, zeros[:, 0:P], zeros[:], start=True, stop=False, skip_group_check=True)

            def add_tile(t, u):
                pe.wait_ge(high_done, t + 1)
                pe.wait_ge(spread, 2 * t + 2)
                for i in range(GROUPS):
                    mine = slice(i * GROUP, (i + 1) * GROUP)
                    for values in (low_token[u], low_tile[u]):
                        mm = t_.matmul(ps_rows[:, i * P:(i + 1) * P],
                                       is_high[u][:, mine].rearrange("p e l -> p (e l)"),
                                       values[:, mine].rearrange("p e l -> p (e l)"),
                                       start=False, stop=False, skip_group_check=True)
                mm.then_inc(summed, 1)

            with pe.Fori(0, ALL_TILES // 2, 1) as it:
                add_tile(it * 2, 0)
                add_tile(it * 2 + 1, 1)
            pe.wait_ge(found_out, 32)
            t_.transpose(ps_turn, by_half[:], ident[0:2 * EXPERTS, 0:2 * EXPERTS]).then_inc(turned, 1)


def experts(nc, dram, passed, gather_rows, scatter_rows, out):
    with ExitStack() as ctx:
        def sb(name, shape, dt=F32):
            return ctx.enter_context(nc.sbuf_tensor("e_" + name, shape, dt))

        sem = phase_semaphores(nc, ctx, "e")

        def ps(name, shape, dt=F32):
            return ctx.enter_context(nc.psum_tensor("e_" + name, shape, dt))

        FH = FFN // 2
        HALVES = CAPACITY // P
        W = D + EXPERTS
        ident = sb("ident", [P, P])
        up_w = [sb(f"up_w{r}", [P, 2, 2 * FFN]) for r in range(3)]
        down_w = [sb(f"down_w{r}", [FH, 2, D]) for r in range(3)]
        rows = [sb(f"rows{r}", [P, HALVES, W]) for r in range(3)]
        rows_t = sb("rows_t", [P, 2, CAPACITY])
        silu = sb("silu", [FH, 2, CAPACITY])
        hidden_t = sb("hidden_t", [FH, 2, CAPACITY])
        weight = sb("weight", [P, HALVES, 1])
        y = [sb(f"y{r}", [P, HALVES, D]) for r in range(3)]
        gather_now = [sb(f"gather_now{r}", [P, HALVES], U32) for r in range(3)]
        scatter_now = [sb(f"scatter_now{r}", [P, HALVES], U32) for r in range(3)]
        ps_x = ps("ps_x", [P, 2, CAPACITY])
        ps_gate = ps("ps_gate", [FH, 2, CAPACITY])
        ps_up = ps("ps_up", [FH, 2, CAPACITY])
        ps_y = ps("ps_y", [P, HALVES, D])

        consts, ident_done = sem("consts"), sem("ident_done")
        up_in = [sem(f"up_in{r}") for r in range(3)]
        down_in = [sem(f"down_in{r}") for r in range(3)]
        gathered = [sem(f"gathered{r}") for r in range(3)]
        scattered = [sem(f"scattered{r}") for r in range(3)]
        gather_at, scatter_at = sem("gather_at"), sem("scatter_at")
        x_turned, x_out = sem("x_turned"), sem("x_out")
        gate_ready, up_ready, silu_done, hidden_done = (
            sem(n) for n in ("gate_ready", "up_ready", "silu_done", "hidden_done"))
        y_ready, weight_done, y_done = sem("y_ready"), sem("weight_done"), sem("y_done")

        FIRST, LAST = -2, EXPERTS - 1
        STEADY = (3, EXPERTS - 3)

        def stages(s):
            return s, s.shift(1), s.shift(2), s.shift(-1)

        block = ctx.enter_context(nc.Block())

        @block.sync
        def _(sp):
            def step(s):
                a, c, e, z = stages(s)
                if e.exists():
                    if z.exists():
                        sp.wait_ge(y_ready, z.number + 1)
                    sp.dma_start(up_w[e.slot][:], dram["up_w"][bass.ds(e.number, 1)].rearrange(
                        "e p c f -> p (e c) f")).then_inc(up_in[e.slot], 16)
                    sp.dma_start(down_w[e.slot][:], dram["down_w"][bass.ds(e.number, 1)].rearrange(
                        "e p c d -> p (e c) d")).then_inc(down_in[e.slot], 16)

            pipeline(sp, step, FIRST, LAST, *STEADY, count=EXPERTS)

        @block.gpsimd
        def _(pool):
            g = nc.gpsimd
            pool.wait_ge(consts, 1)
            g.affine_select(out=ident[:], in_=ident[:], compare_op=ALU.not_equal, fill=1.0, base=0,
                            pattern=[[-1, P]], channel_multiplier=1).then_inc(ident_done, 1)

            def step(s):
                a, c, e, z = stages(s)
                if e.exists():
                    if z.exists():
                        pool.wait_ge(x_turned, z.number + 1)
                        pool.wait_ge(weight_done, z.number + 1)
                    pool.sem_inc(passed, 1)
                    g.tensor_copy(gather_now[e.slot][:], gather_rows[:, bass.ds(e.number * HALVES, HALVES)]
                                  ).then_inc(gather_at, 1)
                    pool.wait_ge(gather_at, e.number + 1)
                    pool.sem_inc(passed, 1)
                    for half in range(HALVES):
                        g.indirect_dma_start(rows[e.slot][:, half, :], None, dram["table"],
                                             bass.IndirectOffsetOnAxis(
                                                 gather_now[e.slot][:, half:half + 1], 0)
                                             ).then_inc(gathered[e.slot], 16)
                if a.exists():
                    if s.shift(-3).exists():
                        pool.wait_ge(scattered[a.slot], 32 * a.turns)
                    pool.sem_inc(passed, 1)
                    g.tensor_copy(scatter_now[a.slot][:], scatter_rows[:, bass.ds(a.number * HALVES, HALVES)]
                                  ).then_inc(scatter_at, 1)
                    pool.wait_ge(scatter_at, a.number + 1)
                    pool.wait_ge(y_done, 2 * a.number + 2)
                    if z.exists():
                        pool.wait_ge(scattered[z.slot], 32 * (z.turns + 1))
                    pool.sem_inc(passed, 1)
                    for half in range(HALVES):
                        g.indirect_dma_start(out, bass.IndirectOffsetOnAxis(
                                                 scatter_now[a.slot][:, half:half + 1], 0),
                                             y[a.slot][:, half, :], None, bounds_check=TOKENS - 1,
                                             oob_is_err=False, compute_op=ALU.add
                                             ).then_inc(scattered[a.slot], 16)

            pipeline(pool, step, FIRST, LAST, *STEADY, count=EXPERTS)
            for r in range(3):
                pool.wait_ge(scattered[r], 32 * len(range(r, EXPERTS, 3)))

        @block.vector
        def _(dve):
            v = nc.vector
            v.memset(ident[:], 0.0).then_inc(consts, 1)

            def step(s):
                a, c, e, z = stages(s)
                if a.exists():
                    dve.wait_ge(gathered[a.slot], 32 * (a.turns + 1))
                    if z.exists():
                        dve.wait_ge(y_done, 2 * a.number)
                    v.tensor_copy(weight[:], rows[a.slot][:, :, bass.ds(a.number + D, 1)]
                                  ).then_inc(weight_done, 1)
                    dve.wait_ge(weight_done, a.number + 1)
                    dve.wait_ge(y_ready, a.number + 1)
                    if s.shift(-3).exists():
                        dve.wait_ge(scattered[a.slot], 32 * a.turns)
                    for half in range(HALVES):
                        v.tensor_scalar(y[a.slot][:, half], ps_y[:, half], weight[:, half], None,
                                        ALU.mult).then_inc(y_done, 1)
                if c.exists():
                    dve.wait_ge(silu_done, c.number + 1)
                    dve.wait_ge(up_ready, c.number + 1)
                    if a.exists():
                        dve.wait_ge(y_ready, c.number)
                    v.tensor_tensor(hidden_t[:], silu[:], ps_up[:], ALU.mult).then_inc(hidden_done, 1)

            pipeline(dve, step, FIRST, LAST, *STEADY, count=EXPERTS)

        @block.scalar
        def _(act):
            s_ = nc.scalar

            def step(s):
                a, c, e, z = stages(s)
                if c.exists():
                    act.wait_ge(x_turned, c.number + 1)
                    if a.exists():
                        act.wait_ge(up_ready, c.number)
                    s_.copy(rows_t[:], ps_x[:]).then_inc(x_out, 1)
                    act.wait_ge(gate_ready, c.number + 1)
                    if a.exists():
                        act.wait_ge(hidden_done, c.number)
                    s_.activation(silu[:], ps_gate[:], ACT.Silu).then_inc(silu_done, 1)

            pipeline(act, step, FIRST, LAST, *STEADY, count=EXPERTS)

        @block.tensor
        def _(pe):
            t_ = nc.tensor
            pe.wait_ge(ident_done, 1)

            def step(s):
                a, c, e, z = stages(s)
                if c.exists():
                    pe.wait_ge(gathered[c.slot], 32 * (c.turns + 1))
                    if a.exists():
                        pe.wait_ge(x_out, c.number)
                    for half in range(HALVES):
                        for k in range(2):
                            mm = t_.transpose(ps_x[:, k, half * P:(half + 1) * P],
                                              rows[c.slot][:, half, k * P:(k + 1) * P], ident[:])
                    mm.then_inc(x_turned, 1)
                if a.exists():
                    pe.wait_ge(hidden_done, a.number + 1)
                    pe.wait_ge(down_in[a.slot], 16 * (a.turns + 1))
                    if z.exists():
                        pe.wait_ge(y_done, 2 * a.number)
                    for half in range(HALVES):
                        for k in range(2):
                            mm = t_.matmul(ps_y[:, half], hidden_t[:, k, half * P:(half + 1) * P],
                                           down_w[a.slot][:, k], start=k == 0, stop=k == 1)
                    mm.then_inc(y_ready, 1)
                if c.exists():
                    pe.wait_ge(x_out, c.number + 1)
                    pe.wait_ge(up_in[c.slot], 16 * (c.turns + 1))
                    for dst, first, ready, used in ((ps_gate, 0, gate_ready, silu_done),
                                                    (ps_up, FFN, up_ready, hidden_done)):
                        if a.exists():
                            pe.wait_ge(used, c.number)
                        for m in range(2):
                            for k in range(2):
                                mm = t_.matmul(dst[:, m],
                                               up_w[c.slot][:, k, first + m * FH:first + (m + 1) * FH],
                                               rows_t[:, k], start=k == 0, stop=k == 1)
                        mm.then_inc(ready, 1)

            pipeline(pe, step, FIRST, LAST, *STEADY, count=EXPERTS)


def program(nc, dram, out):
    with ExitStack() as ctx:
        x_res = ctx.enter_context(nc.sbuf_tensor("x_res", [P, BATCHES * ROW], F32))
        gates = ctx.enter_context(nc.sbuf_tensor("gates", [P, 4], F32))
        gates_in = ctx.enter_context(nc.semaphore("gates_in"))
        gates_done = ctx.enter_context(nc.semaphore("gates_done"))
        passed = ctx.enter_context(nc.semaphore("passed"))
        with nc.Block() as block:
            @block.sync
            def _(sp):
                sp.dma_start(gates[:], dram["gates"].partition_broadcast(P)).then_inc(gates_in, 16)

            @block.scalar
            def _(act):
                act.wait_ge(gates_in, 16)
                nc.scalar.activation(gates[:], gates[:], ACT.Tanh).then_inc(gates_done, 1)
                act.wait_ge(gates_done, 1)
        cross_attention(nc, dram, passed, x_res, gates)
        ternary_ffn(nc, dram, passed, x_res, gates)
        logits = ctx.enter_context(nc.sbuf_tensor("logits", [P, EXPERTS, ALL_TILES], F32))
        gather_rows = ctx.enter_context(nc.sbuf_tensor("gather_rows", [P, 2 * EXPERTS], U32))
        scatter_rows = ctx.enter_context(nc.sbuf_tensor("scatter_rows", [P, 2 * EXPERTS], U32))
        causal_attention(nc, dram, passed, x_res, gates, logits, out)
        routing(nc, dram, passed, gates, logits, gather_rows, scatter_rows)
        experts(nc, dram, passed, gather_rows, scatter_rows, out)


def kernel(**inputs):
    import numpy as np
    import concourse.bacc as bacc
    from concourse.bass_utils import run_bass_kernel_spmd

    def arr(name):
        return np.asarray(inputs[name])

    def chunks(w):
        return w.reshape(-1, P, w.shape[1]).transpose(1, 0, 2)

    qk_bias = np.stack([arr("L0_xattn_bq").reshape(2, P), arr("L0_xattn_bk").reshape(2, P)])
    arrays = {
        "x": arr("x"),
        "ctx": arr("ctx_1024"),
        "ctx_t": arr("ctx_1024").transpose(0, 2, 1),
        "mask": arr("mask_Bx1xSxS2_if1").reshape(BATCHES, SEQ, SEQ),
        "gates": np.stack([arr("g_xattn"), arr("g_ffn")]).reshape(4),
        "wq": chunks(arr("L0_xattn_Wq").T),
        "wk": chunks(arr("L0_xattn_Wk").T),
        "wv": chunks(arr("L0_xattn_Wv").T),
        "wo": chunks(arr("L0_xattn_Wo").T),
        "qk_bias": qk_bias.reshape(4, P).T,
        "bv": arr("L0_xattn_bv"),
        "w1": chunks(arr("L0_ffn_w1").T),
        "b1": arr("L0_ffn_b1"),
        "w2": chunks(arr("L0_ffn_w2").T),
        "b2": arr("L0_ffn_b2"),
        "gate_w": chunks(arr("L1_ffn_gate_weight").T),
        "up_w": arr("L1_ffn_gate_up_proj").transpose(0, 2, 1).reshape(EXPERTS, 2, P, 2 * FFN)
        .transpose(0, 2, 1, 3),
        "down_w": arr("L1_ffn_down_proj").transpose(0, 2, 1).reshape(EXPERTS, 2, FFN // 2, D)
        .transpose(0, 2, 1, 3),
        "bo": arr("L0_xattn_bo"),
    }
    arrays = {k: np.ascontiguousarray(a) for k, a in arrays.items()}
    nc = bacc.Bacc("TRN2", target_bir_lowering=False, num_devices=1)
    dram = {k: nc.dram_tensor(f"in_{k}", a.shape, mybir.dt.from_np(a.dtype), kind="ExternalInput").ap()
            for k, a in arrays.items()}
    dram["parts"] = nc.dram_tensor("parts_dram", (3, 2, 3, D, SEQ), BF16, kind="Internal").ap()
    dram["table"] = nc.dram_tensor("table", (TOKENS + 1, D + EXPERTS), F32, kind="Internal").ap()
    dram["places"] = nc.dram_tensor("places", (EXPERTS * CAPACITY,), F32, kind="Internal").ap()
    out = nc.dram_tensor("out", (TOKENS, D), F32, kind="ExternalOutput").ap()
    program(nc, dram, out)
    r = run_bass_kernel_spmd(nc, [{f"in_{k}": a for k, a in arrays.items()}], core_ids=[0])
    return r.results[0]["out"].reshape(BATCHES, SEQ, D)
```

```python
from contextlib import ExitStack

import concourse.bass as bass
from concourse import mybir

F32 = mybir.dt.float32
BF16 = mybir.dt.bfloat16
I32 = mybir.dt.int32
U32 = mybir.dt.uint32
ALU = mybir.AluOpType
ACT = mybir.ActivationFunctionType
AX_X = mybir.AxisListType.X

P = 128
BATCHES = 32
SEQ = 256
D = 256
TILES = SEQ // P
ROW = TILES * D
HEADS = 16
DK = D // HEADS
PAIRS = 6
KROWS = PAIRS * DK
SHIFT = 3
HIDDEN = 1024
EXPERTS = 32
TOPK = 8
CAPACITY = 256
FFN = 192
TOKENS = BATCHES * SEQ
ALL_TILES = TOKENS // P
LN_EPS = 1e-5
RMS_EPS = 1e-6
QUANT_EPS = 1e-5
MASKED = -1e30
ROUND = 12582912.0
Q_PARTS = [(0, 0, 3, True), (3, 1, 2, True), (5, 2, 1, True)]
K_PARTS = [(0, 0, 3, False), (3, 0, 2, False), (5, 0, 1, False)]


class Seq:

    def __init__(self, turns, slot, known, count):
        self.turns, self.slot, self.known, self.count = turns, slot, known, count

    def shift(self, k):
        s = self.slot + k
        known = None if self.known is None else self.known + k
        return Seq(self.turns + s // 3, s % 3, known, self.count)

    @property
    def number(self):
        return self.turns * 3 + self.slot

    def exists(self):
        return self.known is None or 0 <= self.known < self.count


def pipeline(eng, step, first, last, steady_first, steady_last, count=BATCHES):
    for n in range(first, steady_first):
        step(Seq(n // 3, n % 3, n, count))
    turns = (steady_last - steady_first + 1) // 3
    with eng.Fori(0, turns, 1) as it:
        for s in range(steady_first, steady_first + 3):
            step(Seq(it + s // 3, s % 3, None, count))
    for n in range(steady_first + 3 * turns, last + 1):
        step(Seq(n // 3, n % 3, n, count))


def phase_semaphores(nc, ctx, prefix):
    made = []

    def clear():
        nc.clear_and_free_semaphores(made)
        nc.all_engine_barrier()

    ctx.callback(clear)

    def sem(name):
        made.append(nc.alloc_semaphore(name=f"{prefix}_{name}"))
        return made[-1]

    return sem


def cross_attention(nc, dram, passed, x_res, gates):
    with ExitStack() as ctx:
        def sb(name, shape, dt=F32):
            return ctx.enter_context(nc.sbuf_tensor(name, shape, dt))

        sem = phase_semaphores(nc, ctx, "x")

        q_stack = [sb(f"q_stack{r}", [KROWS + SHIFT, HEADS, SEQ], BF16) for r in range(3)]
        k_stack = [sb(f"k_stack{r}", [KROWS + SHIFT, HEADS, SEQ], BF16) for r in range(3)]
        ctx_t = [sb(f"ctx_t{r}", [P, 2, SEQ]) for r in range(3)]
        mask_raw = [sb(f"mask_raw{r}", [P, TILES, SEQ], I32) for r in range(3)]
        masked = [sb(f"masked{r}", [P, TILES, SEQ], BF16) for r in range(3)]
        values = [sb(f"values{r}", [P, TILES, HEADS, 32]) for r in range(3)]
        any_masked = [sb(f"any_masked{r}", [1, 1]) for r in range(3)]
        pair_masked = [sb(f"pair_masked{r}", [1, 1], I32) for r in range(3)]
        masked_cols = sb("masked_cols", [P, 1])
        wq, wk, wv = (sb(n, [P, 2, D]) for n in ("wq", "wk", "wv"))
        wo = sb("wo", [P, 2, D])
        o_bias = sb("o_bias", [P, D])
        qk_bias = sb("qk_bias", [P, 4])
        v_bias = sb("v_bias", [P, D])
        stats = sb("stats", [P, TILES, 6])
        mean_var = sb("mean_var", [P, TILES, 2])
        rstd = sb("rstd", [P, TILES])
        neg_half = sb("neg_half", [P, TILES])
        xn = sb("xn", [P, TILES, D])
        xn_t = sb("xn_t", [P, 2, SEQ])
        full = sb("full", [P, 4, SEQ])
        rest = sb("rest", [P, 4, SEQ])
        parts = sb("parts", [P, 4, 3, SEQ], BF16)
        row_max = sb("row_max", [P, TILES, HEADS])
        max_rest = sb("max_rest", [P, TILES, HEADS])
        max_parts = sb("max_parts", [P, TILES, 3, HEADS], BF16)
        max_rows = sb("max_rows", [3 * HEADS, SEQ], BF16)
        probs = [sb(f"probs{u}", [P, 4, SEQ]) for u in range(2)]
        out_raw = sb("out_raw", [P, 4, SEQ])
        inv_sum = sb("inv_sum", [P, TILES, HEADS])
        heads_out = sb("heads_out", [P, TILES, D])
        heads_t = sb("heads_t", [P, 2, SEQ])
        ident = sb("ident", [P, P])
        ident_b = sb("ident_b", [P, P], BF16)
        ident_mask = sb("ident_mask", [P, 3 * P], BF16)
        ones_col = sb("ones_col", [P, 1])
        ones_rows = sb("ones_rows", [SHIFT, SEQ], BF16)
        ones_b = sb("ones_b", [P, 1], BF16)

        def ps(name, shape, dt=F32):
            return ctx.enter_context(nc.psum_tensor(name, shape, dt))

        ps_max = [ps(f"ps_max{u}", [P, TILES, SEQ]) for u in range(2)]
        ps_exp = [ps(f"ps_exp{u}", [P, 4, SEQ]) for u in range(2)]
        ps_out = ps("ps_out", [P, 2, SEQ])
        ps_misc = ps("ps_misc", [P, 2, SEQ])
        ps_bits = ps_misc[0:3 * HEADS, 0, :].bitcast(BF16)[:, 0:SEQ]

        weights_in = sem("weights_in")
        ones_in = sem("ones_in")
        x_in = [sem(f"x_in{r}") for r in range(3)]
        ctx_in = [sem(f"ctx_in{r}") for r in range(3)]
        mask_in = [sem(f"mask_in{r}") for r in range(3)]
        consts_dve = sem("consts_dve")
        consts_pool = sem("consts_pool")
        stats_done, aggr_done, var_eps, rstd_done, xn_done = (
            sem(n) for n in ("stats_done", "aggr_done", "var_eps", "rstd_done", "xn_done"))
        xnt_ready, xnt_out = sem("xnt_ready"), sem("xnt_out")
        q_ready, q_out, k_ready, k_out = (sem(n) for n in ("q_ready", "q_out", "k_ready", "k_out"))
        rest1, mid, rest_low = sem("rest1"), sem("mid"), sem("rest_low")
        parts_out = [sem(f"parts_out{r}") for r in range(3)]
        stack_in = [sem(f"stack_in{r}") for r in range(3)]
        v_ready, v_out = sem("v_ready"), sem("v_out")
        scores_max, max_done = sem("scores_max"), sem("max_done")
        max_hi, max_mid_rest, max_mid, max_low_rest, max_split = (
            sem(n) for n in ("max_hi", "max_mid_rest", "max_mid", "max_low_rest", "max_split"))
        max_t, max_t_out = sem("max_t"), sem("max_t_out")
        shift_in = [sem(f"shift_in{r}") for r in range(3)]
        scores_exp, exp_done, pv_done = sem("scores_exp"), sem("exp_done"), sem("pv_done")
        out_copied = sem("out_copied")
        nat_ready, inv_done, nat_done = sem("nat_ready"), sem("inv_done"), sem("nat_done")
        heads_ready, heads_out_t = sem("heads_ready"), sem("heads_out_t")
        bias_done = sem("bias_done")
        wo_ready, res_done = sem("wo_ready"), sem("res_done")
        mask_done = sem("mask_done")
        cols_ready, cols_out, count_ready, count_out = (
            sem(n) for n in ("cols_ready", "cols_out", "count_ready", "count_out"))

        FIRST, LAST = -4, BATCHES
        STEADY = (2, BATCHES - 6)
        HEADS_AT = {(0, 1): 0, (0, 2): 1, **{(1 + i // 3, i % 3): 2 + i for i in range(14)}}

        def stages(s):
            return s, s.shift(1), s.shift(2), s.shift(3), s.shift(4)

        block = ctx.enter_context(nc.Block())

        @block.sync
        def _(sp):
            for t, name in ((wq, "wq"), (wk, "wk"), (wv, "wv"), (wo, "wo"), (qk_bias, "qk_bias")):
                sp.dma_start(t[:], dram[name]).then_inc(weights_in, 16)
            sp.dma_start(v_bias[:], dram["bv"].partition_broadcast(P)).then_inc(weights_in, 16)
            sp.dma_start(o_bias[:], dram["bo"].partition_broadcast(P)).then_inc(weights_in, 16)

            sp.wait_ge(consts_dve, 7)
            for r in range(3):
                sp.dma_start(k_stack[r][KROWS:KROWS + SHIFT],
                             ones_rows[:].unsqueeze(1).to_broadcast([SHIFT, HEADS, SEQ])
                             ).then_inc(ones_in, 16)

            def load_x(n):
                sp.dma_start(x_res[:, bass.ds(n.number * ROW, ROW)].rearrange("p (t d) -> p t d", t=TILES),
                             dram["x"][bass.ds(n.number, 1)].rearrange("b (t p) d -> p (b t) d", p=P)
                             ).then_inc(x_in[n.slot], 16)

            def load_ctx(n):
                sp.dma_start(ctx_t[n.slot][:], dram["ctx_t"][bass.ds(n.number, 1)].rearrange(
                    "b (c p) k -> p (b c) k", p=P)).then_inc(ctx_in[n.slot], 16)

            def load_mask(n):
                sp.dma_start(mask_raw[n.slot][:], dram["mask"][bass.ds(n.number, 1)].rearrange(
                    "b (t p) k -> p (b t) k", p=P)).then_inc(mask_in[n.slot], 16)

            def step(s):
                a, b, d, c, e = stages(s)
                f = s.shift(5)
                if f.exists():
                    if d.exists():
                        sp.wait_ge(aggr_done, 2 * d.number + 2)
                    load_x(f)
                if e.exists():
                    if b.exists():
                        sp.wait_ge(v_out, 2 * b.number + 2)
                    load_ctx(e)
                if c.exists():
                    if a.exists():
                        sp.wait_ge(mask_done, a.number + 1)
                    load_mask(c)
                    sp.wait_ge(rest_low, 2 * c.number + 2)
                    sp.sem_inc(passed, 1)
                    if a.exists():
                        sp.wait_ge(stack_in[c.slot], 96 * c.turns)
                    for m in range(4):
                        sp.dma_start(dram["parts"][c.slot, m // 2, :, (m % 2) * P:(m % 2 + 1) * P, :]
                                     .rearrange("i p t -> p i t"), parts[:, m]
                                     ).then_inc(parts_out[c.slot], 16)
                if b.exists():
                    sp.wait_ge(max_t_out, b.number + 1)
                    for part in range(SHIFT):
                        sp.dma_start(q_stack[b.slot][KROWS + part:KROWS + part + 1, :, :],
                                     max_rows[part * HEADS:(part + 1) * HEADS, :]
                                     ).then_inc(shift_in[b.slot], 16)
                if c.exists():
                    sp.wait_ge(parts_out[c.slot], 64 * (c.turns + 1))
                    if a.exists():
                        sp.wait_ge(scores_exp, 8 * a.number + 8)
                    for which, stack, order in ((0, q_stack, Q_PARTS), (1, k_stack, K_PARTS)):
                        for group, part, n, same in order:
                            if same:
                                src = dram["parts"][c.slot, which, part:part + 1].to_broadcast([n, D, SEQ])
                            else:
                                src = dram["parts"][c.slot, which, part:part + n]
                            sp.dma_start(stack[c.slot][group * DK:(group + n) * DK, :, :]
                                         .rearrange("p h t -> p (h t)"),
                                         src.rearrange("i (d h) t -> i d (h t)", d=DK)
                                         ).then_inc(stack_in[c.slot], 16)

            pipeline(sp, step, FIRST - 1, LAST, *STEADY)

        @block.gpsimd
        def _(pool):
            g = nc.gpsimd
            pool.wait_ge(consts_dve, 3)
            for m, fill in ((ident[:], 1.0), (ident_b[:], 1.0), (ident_mask[:, P:2 * P], MASKED)):
                g.affine_select(out=m, in_=m, compare_op=ALU.not_equal, fill=fill, base=0,
                                pattern=[[-1, P]], channel_multiplier=1).then_inc(consts_pool, 1)

            def step(s):
                a, b, d, c, e = stages(s)
                if e.exists():
                    pool.wait_ge(aggr_done, 2 * e.number + 2)
                    pool.sem_inc(passed, 1)
                    g.tensor_scalar(rstd[:], mean_var[:, :, 1], LN_EPS, None, ALU.add
                                    ).then_inc(var_eps, 1)
                    pool.wait_ge(var_eps, e.number + 1)
                    g.tensor_tensor(rstd[:], rstd[:], neg_half[:], ALU.pow).then_inc(rstd_done, 1)
                if d.exists():
                    pool.wait_ge(mask_in[d.slot], 16 * (d.turns + 1))
                    if s.shift(-1).exists():
                        pool.wait_ge(scores_exp, 8 * s.number)
                    pool.sem_inc(passed, 1)
                    g.tensor_scalar(masked[d.slot][:], mask_raw[d.slot][:], 0, None, ALU.is_equal
                                    ).then_inc(mask_done, 1)
                if c.exists():
                    for which, out in ((0, q_out), (1, k_out)):
                        sl = slice(2 * which, 2 * which + 2)
                        pool.wait_ge(out, 4 * c.number + 4)
                        if which == 0 and c.shift(-1).exists():
                            pool.wait_ge(rest_low, 2 * c.number)
                        g.tensor_tensor(rest[:, sl], full[:, sl], parts[:, sl, 0], ALU.subtract
                                        ).then_inc(rest1, 1)
                        pool.wait_ge(mid, 2 * c.number + which + 1)
                        g.tensor_tensor(parts[:, sl, 2], rest[:, sl], parts[:, sl, 1], ALU.subtract
                                        ).then_inc(rest_low, 1)
                if d.exists():
                    pool.wait_ge(xn_done, 2 * d.number + 2)
                    xs = x_res[:, bass.ds(d.number * ROW, ROW)].rearrange("p (t d) -> p t d", t=TILES)
                    g.tensor_tensor(xs, xs, o_bias[:].unsqueeze(1).to_broadcast([P, TILES, D]), ALU.add
                                    ).then_inc(bias_done, 1)

            pipeline(pool, step, FIRST, LAST, *STEADY)

        @block.vector
        def _(dve):
            v = nc.vector
            v.memset(ident[:], 0.0).then_inc(consts_dve, 1)
            v.memset(ident_b[:], 0.0).then_inc(consts_dve, 1)
            v.memset(ident_mask[:], 0.0).then_inc(consts_dve, 1)
            v.memset(neg_half[:], -0.5).then_inc(consts_dve, 1)
            v.memset(ones_col[:], 1.0).then_inc(consts_dve, 1)
            v.memset(ones_b[:], 1.0).then_inc(consts_dve, 1)
            v.memset(ones_rows[:], 1.0).then_inc(consts_dve, 1)
            for r in range(3):
                v.memset(values[r][:], 0.0).then_inc(consts_dve, 1)
            dve.wait_ge(consts_dve, 10)
            for r in range(3):
                v.memset(values[r][:, :, :, DK:DK + 1], 1.0).then_inc(consts_dve, 1)
            dve.wait_ge(weights_in, 112)
            v.tensor_scalar(qk_bias[:, 0:2], qk_bias[:, 0:2], 0.25, None, ALU.mult).then_inc(consts_dve, 1)

            v.tensor_scalar(o_bias[:], o_bias[:], gates[:, 0:1], None, ALU.mult).then_inc(consts_dve, 1)

            def step(s):
                a, b, d, c, e = stages(s)
                z = s.shift(-1)

                def maxima(first, last):
                    if not b.exists():
                        return
                    for h in range(first, last + 1):
                        dve.wait_ge(scores_max, HEADS * b.number + h + 1)
                        if h == 0 and s.exists():
                            dve.wait_ge(max_split, s.number + 1)
                        v.tensor_reduce(row_max[:, :, h], ps_max[h % 2][:], AX_X, ALU.max,
                                        negate=True).then_inc(max_done, 1)

                def normalise(t):
                    if not z.exists():
                        return
                    dve.wait_ge(nat_ready, 2 * z.number + t + 1)
                    if t == 0 and z.shift(-1).exists():
                        dve.wait_ge(heads_ready, z.number)
                    nat = ps_misc[:].rearrange("p g (h k) -> p (g h) k", k=32)
                    v.reciprocal(inv_sum[:, t], nat[:, :, DK]).then_inc(inv_done, 1)
                    dve.wait_ge(inv_done, 2 * z.number + t + 1)
                    v.tensor_tensor(heads_out[:, t].rearrange("p (h k) -> p h k", k=DK),
                                    nat[:, :, 0:DK],
                                    inv_sum[:, t].unsqueeze(2).to_broadcast([P, HEADS, DK]), ALU.mult
                                    ).then_inc(nat_done, 1)

                if e.exists():
                    dve.wait_ge(x_in[e.slot], 16 * (e.turns + 1))
                    if c.exists():
                        dve.wait_ge(xn_done, 2 * e.number)
                    dve.sem_inc(passed, 1)
                    for t in range(TILES):
                        v.bn_stats(stats[:, t], x_res[:, bass.ds(e.number * ROW + t * D, D)]
                                   ).then_inc(stats_done, 1)
                    dve.wait_ge(stats_done, 2 * e.number + 2)
                    dve.sem_inc(passed, 1)
                    for t in range(TILES):
                        v.bn_aggr(mean_var[:, t], stats[:, t]).then_inc(aggr_done, 1)
                maxima(0, 2)
                normalise(0)
                maxima(3, 4)
                normalise(1)
                maxima(5, 5)
                if e.exists():
                    dve.wait_ge(rstd_done, e.number + 1)
                    if c.exists():
                        dve.wait_ge(xnt_ready, c.number + 1)
                    for t in range(TILES):
                        v.tensor_scalar(xn[:, t], x_res[:, bass.ds(e.number * ROW + t * D, D)],
                                        mean_var[:, t, 0:1], rstd[:, t:t + 1], ALU.subtract, ALU.mult
                                        ).then_inc(xn_done, 1)
                maxima(6, 6)
                if c.exists():
                    dve.wait_ge(rest1, 2 * c.number + 1)
                    v.tensor_copy(parts[:, 0:2, 1], rest[:, 0:2]).then_inc(mid, 1)
                maxima(7, 10)
                if z.exists():
                    dve.wait_ge(wo_ready, z.number + 1)
                    dve.wait_ge(bias_done, z.number + 1)
                    xs = x_res[:, bass.ds(z.number * ROW, ROW)]
                    v.scalar_tensor_tensor(xs, ps_misc[:].rearrange("p t d -> p (t d)"),
                                           gates[:, 0:1], xs, ALU.mult, ALU.add).then_inc(res_done, 1)
                maxima(11, 11)
                if c.exists():
                    dve.wait_ge(rest1, 2 * c.number + 2)
                    v.tensor_copy(parts[:, 2:4, 1], rest[:, 2:4]).then_inc(mid, 1)
                maxima(12, 12)
                if d.exists():
                    dve.wait_ge(v_ready, d.number + 1)
                    if z.exists():
                        dve.wait_ge(pv_done, 8 * z.number + 8)
                    for t in range(TILES):
                        v.tensor_tensor(values[d.slot][:, t, :, 0:DK],
                                        ps_misc[:, t].rearrange("p (h k) -> p h k", k=DK),
                                        v_bias[:].rearrange("p (h k) -> p h k", k=DK), ALU.add
                                        ).then_inc(v_out, 1)
                maxima(13, 14)
                if d.exists():
                    dve.wait_ge(cols_ready, d.number + 1)
                    v.tensor_copy(masked_cols[:], ps_misc[:, 0, 0:1]).then_inc(cols_out, 1)
                maxima(15, 15)
                if b.exists():
                    dve.wait_ge(max_done, HEADS * b.number + HEADS)
                    if s.exists():
                        dve.wait_ge(max_t, s.number + 1)
                    v.tensor_copy(max_parts[:, :, 0], row_max[:]).then_inc(max_hi, 1)
                    dve.wait_ge(max_hi, b.number + 1)
                    v.tensor_tensor(max_rest[:], row_max[:], max_parts[:, :, 0], ALU.subtract
                                    ).then_inc(max_mid_rest, 1)
                    dve.wait_ge(max_mid_rest, b.number + 1)
                    v.tensor_copy(max_parts[:, :, 1], max_rest[:]).then_inc(max_mid, 1)
                    dve.wait_ge(max_mid, b.number + 1)
                    v.tensor_tensor(max_parts[:, :, 2], max_rest[:], max_parts[:, :, 1], ALU.subtract
                                    ).then_inc(max_split, 1)
                if d.exists():
                    dve.wait_ge(count_ready, d.number + 1)
                    v.tensor_copy(any_masked[d.slot][:], ps_misc[0:1, 0, 0:1]).then_inc(count_out, 1)
                    if b.exists():
                        v.tensor_tensor(pair_masked[d.slot][:], ps_misc[0:1, 0, 0:1],
                                        any_masked[b.slot][:], ALU.add).then_inc(count_out, 1)
                    else:
                        v.tensor_copy(pair_masked[d.slot][:], ps_misc[0:1, 0, 0:1]).then_inc(count_out, 1)

            pipeline(dve, step, FIRST, LAST, *STEADY)

        @block.scalar
        def _(act):
            s_ = nc.scalar
            act.wait_ge(weights_in, 112)
            act.wait_ge(consts_dve, 14)

            def step(s):
                a, b, d, c, e = stages(s)
                z = s.shift(-1)

                def exponentials(u):
                    if not a.exists():
                        return
                    act.wait_ge(scores_exp, 8 * a.number + u + 1)
                    if u >= 2 or a.shift(-1).exists():
                        act.wait_ge(pv_done, 8 * a.number + u - 1)
                    s_.activation(probs[u % 2][:], ps_exp[u % 2][:], ACT.Exp).then_inc(exp_done, 1)

                def copy_out(n, pair):
                    if not n.exists():
                        return
                    act.wait_ge(pv_done, 8 * n.number + 4 * pair + 4)
                    if pair == 0 and n.shift(-1).exists():
                        act.wait_ge(nat_ready, 2 * n.number)
                    s_.copy(out_raw[:, 2 * pair:2 * pair + 2], ps_out[:]).then_inc(out_copied, 1)

                def parts_of(which, ready, out):
                    if not c.exists():
                        return
                    act.wait_ge(ready, c.number + 1)
                    if c.shift(-1).exists():
                        act.wait_ge(rest_low, 2 * c.number)
                        before = c.shift(-1)
                        act.wait_ge(parts_out[before.slot], 64 * (before.turns + 1))
                    scale = 0.25 if which == 0 else 1.0
                    for m in range(2):
                        bias = qk_bias[:, 2 * which + m:2 * which + m + 1]
                        s_.activation(full[:, 2 * which + m], ps_misc[:, m], ACT.Identity, bias=bias,
                                      scale=scale).then_inc(out, 1)
                        s_.activation(parts[:, 2 * which + m, 0], ps_misc[:, m], ACT.Identity,
                                      bias=bias, scale=scale).then_inc(out, 1)

                if c.exists():
                    act.wait_ge(xnt_ready, c.number + 1)
                    if c.shift(-1).exists():
                        act.wait_ge(q_ready, c.number)
                    s_.copy(xn_t[:], ps_misc[:]).then_inc(xnt_out, 1)
                copy_out(z, 1)
                parts_of(0, q_ready, q_out)
                exponentials(0)
                exponentials(1)
                exponentials(2)
                if z.exists():
                    act.wait_ge(heads_ready, z.number + 1)
                    if z.shift(-1).exists():
                        act.wait_ge(wo_ready, z.number)
                    s_.copy(heads_t[:], ps_misc[:]).then_inc(heads_out_t, 1)
                parts_of(1, k_ready, k_out)
                exponentials(3)
                exponentials(4)
                copy_out(a, 0)
                exponentials(5)
                exponentials(6)
                if b.exists():
                    act.wait_ge(max_t, b.number + 1)
                    if s.exists():
                        act.wait_ge(shift_in[s.slot], 48 * (s.turns + 1))
                    s_.copy(max_rows[:], ps_bits).then_inc(max_t_out, 1)
                exponentials(7)

            pipeline(act, step, FIRST, LAST, *STEADY)

        @block.tensor
        def _(pe):
            t_ = nc.tensor
            flag = pe.alloc_register("flag")
            pe.wait_ge(weights_in, 112)
            pe.wait_ge(consts_dve, 13)
            pe.wait_ge(ones_in, 48)
            pe.wait_ge(consts_pool, 3)

            def step(s):
                a, b, d, c, e = stages(s)
                z = s.shift(-1)

                def exp_scores(u, with_mask):
                    if not a.exists():
                        return
                    group, kt = u // 2, u % 2
                    if u == 0:
                        pe.wait_ge(shift_in[a.slot], 48 * (a.turns + 1))
                    if u >= 2 or a.shift(-1).exists():
                        pe.wait_ge(exp_done, 8 * a.number + u - 1)
                    for i in range(4):
                        h = 4 * group + i
                        out = ps_exp[u % 2][:, i]
                        mm = t_.matmul(out, k_stack[a.slot][:, h, kt * P:(kt + 1) * P],
                                       q_stack[a.slot][:, h, :], start=True, stop=not with_mask)
                        if with_mask:
                            for t in range(TILES):
                                mm = t_.matmul(out, masked[a.slot][:, t, kt * P:(kt + 1) * P],
                                               ident_mask[:, (1 - t) * P:(3 - t) * P],
                                               start=False, stop=t == TILES - 1)
                    mm.then_inc(scores_exp, 1)

                def max_scores(slot, point, with_mask):
                    if not b.exists() or (slot, point) not in HEADS_AT:
                        return
                    h = HEADS_AT[slot, point]
                    if h == 0:
                        pe.wait_ge(stack_in[b.slot], 96 * (b.turns + 1))
                    if h >= 2 or s.exists():
                        pe.wait_ge(max_done, HEADS * b.number + h - 1)
                    for t in range(TILES):
                        out = ps_max[h % 2][:, t]
                        mm = t_.matmul(out, q_stack[b.slot][0:KROWS, h, t * P:(t + 1) * P],
                                       k_stack[b.slot][0:KROWS, h, :], start=True, stop=not with_mask)
                        if with_mask:
                            mm = t_.matmul(out, ident_mask[:, P:2 * P], masked[b.slot][:, t, :],
                                           start=False, stop=True)
                    mm.then_inc(scores_max, 1)

                def weigh_values(n, u):
                    if not n.exists():
                        return
                    group, kt = u // 2, u % 2
                    pe.wait_ge(exp_done, 8 * n.number + u + 1)
                    if u % 4 == 0 and (u or n.shift(-1).exists()):
                        pe.wait_ge(out_copied, 2 * n.number + u // 4)
                    for i in range(4):
                        mm = t_.matmul(ps_out[32 * i:32 * i + 32, group % 2, :],
                                       values[n.slot][:, kt, 4 * group + i, :], probs[u % 2][:, i, :],
                                       start=kt == 0, stop=kt == 1, skip_group_check=True)
                    mm.then_inc(pv_done, 1)

                def misc(slot):
                    if slot == 0 and c.exists():
                        pe.wait_ge(xn_done, 2 * c.number + 2)
                        if b.exists():
                            pe.wait_ge(count_out, 2 * b.number + 2)
                        elif d.exists():
                            pe.wait_ge(k_out, 4 * d.number + 4)
                        for t in range(TILES):
                            for k in range(2):
                                mm = t_.transpose(ps_misc[:, k, t * P:(t + 1) * P],
                                                  xn[:, t, k * P:(k + 1) * P], ident[:])
                        mm.then_inc(xnt_ready, 1)
                    if slot in (1.5, 2) and z.exists():
                        t = 0 if slot == 1.5 else 1
                        if t == 1:
                            pe.wait_ge(nat_done, 2 * z.number + 1)
                        else:
                            pe.wait_ge(out_copied, 2 * z.number + 2)
                            if c.exists():
                                pe.wait_ge(q_out, 4 * c.number + 4)
                            elif b.exists():
                                pe.wait_ge(count_out, 2 * b.number + 2)
                            elif s.exists():
                                pe.wait_ge(max_t_out, s.number + 1)
                            else:
                                pe.wait_ge(res_done, z.number)
                        for k in range(4):
                            mm = t_.transpose(ps_misc[:, k // 2, (k % 2) * P:(k % 2 + 1) * P],
                                              out_raw[:, k, t * P:(t + 1) * P], ident[:])
                        mm.then_inc(nat_ready, 1)
                    if slot in (0.25, 3) and c.exists():
                        if slot == 0.25:
                            pe.wait_ge(xnt_out, c.number + 1)
                            w, moving, ready = wq, xn_t, q_ready
                        else:
                            pe.wait_ge(q_out, 4 * c.number + 4)
                            pe.wait_ge(ctx_in[c.slot], 16 * (c.turns + 1))
                            if z.exists():
                                pe.wait_ge(heads_out_t, z.number + 1)
                            w, moving, ready = wk, ctx_t[c.slot], k_ready
                        for m in range(2):
                            for k in range(2):
                                mm = t_.matmul(ps_misc[:, m], w[:, k, m * P:(m + 1) * P],
                                               moving[:, k, :], start=k == 0, stop=k == 1)
                        mm.then_inc(ready, 1)
                    if slot == 2.5 and z.exists():
                        pe.wait_ge(nat_done, 2 * z.number + 2)
                        if c.exists():
                            pe.wait_ge(q_out, 4 * c.number + 4)
                        for t in range(TILES):
                            for k in range(2):
                                mm = t_.transpose(ps_misc[:, k, t * P:(t + 1) * P],
                                                  heads_out[:, t, k * P:(k + 1) * P], ident[:])
                        mm.then_inc(heads_ready, 1)
                    if slot == 4 and z.exists():
                        pe.wait_ge(heads_out_t, z.number + 1)
                        if c.exists():
                            pe.wait_ge(k_out, 4 * c.number + 4)
                        for t in range(TILES):
                            for k in range(2):
                                mm = t_.matmul(ps_misc[:, t], heads_t[:, k, t * P:(t + 1) * P],
                                               wo[:, k, :], start=k == 0, stop=k == 1)
                        mm.then_inc(wo_ready, 1)
                    if slot == 4.5 and d.exists():
                        pe.wait_ge(ctx_in[d.slot], 16 * (d.turns + 1))
                        if z.exists():
                            pe.wait_ge(res_done, z.number + 1)
                        else:
                            pe.wait_ge(k_out, 4 * c.number + 4)
                        for t in range(TILES):
                            for k in range(2):
                                mm = t_.matmul(ps_misc[:, t], ctx_t[d.slot][:, k, t * P:(t + 1) * P],
                                               wv[:, k, :], start=k == 0, stop=k == 1)
                        mm.then_inc(v_ready, 1)
                    if slot == 5.5 and d.exists():
                        pe.wait_ge(v_out, 2 * d.number + 2)
                        pe.wait_ge(mask_done, d.number + 1)
                        for n in range(2 * TILES):
                            mm = t_.matmul(ps_misc[:, 0, 0:1],
                                           masked[d.slot][:, n // 2, (n % 2) * P:(n % 2 + 1) * P],
                                           ones_b[:], start=n == 0, stop=n == 2 * TILES - 1)
                        mm.then_inc(cols_ready, 1)
                    if slot == 6.5 and b.exists():
                        pe.wait_ge(max_split, b.number + 1)
                        if d.exists():
                            pe.wait_ge(cols_out, d.number + 1)
                        elif z.exists():
                            pe.wait_ge(res_done, z.number + 1)
                        pe.sem_inc(passed, 1)
                        for t in range(TILES):
                            mm = t_.transpose(ps_bits[:, t * P:(t + 1) * P],
                                              max_parts[:, t].rearrange("p i h -> p (i h)"), ident_b[:])
                        mm.then_inc(max_t, 1)
                    if slot == 7.5 and d.exists():
                        pe.wait_ge(cols_out, d.number + 1)
                        if b.exists():
                            pe.wait_ge(max_t_out, b.number + 1)
                        t_.matmul(ps_misc[0:1, 0, 0:1], masked_cols[:], ones_col[:], start=True,
                                  stop=True).then_inc(count_ready, 1)

                def body(with_mask):
                    for slot in range(8):
                        misc(slot)
                        max_scores(slot, 0, with_mask)
                        if slot == 0:
                            weigh_values(z, 7)
                            misc(0.25)
                            max_scores(slot, 1, with_mask)
                        exp_scores(slot, with_mask)
                        if slot == 6:
                            weigh_values(a, slot - 1)
                        if slot in (2, 4):
                            max_scores(slot, 1, with_mask)
                        misc(slot + 0.5)
                        if slot not in (0, 2, 4):
                            max_scores(slot, 1, with_mask)
                        if slot and slot != 6:
                            weigh_values(a, slot - 1)
                        max_scores(slot, 2, with_mask)

                if a.exists() or b.exists():
                    if b.exists():
                        pe.wait_ge(count_out, 2 * b.number + 2)
                        pe.sem_inc(passed, 1)
                    pe.reg_load(flag, pair_masked[(b if b.exists() else a).slot][0:1, 0:1])
                    with pe.If_ne(flag, 0):
                        body(True)
                    with pe.Else():
                        body(False)
                else:
                    body(False)

            pipeline(pe, step, FIRST, LAST, *STEADY)


def ternary_ffn(nc, dram, passed, x_res, gates):
    with ExitStack() as ctx:
        def sb(name, shape, dt=F32):
            return ctx.enter_context(nc.sbuf_tensor(name, shape, dt))

        sem = phase_semaphores(nc, ctx, "f")

        def ps(name, shape, dt=F32):
            return ctx.enter_context(nc.psum_tensor(name, shape, dt))

        KH = HIDDEN // P
        w1 = sb("f_w1", [P, 2 * HIDDEN])
        w2 = sb("f_w2", [P, KH * D])
        w1_q = sb("f_w1_q", [P, 2, HIDDEN], BF16)
        w2_q = sb("f_w2_q", [P, KH, D], BF16)
        b1 = sb("f_b1", [P, HIDDEN])
        b2 = sb("f_b2", [P, D])
        abs_sum = sb("f_abs_sum", [P, 2])
        w_mean = sb("f_w_mean", [P, 2])
        w_inv = sb("f_w_inv", [P, 2])
        out_scale = sb("f_out_scale", [P, 2])
        ones = sb("f_ones", [P, P])
        ident = sb("f_ident", [P, P])
        neg_half = sb("f_neg_half", [P, TILES])
        neg_one = sb("f_neg_one", [P, TILES])
        stats = sb("f_stats", [P, TILES, 6])
        mean_var = sb("f_mean_var", [P, TILES, 2])
        neg_mean = sb("f_neg_mean", [P, TILES])
        centred = sb("f_centred", [P, TILES, D])
        x_max = sb("f_x_max", [P, TILES])
        chain = sb("f_chain", [P, 3, TILES])
        x_mul = [sb(f"f_x_mul{r}", [P, TILES]) for r in range(3)]
        x_scale = [sb(f"f_x_scale{r}", [P, TILES]) for r in range(3)]
        x_int = sb("f_x_int", [P, TILES, D])
        x_int_t = sb("f_x_int_t", [P, 2, SEQ], BF16)
        h = [sb(f"f_h{r}", [P, TILES, HIDDEN]) for r in range(3)]
        squares = sb("f_squares", [P, HIDDEN], BF16)
        h_sum = sb("f_h_sum", [P, TILES])
        h_max = sb("f_h_max", [P, TILES])
        h_chain = sb("f_h_chain", [P, 3, TILES])
        h_mul = [sb(f"f_h_mul{r}", [P, TILES]) for r in range(3)]
        h_scale = [sb(f"f_h_scale{r}", [P, TILES]) for r in range(3)]
        h_int_t = [sb(f"f_h_int_t{t}", [P, KH, P], BF16) for t in range(TILES)]
        ps_h = [ps(f"f_ps_h{t}", [P, HIDDEN]) for t in range(TILES)]
        ps_x = ps("f_ps_x", [P, 2, SEQ])
        ps_g = ps("f_ps_g", [P, KH, P])
        ps_o = ps("f_ps_o", [P, TILES, D])

        mean_done = sem("f_mean_done")
        w_in, consts = sem("f_w_in"), sem("f_consts")
        ident_done = sem("f_ident_done")
        w_abs, w_total, w_done = sem("f_w_abs"), sem("f_w_total"), sem("f_w_done")
        stats_done, aggr_done, centred_done, max_done = (
            sem(f"f_{n}") for n in ("stats_done", "aggr_done", "centred_done", "max_done"))
        chain1, x_scaled, bias_done = sem("f_chain1"), sem("f_x_scaled"), sem("f_bias_done")
        x_int_done, x_turned, x_int_out = (sem(f"f_{n}") for n in ("x_int_done", "x_turned", "x_int_out"))
        h_ready, h_done, gelu_done, sum_done, hmax_done = (
            sem(f"f_{n}") for n in ("h_ready", "h_done", "gelu_done", "sum_done", "hmax_done"))
        chain2, h_scaled = sem("f_chain2"), sem("f_h_scaled")
        h_int_done, h_turned, h_int_out, o_ready, res_done = (
            sem(f"f_{n}") for n in ("h_int_done", "h_turned", "h_int_out", "o_ready", "res_done"))

        FIRST, LAST = -2, BATCHES
        STEADY = (2, BATCHES - 3)

        def stages(s):
            return s, s.shift(1), s.shift(2)

        block = ctx.enter_context(nc.Block())

        @block.sync
        def _(sp):
            sp.dma_start(w1[:], dram["w1"].rearrange("p c h -> p (c h)")).then_inc(w_in, 16)
            sp.dma_start(w2[:], dram["w2"].rearrange("p c d -> p (c d)")).then_inc(w_in, 16)
            sp.dma_start(b1[:], dram["b1"].partition_broadcast(P)).then_inc(w_in, 16)
            sp.dma_start(b2[:], dram["b2"].partition_broadcast(P)).then_inc(w_in, 16)
            sp.wait_ge(w_in, 64)

        @block.gpsimd
        def _(pool):
            g = nc.gpsimd
            pool.wait_ge(consts, 4)
            g.affine_select(out=ident[:], in_=ident[:], compare_op=ALU.not_equal, fill=1.0, base=0,
                            pattern=[[-1, P]], channel_multiplier=1).then_inc(ident_done, 1)
            pool.wait_ge(w_done, 12)

            def step(s):
                a, c, e = stages(s)
                if e.exists():
                    pool.wait_ge(aggr_done, 2 * e.number + 2)
                    pool.wait_ge(max_done, e.number + 1)
                    if s.shift(-1).exists():
                        pool.wait_ge(h_done, 2 * s.number)
                    factor, scale, inv = chain[:, 0], chain[:, 1], chain[:, 2]
                    n = 5 * e.number
                    pool.sem_inc(passed, 1)
                    g.tensor_scalar(factor, mean_var[:, :, 1], 1.0 + RMS_EPS, RMS_EPS * LN_EPS, ALU.mult,
                                    ALU.add).then_inc(chain1, 1)
                    pool.wait_ge(chain1, n + 1)
                    g.tensor_tensor(factor, factor, neg_half[:], ALU.pow).then_inc(chain1, 1)
                    pool.wait_ge(chain1, n + 2)
                    g.tensor_tensor(scale, x_max[:], factor, ALU.mult).then_inc(chain1, 1)
                    pool.wait_ge(chain1, n + 3)
                    pool.sem_inc(passed, 1)
                    g.tensor_scalar(scale, scale, QUANT_EPS, 1.0 / 127.0, ALU.max, ALU.mult
                                    ).then_inc(chain1, 1)
                    pool.wait_ge(chain1, n + 4)
                    g.tensor_tensor(inv, scale, neg_one[:], ALU.pow).then_inc(chain1, 1)
                    pool.wait_ge(chain1, n + 5)
                    g.tensor_tensor(x_mul[e.slot][:], inv, factor, ALU.mult).then_inc(x_scaled, 1)
                    g.tensor_scalar(x_scale[e.slot][:], scale, out_scale[:, 0:1], None, ALU.mult
                                    ).then_inc(x_scaled, 1)
                    pool.wait_ge(centred_done, 2 * e.number + 2)
                    xs = x_res[:, bass.ds(e.number * ROW, ROW)].rearrange("p (t d) -> p t d", t=TILES)
                    g.tensor_tensor(xs, xs, b2[:].unsqueeze(1).to_broadcast([P, TILES, D]), ALU.add
                                    ).then_inc(bias_done, 1)
                if c.exists():
                    pool.wait_ge(sum_done, 2 * c.number + 2)
                    pool.wait_ge(hmax_done, 2 * c.number + 2)
                    if s.shift(-1).exists():
                        pool.wait_ge(res_done, 2 * s.number)
                    factor, scale, inv = h_chain[:, 0], h_chain[:, 1], h_chain[:, 2]
                    n = 5 * c.number
                    pool.sem_inc(passed, 1)
                    g.tensor_scalar(factor, h_sum[:], 1.0 / HIDDEN, RMS_EPS, ALU.mult, ALU.add
                                    ).then_inc(chain2, 1)
                    pool.wait_ge(chain2, n + 1)
                    g.tensor_tensor(factor, factor, neg_half[:], ALU.pow).then_inc(chain2, 1)
                    pool.wait_ge(chain2, n + 2)
                    g.tensor_tensor(scale, h_max[:], factor, ALU.mult).then_inc(chain2, 1)
                    pool.wait_ge(chain2, n + 3)
                    pool.sem_inc(passed, 1)
                    g.tensor_scalar(scale, scale, QUANT_EPS, 1.0 / 127.0, ALU.max, ALU.mult
                                    ).then_inc(chain2, 1)
                    pool.wait_ge(chain2, n + 4)
                    g.tensor_tensor(inv, scale, neg_one[:], ALU.pow).then_inc(chain2, 1)
                    pool.wait_ge(chain2, n + 5)
                    g.tensor_tensor(h_mul[c.slot][:], inv, factor, ALU.mult).then_inc(h_scaled, 1)
                    g.tensor_scalar(h_scale[c.slot][:], scale, out_scale[:, 1:2], None, ALU.mult
                                    ).then_inc(h_scaled, 1)

            pipeline(pool, step, FIRST, LAST, *STEADY)

        @block.vector
        def _(dve):
            v = nc.vector
            v.memset(ones[:], 1.0).then_inc(consts, 1)
            v.memset(ident[:], 0.0).then_inc(consts, 1)
            v.memset(neg_half[:], -0.5).then_inc(consts, 1)
            v.memset(neg_one[:], -1.0).then_inc(consts, 1)
            dve.wait_ge(w_in, 64)
            for i, w in ((0, w1), (1, w2)):
                v.tensor_reduce(abs_sum[:, i:i + 1], w[:], AX_X, ALU.add,
                                apply_absolute_value=True).then_inc(w_abs, 1)
            dve.wait_ge(w_total, 1)
            v.tensor_scalar(w_mean[:], ps_o[:, 0, 0:2], 1.0 / (HIDDEN * D), QUANT_EPS, ALU.mult, ALU.max
                            ).then_inc(w_done, 1)
            dve.wait_ge(w_done, 1)
            v.reciprocal(w_inv[:], w_mean[:]).then_inc(w_done, 1)
            v.tensor_copy(out_scale[:], w_mean[:]).then_inc(w_done, 1)
            dve.wait_ge(w_done, 3)
            v.tensor_scalar(out_scale[:, 1:2], out_scale[:, 1:2], gates[:, 2:3], None, ALU.mult
                            ).then_inc(w_done, 1)
            v.tensor_scalar(b2[:], b2[:], gates[:, 2:3], None, ALU.mult).then_inc(w_done, 1)
            n = 5
            for i, w, q in ((0, w1, w1_q), (1, w2, w2_q)):
                flat = q[:].rearrange("p c n -> p (c n)")
                v.tensor_scalar(w[:], w[:], w_inv[:, i:i + 1], ROUND, ALU.mult, ALU.add).then_inc(w_done, 1)
                dve.wait_ge(w_done, n + 1)
                v.tensor_scalar(w[:], w[:], ROUND, 1.0, ALU.subtract, ALU.min).then_inc(w_done, 1)
                dve.wait_ge(w_done, n + 2)
                v.tensor_scalar(flat, w[:], -1.0, None, ALU.max).then_inc(w_done, 1)
                n += 3
            v.memset(squares[:], 0.0).then_inc(w_done, 1)
            dve.wait_ge(w_done, 12)

            def step(s):
                a, c, e = stages(s)

                def quantise_h(t):
                    if a.exists():
                        dve.wait_ge(h_scaled, 2 * a.number + 2)
                        hs = h[a.slot][:, t]
                        v.tensor_scalar(hs, hs, h_mul[a.slot][:, t:t + 1], ROUND, ALU.mult, ALU.add
                                        ).then_inc(h_int_done, 1)

                def hidden(t):
                    if c.exists():
                        dve.wait_ge(h_ready, 2 * c.number + t + 1)
                        if s.shift(-2).exists():
                            dve.wait_ge(h_turned, 2 * s.number - 2)
                        v.scalar_tensor_tensor(h[c.slot][:, t], ps_h[t][:], x_scale[c.slot][:, t:t + 1],
                                               b1[:], ALU.mult, ALU.add).then_inc(h_done, 1)

                if e.exists():
                    def x_tile(t):
                        return x_res[:, bass.ds(e.number * ROW + t * D, D)]

                    if c.exists():
                        dve.wait_ge(x_scaled, 2 * e.number)
                        dve.wait_ge(x_int_done, 2 * e.number)
                    dve.sem_inc(passed, 1)
                    for t in range(TILES):
                        v.bn_stats(stats[:, t], x_tile(t)).then_inc(stats_done, 1)
                    dve.wait_ge(stats_done, 2 * e.number + 2)
                    dve.sem_inc(passed, 1)
                    for t in range(TILES):
                        v.bn_aggr(mean_var[:, t], stats[:, t]).then_inc(aggr_done, 1)
                    dve.wait_ge(aggr_done, 2 * e.number + 2)
                    v.tensor_scalar(neg_mean[:], mean_var[:, :, 0], -1.0, None, ALU.mult
                                    ).then_inc(mean_done, 1)
                hidden(0)
                if e.exists():
                    dve.wait_ge(centred_done, 2 * e.number + 2)
                    v.tensor_reduce(x_max[:], centred[:], AX_X, ALU.max, apply_absolute_value=True
                                    ).then_inc(max_done, 1)
                quantise_h(0)
                z = s.shift(-1)
                if z.exists():
                    dve.wait_ge(bias_done, z.number + 1)
                    dve.wait_ge(o_ready, TILES * z.number + TILES)
                    for t in range(TILES):
                        xs = x_res[:, bass.ds(z.number * ROW + t * D, D)]
                        v.scalar_tensor_tensor(xs, ps_o[:, t], h_scale[z.slot][:, t:t + 1], xs,
                                               ALU.mult, ALU.add).then_inc(res_done, 1)
                hidden(1)
                quantise_h(1)
                if e.exists():
                    dve.wait_ge(x_scaled, 2 * e.number + 2)
                    if c.exists():
                        dve.wait_ge(x_turned, c.number + 1)
                    for t in range(TILES):
                        v.tensor_scalar(x_int[:, t], centred[:, t], x_mul[e.slot][:, t:t + 1], ROUND,
                                        ALU.mult, ALU.add).then_inc(x_int_done, 1)
                if c.exists():
                    for t in range(TILES):
                        dve.wait_ge(gelu_done, 2 * c.number + t + 1)
                        if a.exists():
                            dve.wait_ge(h_scaled, 2 * a.number + 2)
                        v.tensor_reduce(h_max[:, t:t + 1], h[c.slot][:, t], AX_X, ALU.max,
                                        apply_absolute_value=True).then_inc(hmax_done, 1)

            pipeline(dve, step, FIRST, LAST, *STEADY)

        @block.scalar
        def _(act):
            s_ = nc.scalar
            act.wait_ge(w_done, 12)

            def step(s):
                a, c, e = stages(s)

                def turned_h(t):
                    if a.exists():
                        act.wait_ge(h_turned, 2 * a.number + t + 1)
                        if s.shift(-1).exists():
                            act.wait_ge(o_ready, 2 * a.number)
                        s_.activation(h_int_t[t][:], ps_g[:], ACT.Copy, bias=-ROUND).then_inc(h_int_out, 1)

                def gelu(t):
                    if c.exists():
                        hs = h[c.slot][:, t]
                        act.wait_ge(h_done, 2 * c.number + t + 1)
                        s_.activation(hs, hs, ACT.Gelu).then_inc(gelu_done, 1)
                        act.wait_ge(gelu_done, 2 * c.number + t + 1)
                        if a.exists():
                            act.wait_ge(h_scaled, 2 * a.number + 2)
                        if t or a.exists():
                            act.wait_ge(sum_done, 2 * c.number + t)
                        s_.activation(squares[:], hs, ACT.Square, accum_out=h_sum[:, t:t + 1]
                                      ).then_inc(sum_done, 1)

                if e.exists():
                    act.wait_ge(mean_done, e.number + 1)
                    if c.exists():
                        act.wait_ge(x_int_done, 2 * e.number)
                    for t in range(TILES):
                        s_.activation(centred[:, t], x_res[:, bass.ds(e.number * ROW + t * D, D)],
                                      ACT.Identity, bias=neg_mean[:, t:t + 1]).then_inc(centred_done, 1)
                gelu(0)
                turned_h(0)
                gelu(1)
                if e.exists():
                    act.wait_ge(x_turned, e.number + 1)
                    if c.exists():
                        act.wait_ge(h_ready, 2 * c.number + 2)
                    s_.activation(x_int_t[:], ps_x[:], ACT.Copy, bias=-ROUND).then_inc(x_int_out, 1)
                turned_h(1)

            pipeline(act, step, FIRST, LAST, *STEADY)

        @block.tensor
        def _(pe):
            t_ = nc.tensor
            pe.wait_ge(w_abs, 2)
            pe.wait_ge(consts, 4)
            t_.matmul(ps_o[:, 0, 0:2], ones[:], abs_sum[:], start=True, stop=True).then_inc(w_total, 1)
            pe.wait_ge(ident_done, 1)
            pe.wait_ge(w_done, 12)

            def step(s):
                a, c, e = stages(s)

                def first(t):
                    if c.exists():
                        if t == 0:
                            pe.wait_ge(x_int_out, c.number + 1)
                        if a.exists():
                            pe.wait_ge(h_done, 2 * c.number + t - 1)
                        for half in range(2):
                            for k in range(2):
                                mm = t_.matmul(ps_h[t][:, half * 512:half * 512 + 512],
                                               x_int_t[:, k, t * P:(t + 1) * P],
                                               w1_q[:, k, half * 512:half * 512 + 512],
                                               start=k == 0, stop=k == 1)
                        mm.then_inc(h_ready, 1)

                def turn(t):
                    if a.exists():
                        pe.wait_ge(h_int_done, 2 * a.number + t + 1)
                        if t or s.shift(-1).exists():
                            pe.wait_ge(h_int_out, 2 * a.number + t)
                        for k in range(KH):
                            mm = t_.transpose(ps_g[:, k], h[a.slot][:, t, k * P:(k + 1) * P], ident[:])
                        mm.then_inc(h_turned, 1)

                def second(n, t):
                    if n.exists():
                        pe.wait_ge(h_int_out, 2 * n.number + t + 1)
                        if t == 0 and n.shift(-1).exists():
                            pe.wait_ge(res_done, 2 * n.number)
                        for k in range(KH):
                            mm = t_.matmul(ps_o[:, t], h_int_t[t][:, k], w2_q[:, k],
                                           start=k == 0, stop=k == KH - 1)
                        mm.then_inc(o_ready, 1)

                first(0)
                second(s.shift(-1), 1)
                first(1)
                turn(0)
                second(a, 0)
                turn(1)
                if e.exists():
                    pe.wait_ge(x_int_done, 2 * e.number + 2)
                    if c.exists():
                        pe.wait_ge(x_int_out, c.number + 1)
                    for t in range(TILES):
                        for k in range(2):
                            mm = t_.transpose(ps_x[:, k, t * P:(t + 1) * P],
                                              x_int[:, t, k * P:(k + 1) * P], ident[:])
                    mm.then_inc(x_turned, 1)

            pipeline(pe, step, FIRST, LAST, *STEADY)


def causal_attention(nc, dram, passed, x_res, gates, logits, out):
    with ExitStack() as ctx:
        def sb(name, shape, dt=F32):
            return ctx.enter_context(nc.sbuf_tensor("c_" + name, shape, dt))

        sem = phase_semaphores(nc, ctx, "c")

        def ps(name, shape, dt=F32):
            return ctx.enter_context(nc.psum_tensor("c_" + name, shape, dt))

        KEYS = P + SEQ
        ctx_t = [sb(f"ctx_t{r}", [P, 2, SEQ]) for r in range(3)]
        ctx_n = [sb(f"ctx_n{r}", [P, TILES, D]) for r in range(3)]
        gate_w = sb("gate_w", [P, 2, EXPERTS])
        ident = sb("ident", [P, P])
        causal = sb("causal", [P, KEYS])
        zero_row = sb("zero_row", [1, D + EXPERTS])
        neg_half = sb("neg_half", [P, TILES])
        stats = sb("stats", [P, 2, TILES, 6])
        mean_var = sb("mean_var", [P, 2, TILES, 2])
        rstd = sb("rstd", [P, 2, TILES])
        xn = sb("xn", [P, TILES, D])
        xn_t = sb("xn_t", [P, 2, SEQ])
        scores = sb("scores", [P, KEYS])
        neg_max = sb("neg_max", [P, TILES])
        probs = [sb(f"probs{r}", [P, KEYS]) for r in range(3)]
        sums = [sb(f"sums{r}", [P, TILES]) for r in range(3)]
        inv = sb("inv", [P, TILES])
        probs_t = sb("probs_t", [P, KEYS])
        y = [sb(f"y{r}", [P, TILES, D]) for r in range(3)]
        y_t = sb("y_t", [P, 2, SEQ])
        ps_x = ps("ps_x", [P, 2, SEQ])
        ps_s = ps("ps_s", [P, 512])
        ps_p = ps("ps_p", [P, 512])
        ps_v = ps("ps_v", [P, TILES, D])
        ps_y = ps("ps_y", [P, 2, SEQ])
        ps_l = ps("ps_l", [P, TILES, EXPERTS])

        w_in, consts, pool_consts = sem("w_in"), sem("consts"), sem("pool_consts")
        ctx_t_in = [sem(f"ctx_t_in{r}") for r in range(3)]
        ctx_n_in = [sem(f"ctx_n_in{r}") for r in range(3)]
        stats1, aggr1, rstd1, xn_done = sem("stats1"), sem("aggr1"), sem("rstd1"), sem("xn_done")
        stats2, aggr2, rstd2, y_done = sem("stats2"), sem("aggr2"), sem("rstd2"), sem("y_done")
        x_turned, x_out, s_ready, s_done = sem("x_turned"), sem("x_out"), sem("s_ready"), sem("s_done")
        max_done, exp_done = sem("max_done"), sem("exp_done")
        p_turned, p_out, v_ready = sem("p_turned"), sem("p_out"), sem("v_ready")
        inv_done, res_done = sem("inv_done"), sem("res_done")
        y_turned, y_out, l_ready, l_out = sem("y_turned"), sem("y_out"), sem("l_ready"), sem("l_out")
        table_out = [sem(f"table_out{r}") for r in range(3)]
        result_out = [sem(f"result_out{r}") for r in range(3)]
        zero_out = sem("zero_out")

        FIRST, LAST = -2, BATCHES
        STEADY = (4, BATCHES - 3)

        def stages(s):
            return s, s.shift(1), s.shift(2), s.shift(-1)

        def tile(n, t):
            return x_res[:, bass.ds(n.number * ROW + t * D, D)]

        block = ctx.enter_context(nc.Block())

        @block.sync
        def _(sp):
            sp.dma_start(gate_w[:], dram["gate_w"]).then_inc(w_in, 16)
            sp.wait_ge(consts, 3)
            sp.dma_start(dram["table"][0:1, :], zero_row[:]).then_inc(zero_out, 16)

            def step(s):
                a, c, e, z = stages(s)
                if e.exists():
                    if z.exists():
                        sp.wait_ge(s_ready, z.number + 1)
                        sp.wait_ge(v_ready, z.number + 1)
                    sp.dma_start(ctx_t[e.slot][:], dram["ctx_t"][bass.ds(e.number, 1)].rearrange(
                        "b (c p) k -> p (b c) k", p=P)).then_inc(ctx_t_in[e.slot], 16)
                    sp.dma_start(ctx_n[e.slot][:], dram["ctx"][bass.ds(e.number, 1)].rearrange(
                        "b (t p) d -> p (b t) d", p=P)).then_inc(ctx_n_in[e.slot], 16)
                if z.exists():
                    sp.wait_ge(y_done, 2 * z.number + 2)
                    rows = dram["table"][bass.ds(z.number * SEQ + 1, SEQ), 0:D]
                    sp.dma_start(rows.rearrange("(t p) d -> p t d", p=P), y[z.slot][:]
                                 ).then_inc(table_out[z.slot], 16)
                    sp.dma_start(out[bass.ds(z.number * SEQ, SEQ), :].rearrange("(t p) d -> p t d", p=P),
                                 x_res[:, bass.ds(z.number * ROW, ROW)].rearrange(
                                     "p (t d) -> p t d", t=TILES)).then_inc(result_out[z.slot], 16)

            pipeline(sp, step, FIRST, LAST, *STEADY)
            sp.wait_ge(zero_out, 16)
            for r in range(3):
                uses = len(range(r, BATCHES, 3))
                sp.wait_ge(table_out[r], 16 * uses)
                sp.wait_ge(result_out[r], 16 * uses)

        @block.gpsimd
        def _(pool):
            g = nc.gpsimd
            pool.wait_ge(consts, 4)
            g.affine_select(out=ident[:], in_=ident[:], compare_op=ALU.not_equal, fill=1.0, base=0,
                            pattern=[[-1, P]], channel_multiplier=1).then_inc(pool_consts, 1)
            for lo, hi, base in ((0, P, 0), (P, KEYS, P)):
                g.affine_select(out=causal[:, lo:hi], in_=causal[:, lo:hi], compare_op=ALU.is_ge,
                                fill=MASKED, base=base, pattern=[[-1, hi - lo]], channel_multiplier=1
                                ).then_inc(pool_consts, 1)

            def step(s):
                a, c, e, z = stages(s)
                for n, i, aggr, done, used in ((e, 0, aggr1, rstd1, xn_done), (a, 1, aggr2, rstd2, y_done)):
                    if n.exists():
                        pool.wait_ge(aggr, 2 * n.number + 2)
                        pool.sem_inc(passed, 1)
                        g.tensor_scalar(rstd[:, i], mean_var[:, i, :, 1], LN_EPS, None, ALU.add
                                        ).then_inc(done, 1)
                        pool.wait_ge(done, 2 * n.number + 1)
                        g.tensor_tensor(rstd[:, i], rstd[:, i], neg_half[:], ALU.pow).then_inc(done, 1)

            pipeline(pool, step, FIRST, LAST, *STEADY)

        @block.vector
        def _(dve):
            v = nc.vector
            v.memset(ident[:], 0.0).then_inc(consts, 1)
            v.memset(causal[:], 0.0).then_inc(consts, 1)
            v.memset(zero_row[:], 0.0).then_inc(consts, 1)
            v.memset(neg_half[:], -0.5).then_inc(consts, 1)
            dve.wait_ge(pool_consts, 3)

            def tile_stats(n, i, done):
                dve.sem_inc(passed, 1)
                for t in range(TILES):
                    v.bn_stats(stats[:, i, t], tile(n, t)).then_inc(done, 1)

            def mean_variance(n, i, stats_done, done):
                dve.wait_ge(stats_done, 2 * n.number + 2)
                dve.sem_inc(passed, 1)
                for t in range(TILES):
                    v.bn_aggr(mean_var[:, i, t], stats[:, i, t]).then_inc(done, 1)

            def step(s):
                a, c, e, z = stages(s)
                if e.exists():
                    if c.exists():
                        dve.wait_ge(xn_done, 2 * e.number)
                    tile_stats(e, 0, stats1)
                if a.exists():
                    dve.wait_ge(exp_done, 2 * a.number + 2)
                    if z.exists():
                        dve.wait_ge(res_done, 2 * a.number)
                    v.reciprocal(inv[:], sums[a.slot][:]).then_inc(inv_done, 1)
                if e.exists():
                    mean_variance(e, 0, stats1, aggr1)
                if a.exists():
                    dve.wait_ge(inv_done, 2 * a.number + 1)
                    v.tensor_scalar(inv[:], inv[:], gates[:, 1:2], None, ALU.mult).then_inc(inv_done, 1)
                if z.exists():
                    dve.wait_ge(rstd2, 2 * z.number + 2)
                    if s.shift(-4).exists():
                        dve.wait_ge(table_out[z.slot], 16 * z.turns)
                    for t in range(TILES):
                        v.tensor_scalar(y[z.slot][:, t], tile(z, t), mean_var[:, 1, t, 0:1],
                                        rstd[:, 1, t:t + 1], ALU.subtract, ALU.mult).then_inc(y_done, 1)
                if c.exists():
                    dve.wait_ge(s_ready, c.number + 1)
                    if a.exists():
                        dve.wait_ge(exp_done, 2 * c.number)
                    v.tensor_tensor(scores[:], ps_s[:, 0:KEYS], causal[:], ALU.add).then_inc(s_done, 1)
                    dve.wait_ge(s_done, c.number + 1)
                    for t, keys in ((0, slice(0, P)), (1, slice(P, KEYS))):
                        v.tensor_reduce(neg_max[:, t:t + 1], scores[:, keys], AX_X, ALU.max, negate=True
                                        ).then_inc(max_done, 1)
                if e.exists():
                    dve.wait_ge(rstd1, 2 * e.number + 2)
                    if c.exists():
                        dve.wait_ge(x_turned, c.number + 1)
                    for t in range(TILES):
                        v.tensor_scalar(xn[:, t], tile(e, t), mean_var[:, 0, t, 0:1],
                                        rstd[:, 0, t:t + 1], ALU.subtract, ALU.mult).then_inc(xn_done, 1)
                if a.exists():
                    dve.wait_ge(inv_done, 2 * a.number + 2)
                    dve.wait_ge(v_ready, a.number + 1)
                    for t in range(TILES):
                        v.scalar_tensor_tensor(tile(a, t), ps_v[:, t], inv[:, t:t + 1], tile(a, t),
                                               ALU.mult, ALU.add).then_inc(res_done, 1)
                if a.exists():
                    dve.wait_ge(res_done, 2 * a.number + 2)
                    if z.exists():
                        dve.wait_ge(y_done, 2 * a.number)
                    tile_stats(a, 1, stats2)
                if a.exists():
                    mean_variance(a, 1, stats2, aggr2)

            pipeline(dve, step, FIRST, LAST, *STEADY)

        @block.scalar
        def _(act):
            s_ = nc.scalar

            def step(s):
                a, c, e, z = stages(s)
                if c.exists():
                    act.wait_ge(x_turned, c.number + 1)
                    if a.exists():
                        act.wait_ge(s_ready, c.number)
                    s_.activation(xn_t[:], ps_x[:], ACT.Copy, scale=float(D) ** -0.5).then_inc(x_out, 1)
                if a.exists():
                    act.wait_ge(p_turned, a.number + 1)
                    if z.exists():
                        act.wait_ge(v_ready, a.number)
                    s_.copy(probs_t[:], ps_p[:, 0:KEYS]).then_inc(p_out, 1)
                if z.exists():
                    act.wait_ge(y_turned, z.number + 1)
                    if s.shift(-2).exists():
                        act.wait_ge(l_ready, z.number)
                    s_.copy(y_t[:], ps_y[:]).then_inc(y_out, 1)
                if c.exists():
                    if s.shift(-2).exists():
                        act.wait_ge(p_turned, c.number - 2)
                        act.wait_ge(inv_done, 2 * c.number - 4)
                    for t, keys in ((0, slice(0, P)), (1, slice(P, KEYS))):
                        act.wait_ge(max_done, 2 * c.number + t + 1)
                        s_.activation(probs[c.slot][:, keys], scores[:, keys], ACT.Exp,
                                      bias=neg_max[:, t:t + 1], accum_out=sums[c.slot][:, t:t + 1]
                                      ).then_inc(exp_done, 1)
                if z.exists():
                    act.wait_ge(l_ready, z.number + 1)
                    s_.copy(logits[:, :, bass.ds(z.number * TILES, TILES)].rearrange("p e t -> p t e"),
                            ps_l[:]).then_inc(l_out, 1)

            pipeline(act, step, FIRST, LAST, *STEADY)

        @block.tensor
        def _(pe):
            t_ = nc.tensor
            pe.wait_ge(pool_consts, 3)
            pe.wait_ge(w_in, 16)

            def turn(dst, src):
                for t in range(TILES):
                    for k in range(2):
                        mm = t_.transpose(dst[:, k, t * P:(t + 1) * P], src[:, t, k * P:(k + 1) * P],
                                          ident[:])
                return mm

            def step(s):
                a, c, e, z = stages(s)
                if c.exists():
                    pe.wait_ge(xn_done, 2 * c.number + 2)
                    if a.exists():
                        pe.wait_ge(x_out, c.number)
                    turn(ps_x, xn).then_inc(x_turned, 1)
                if a.exists():
                    pe.wait_ge(exp_done, 2 * a.number + 2)
                    if z.exists():
                        pe.wait_ge(p_out, a.number)
                    for i in range(3):
                        mm = t_.transpose(ps_p[:, i * P:(i + 1) * P], probs[a.slot][:, i * P:(i + 1) * P],
                                          ident[:])
                    mm.then_inc(p_turned, 1)
                if c.exists():
                    pe.wait_ge(x_out, c.number + 1)
                    pe.wait_ge(ctx_t_in[c.slot], 16 * (c.turns + 1))
                    if a.exists():
                        pe.wait_ge(s_done, c.number)
                    for t, keys in ((0, slice(0, P)), (1, slice(P, KEYS))):
                        for k in range(2):
                            mm = t_.matmul(ps_s[:, keys], xn_t[:, k, t * P:(t + 1) * P],
                                           ctx_t[c.slot][:, k, 0:(t + 1) * P], start=k == 0, stop=k == 1)
                    mm.then_inc(s_ready, 1)
                if z.exists():
                    pe.wait_ge(y_done, 2 * z.number + 2)
                    if s.shift(-2).exists():
                        pe.wait_ge(y_out, z.number)
                    turn(ps_y, y[z.slot]).then_inc(y_turned, 1)
                if a.exists():
                    pe.wait_ge(p_out, a.number + 1)
                    pe.wait_ge(ctx_n_in[a.slot], 16 * (a.turns + 1))
                    if z.exists():
                        pe.wait_ge(res_done, 2 * a.number)
                    t_.matmul(ps_v[:, 0], probs_t[:, 0:P], ctx_n[a.slot][:, 0], start=True, stop=True)
                    for k in range(2):
                        mm = t_.matmul(ps_v[:, 1], probs_t[:, (1 + k) * P:(2 + k) * P],
                                       ctx_n[a.slot][:, k], start=k == 0, stop=k == 1)
                    mm.then_inc(v_ready, 1)
                if z.exists():
                    pe.wait_ge(y_out, z.number + 1)
                    if s.shift(-2).exists():
                        pe.wait_ge(l_out, z.number)
                    for t in range(TILES):
                        for k in range(2):
                            mm = t_.matmul(ps_l[:, t], y_t[:, k, t * P:(t + 1) * P], gate_w[:, k],
                                           start=k == 0, stop=k == 1)
                    mm.then_inc(l_ready, 1)

            pipeline(pe, step, FIRST, LAST, *STEADY)


def routing(nc, dram, passed, gates, logits, gather_rows, scatter_rows):
    with ExitStack() as ctx:
        def sb(name, shape, dt=F32):
            return ctx.enter_context(nc.sbuf_tensor("r_" + name, shape, dt))

        sem = phase_semaphores(nc, ctx, "r")

        N = EXPERTS * ALL_TILES
        DIGIT = 16
        GROUP = P // DIGIT
        GROUPS = EXPERTS // GROUP
        TGROUP = 8
        TGROUPS = ALL_TILES // TGROUP
        BLOCK = 8
        BLOCKS = ALL_TILES // BLOCK
        NONE = 4096.0
        probs = sb("probs", [P, EXPERTS, ALL_TILES])
        mine = [sb(f"mine{u}", [P, TGROUP, EXPERTS]) for u in range(2)]
        mine_top = [sb(f"mine_top{u}", [P, TGROUP, TOPK]) for u in range(2)]
        mine_rest = [sb(f"mine_rest{u}", [P, TGROUP, EXPERTS]) for u in range(2)]
        top = sb("top", [P, ALL_TILES, TOPK])
        row = sb("row", [P, 2, ALL_TILES])
        chosen = sb("chosen", [P, EXPERTS, ALL_TILES], BF16)
        weights = sb("weights", [P, ALL_TILES, EXPERTS])
        restart = sb("restart", [P, EXPERTS, ALL_TILES], BF16)
        before = sb("before", [P, N])
        place = sb("place", [P, N], I32)
        digit = sb("digit", [P, N], I32)
        high = sb("high", [P, EXPERTS, ALL_TILES], BF16)
        low = sb("low", [P, EXPERTS, ALL_TILES], BF16)
        lower = sb("lower", [P, P], BF16)
        ones = sb("ones", [P, P], BF16)
        zeros = sb("zeros", [P, 512], BF16)
        digits_i = sb("digits_i", [P, EXPERTS, DIGIT], I32)
        digits = sb("digits", [P, EXPERTS, DIGIT], BF16)
        token_i = sb("token_i", [P, 1], I32)
        token = sb("token", [P, 1])
        tile_i = sb("tile_i", [P, ALL_TILES], I32)
        tile_base = sb("tile_base", [P, ALL_TILES])
        is_high = [sb(f"is_high{u}", [P, EXPERTS, DIGIT], BF16) for u in range(2)]
        is_low = [sb(f"is_low{u}", [P, EXPERTS, DIGIT], BF16) for u in range(2)]
        low_token = [sb(f"low_token{u}", [P, EXPERTS, DIGIT], BF16) for u in range(2)]
        low_tile = [sb(f"low_tile{u}", [P, EXPERTS, DIGIT], BF16) for u in range(2)]
        own = sb("own", [P, GROUP, DIGIT])
        crossed = sb("crossed", [P, GROUPS, GROUP, DIGIT])
        least = sb("least", [P, BLOCKS])
        open_blocks = sb("open_blocks", [P, BLOCKS], I32)
        found = sb("found", [P, GROUPS, DIGIT])
        by_half = sb("by_half", [2 * EXPERTS, P])
        ident = sb("ident", [P, P])
        empty = sb("empty", [P, 2 * EXPERTS])
        shifted = sb("shifted", [P, 2 * EXPERTS])
        PC = min(N, 512)
        ps_rank = ctx.enter_context(nc.psum_tensor("r_ps_rank", [P, 2048], F32))
        ps_total = ctx.enter_context(nc.psum_tensor("r_ps_total", [P, 2048], F32))
        ps_rows = ps_total[:, 0:512]
        ps_turn = ps_total[:, 512:512 + 2 * EXPERTS]

        steps, consts, pool_consts = sem("steps"), sem("consts"), sem("pool_consts")
        shifted_done, exp_done = sem("shifted_done"), sem("exp_done")
        top_done, replaced, chosen_done = sem("top_done"), sem("replaced"), sem("chosen_done")
        weights_done, weights_out = sem("weights_done"), sem("weights_out")
        ranked, place_read, digits_done = sem("ranked"), sem("place_read"), sem("digits_done")
        cleared, high_done, low_done, spread = sem("cleared"), sem("high_done"), sem("low_done"), sem("spread")
        summed, found_done, found_out = sem("summed"), sem("found_done"), sem("found_out")
        turned, rows_done = sem("turned"), sem("rows_done")
        blocks_known = sem("blocks_known")
        probs_done, mine_in, top_out = sem("probs_done"), sem("mine_in"), sem("top_out")
        flat = "p e t -> p (e t)"

        def in_groups(eng, work):
            for g in range(2):
                work(g, g, True)
            with eng.Fori(1, TGROUPS // 2, 1) as it:
                for u in range(2):
                    work(it * 2 + u, u, False)

        block = ctx.enter_context(nc.Block())

        @block.gpsimd
        def _(pool):
            g = nc.gpsimd
            g.iota(digits_i[:], pattern=[[0, EXPERTS], [1, DIGIT]], base=0, channel_multiplier=0
                   ).then_inc(pool_consts, 1)
            g.iota(token_i[:], pattern=[[0, 1]], base=1, channel_multiplier=1).then_inc(pool_consts, 1)
            g.iota(tile_i[:], pattern=[[P, ALL_TILES]], base=0, channel_multiplier=0
                   ).then_inc(pool_consts, 1)
            pool.wait_ge(consts, 5)
            g.affine_select(out=lower[:], in_=lower[:], compare_op=ALU.is_gt, fill=0.0, base=0,
                            pattern=[[1, P]], channel_multiplier=-1).then_inc(pool_consts, 1)
            g.affine_select(out=ident[:], in_=ident[:], compare_op=ALU.not_equal, fill=1.0, base=0,
                            pattern=[[-1, P]], channel_multiplier=1).then_inc(pool_consts, 1)
            g.affine_select(out=own[:], in_=own[:], compare_op=ALU.is_ge, fill=0.0, base=0,
                            pattern=[[-DIGIT, GROUP], [0, DIGIT]], channel_multiplier=1
                            ).then_inc(pool_consts, 1)
            pool.wait_ge(pool_consts, 6)
            g.affine_select(out=own[:], in_=own[:], compare_op=ALU.is_ge, fill=0.0, base=DIGIT - 1,
                            pattern=[[DIGIT, GROUP], [0, DIGIT]], channel_multiplier=-1
                            ).then_inc(pool_consts, 1)

        @block.sync
        def _(sp):
            sp.wait_ge(weights_done, 1)
            sp.dma_start(dram["table"][1:TOKENS + 1, D:D + EXPERTS].rearrange("(t p) e -> p t e", p=P),
                         weights[:]).then_inc(weights_out, 16)
            sp.wait_ge(found_done, 1)
            sp.dma_start(dram["places"].rearrange("(g p l) -> p g l", g=GROUPS, l=DIGIT), found[:]
                         ).then_inc(found_out, 16)
            sp.wait_ge(found_out, 16)
            sp.dma_start(by_half[:], dram["places"].rearrange("(h p) -> h p", p=P)).then_inc(found_out, 16)
            sp.wait_ge(weights_out, 16)

        @block.scalar
        def _(act):
            is_open = act.alloc_register("act_is_open")
            act.wait_ge(shifted_done, 1)
            nc.scalar.activation(probs[:], probs[:], ACT.Exp).then_inc(exp_done, 1)
            act.wait_ge(probs_done, 1)

            def copy_in(g, u, first):
                if not first:
                    act.wait_ge(replaced, TGROUP * (g - 1))
                nc.scalar.copy(mine[u][:], probs[:, :, bass.ds(g * TGROUP, TGROUP)]
                               .rearrange("p e t -> p t e")).then_inc(mine_in, 1)

            def copy_out(g, u):
                act.wait_ge(top_done, TGROUP * (g + 1))
                nc.scalar.copy(top[:, bass.ds(g * TGROUP, TGROUP)], mine_top[u][:]).then_inc(top_out, 1)

            copy_in(0, 0, True)
            copy_in(1, 1, True)
            with act.Fori(0, TGROUPS // 2 - 1, 1) as it:
                for u in range(2):
                    copy_out(it * 2 + u, u)
                    copy_in(it * 2 + u + 2, u, False)
            for u in range(2):
                copy_out(TGROUPS - 2 + u, u)
            act.wait_ge(blocks_known, 1)
            with act.Fori(0, BLOCKS, 1) as it:
                act.reg_load(is_open, open_blocks[0:1, bass.ds(it, 1)])
                with act.If_ne(is_open, 0):
                    for i in range(BLOCK):
                        t, u = it * BLOCK + i, i % 2
                        act.wait_ge(low_done, t + 1)
                        nc.scalar.activation(low_token[u][:], is_low[u][:], ACT.Identity,
                                             scale=token[:, 0:1]).then_inc(spread, 1)
                        nc.scalar.activation(low_tile[u][:], is_low[u][:], ACT.Identity,
                                             scale=tile_base[:, bass.ds(t, 1)]).then_inc(spread, 1)

        @block.vector
        def _(dve):
            v = nc.vector
            is_open = dve.alloc_register("dve_is_open")
            links = 0

            def link(ins):
                nonlocal links
                links += 1
                ins.then_inc(steps, 1)
                dve.wait_ge(steps, links)

            v.memset(lower[:], 1.0).then_inc(consts, 1)
            v.memset(ones[:], 1.0).then_inc(consts, 1)
            v.memset(zeros[:], 0.0).then_inc(consts, 1)
            v.memset(ident[:], 0.0).then_inc(consts, 1)
            v.memset(own[:], 1.0).then_inc(consts, 1)
            link(v.memset(restart[:], 1.0))
            link(v.memset(restart[:, :, 0:1], 0.0))
            dve.wait_ge(pool_consts, 7)
            link(v.tensor_copy(digits[:], digits_i[:]))
            link(v.tensor_copy(token[:], token_i[:]))
            link(v.tensor_copy(tile_base[:], tile_i[:]))

            def spread_row(i):
                return row[:, i].unsqueeze(1).to_broadcast([P, EXPERTS, ALL_TILES])

            link(v.tensor_reduce(row[:, 0], logits[:].rearrange("p e t -> p t e"), AX_X, ALU.max))
            v.tensor_tensor(probs[:], logits[:], spread_row(0), ALU.subtract).then_inc(shifted_done, 1)
            dve.wait_ge(exp_done, 1)
            link(v.tensor_reduce(row[:, 0], probs[:].rearrange("p e t -> p t e"), AX_X, ALU.add))
            link(v.reciprocal(row[:, 1], row[:, 0]))
            v.tensor_tensor(probs[:], probs[:], spread_row(1), ALU.mult).then_inc(probs_done, 1)
            dve.wait_ge(probs_done, 1)
            def top_group(g, u, first):
                dve.wait_ge(mine_in, g + 1)
                if not first:
                    dve.wait_ge(top_out, g - 1)
                dve.sem_inc(passed, 1)
                for i in range(TGROUP):
                    v.max(mine_top[u][:, i], mine[u][:, i]).then_inc(top_done, 1)
                for i in range(TGROUP):
                    dve.wait_ge(top_done, TGROUP * g + i + 1)
                    dve.sem_inc(passed, 1)
                    v.match_replace(out=mine_rest[u][:, i], in_to_replace=mine_top[u][:, i],
                                    in_values=mine[u][:, i], imm_value=-1.0).then_inc(replaced, 1)
                dve.wait_ge(replaced, TGROUP * (g + 1))
                v.tensor_scalar(chosen[:, :, bass.ds(g * TGROUP, TGROUP)].rearrange("p e t -> p t e"),
                                mine_rest[u][:], 0.0, None, ALU.is_lt).then_inc(chosen_done, 1)

            in_groups(dve, top_group)
            dve.wait_ge(top_out, TGROUPS)
            link(v.tensor_reduce(row[:, 0], top[:], AX_X, ALU.add))
            link(v.reciprocal(row[:, 1], row[:, 0]))
            link(v.tensor_scalar(row[:, 1], row[:, 1], gates[:, 3:4], None, ALU.mult))
            v.tensor_tensor(weights[:], probs[:].rearrange("p e t -> p t e"),
                            row[:, 1].unsqueeze(2).to_broadcast([P, ALL_TILES, EXPERTS]), ALU.mult
                            ).then_inc(weights_done, 1)
            dve.wait_ge(ranked, 1)
            total = ps_total[:, 0:N]
            link(v.tensor_tensor_scan(before[:], restart[:].rearrange(flat), total, 0.0, ALU.mult, ALU.add))
            link(v.tensor_tensor(before[:], before[:], total, ALU.subtract))
            link(v.tensor_reduce(least[:], before[:].rearrange("p (e b t) -> p b t e", e=EXPERTS, t=BLOCK)
                                 [:, :, 0, :], AX_X, ALU.min))
            v.tensor_scalar(open_blocks[:], least[:], float(CAPACITY), None, ALU.is_lt
                            ).then_inc(blocks_known, 1)
            link(v.tensor_tensor(before[:], before[:], ps_rank[:, 0:N], ALU.add))
            dve.wait_ge(chosen_done, TGROUPS)
            link(v.scalar_tensor_tensor(before[:], chosen[:].rearrange(flat), -NONE, before[:],
                                        ALU.mult, ALU.add))
            link(v.tensor_scalar(place[:], before[:], NONE, None, ALU.add))
            link(v.tensor_single_scalar(digit[:], place[:], 4, ALU.logical_shift_right))
            link(v.tensor_copy(high[:].rearrange(flat), digit[:]))
            link(v.tensor_single_scalar(digit[:], place[:], DIGIT - 1, ALU.bitwise_and))
            v.tensor_copy(low[:].rearrange(flat), digit[:]).then_inc(digits_done, 1)
            dve.wait_ge(digits_done, 1)

            dve.wait_ge(blocks_known, 1)
            with dve.Fori(0, BLOCKS, 1) as it:
                dve.reg_load(is_open, open_blocks[0:1, bass.ds(it, 1)])
                with dve.If_ne(is_open, 0):
                    for i in range(BLOCK):
                        t, u = it * BLOCK + i, i % 2
                        dve.wait_ge(summed, t + 1)
                        v.tensor_tensor(is_low[u][:],
                                        low[:, :, bass.ds(t, 1)].to_broadcast([P, EXPERTS, DIGIT]),
                                        digits[:], ALU.is_equal).then_inc(low_done, 1)
                        v.tensor_tensor(is_high[u][:],
                                        high[:, :, bass.ds(t, 1)].to_broadcast([P, EXPERTS, DIGIT]),
                                        digits[:], ALU.is_equal).then_inc(high_done, 1)
            dve.wait_ge(summed, ALL_TILES + 2)
            link(v.tensor_tensor(crossed[:].rearrange("p g e l -> p g (e l)"),
                                 ps_rows.rearrange("p (g n) -> p g n", g=GROUPS),
                                 own[:].rearrange("p e l -> p (e l)").unsqueeze(1).to_broadcast(
                                     [P, GROUPS, P]), ALU.mult))
            v.tensor_reduce(found[:], crossed[:].rearrange("p g e l -> p g l e"), AX_X, ALU.add
                            ).then_inc(found_done, 1)
            dve.wait_ge(turned, 1)
            v.tensor_copy(gather_rows[:], ps_turn).then_inc(rows_done, 1)
            link(v.tensor_scalar(empty[:], ps_turn, 0.0, float(TOKENS + 1), ALU.is_equal, ALU.mult))
            link(v.tensor_tensor(shifted[:], empty[:], ps_turn, ALU.add))
            v.tensor_scalar(scatter_rows[:], shifted[:], -1.0, None, ALU.add).then_inc(rows_done, 1)
            dve.wait_ge(rows_done, 2)

        @block.tensor
        def _(pe):
            t_ = nc.tensor
            is_open = pe.alloc_register("pe_is_open")
            pe.wait_ge(pool_consts, 7)
            pe.wait_ge(chosen_done, TGROUPS)
            for i in range(N // PC):
                cols = chosen[:].rearrange(flat)[:, i * PC:(i + 1) * PC]
                t_.matmul(ps_rank[:, i * PC:(i + 1) * PC], lower[:], cols, start=True, stop=True)
                mm = t_.matmul(ps_total[:, i * PC:(i + 1) * PC], ones[:], cols, start=True, stop=True)
            mm.then_inc(ranked, 1)
            pe.wait_ge(digits_done, 1)
            t_.matmul(ps_rows, zeros[:, 0:P], zeros[:], start=True, stop=False, skip_group_check=True
                      ).then_inc(summed, 2)

            def add_tile(t, u):
                pe.wait_ge(high_done, t + 1)
                pe.wait_ge(spread, 2 * t + 2)
                for i in range(GROUPS):
                    mine = slice(i * GROUP, (i + 1) * GROUP)
                    for values in (low_token[u], low_tile[u]):
                        mm = t_.matmul(ps_rows[:, i * P:(i + 1) * P],
                                       is_high[u][:, mine].rearrange("p e l -> p (e l)"),
                                       values[:, mine].rearrange("p e l -> p (e l)"),
                                       start=False, stop=False, skip_group_check=True)
                mm.then_inc(summed, 1)

            pe.wait_ge(blocks_known, 1)
            with pe.Fori(0, BLOCKS, 1) as it:
                pe.reg_load(is_open, open_blocks[0:1, bass.ds(it, 1)])
                with pe.If_ne(is_open, 0):
                    for i in range(BLOCK):
                        add_tile(it * BLOCK + i, i % 2)
                with pe.Else():
                    pe.sem_inc(summed, BLOCK)
            pe.wait_ge(found_out, 32)
            t_.transpose(ps_turn, by_half[:], ident[0:2 * EXPERTS, 0:2 * EXPERTS]).then_inc(turned, 1)


def experts(nc, dram, passed, gather_rows, scatter_rows, out):
    with ExitStack() as ctx:
        def sb(name, shape, dt=F32):
            return ctx.enter_context(nc.sbuf_tensor("e_" + name, shape, dt))

        sem = phase_semaphores(nc, ctx, "e")

        def ps(name, shape, dt=F32):
            return ctx.enter_context(nc.psum_tensor("e_" + name, shape, dt))

        FH = FFN // 2
        HALVES = CAPACITY // P
        W = D + EXPERTS
        ident = sb("ident", [P, P])
        up_w = [sb(f"up_w{r}", [P, 2, 2 * FFN]) for r in range(3)]
        down_w = [sb(f"down_w{r}", [FH, 2, D]) for r in range(3)]
        rows = [sb(f"rows{r}", [P, HALVES, W]) for r in range(3)]
        rows_t = [sb(f"rows_t{r}", [P, 2, CAPACITY]) for r in range(3)]
        silu = sb("silu", [FH, 2, CAPACITY])
        hidden_t = sb("hidden_t", [FH, 2, CAPACITY])
        weight = [sb(f"weight{r}", [P, HALVES, 1]) for r in range(3)]
        y = [sb(f"y{r}", [P, HALVES, D]) for r in range(3)]
        gather_now = [sb(f"gather_now{r}", [P, HALVES], U32) for r in range(3)]
        scatter_now = [sb(f"scatter_now{r}", [P, HALVES], U32) for r in range(3)]
        ps_x = ps("ps_x", [P, 2, CAPACITY])
        ps_gate = ps("ps_gate", [FH, 2, CAPACITY])
        ps_up = ps("ps_up", [FH, 2, CAPACITY])
        ps_y = ps("ps_y", [P, HALVES, D])

        consts, ident_done = sem("consts"), sem("ident_done")
        up_in = [sem(f"up_in{r}") for r in range(3)]
        down_in = [sem(f"down_in{r}") for r in range(3)]
        gathered = [sem(f"gathered{r}") for r in range(3)]
        scattered = [sem(f"scattered{r}") for r in range(3)]
        gather_at, scatter_at = sem("gather_at"), sem("scatter_at")
        x_turned, x_out = sem("x_turned"), sem("x_out")
        gate_ready, up_ready, silu_done, hidden_done = (
            sem(n) for n in ("gate_ready", "up_ready", "silu_done", "hidden_done"))
        y_ready, weight_done, y_done = sem("y_ready"), sem("weight_done"), sem("y_done")

        FIRST, LAST = -2, EXPERTS - 1
        STEADY = (3, EXPERTS - 4)

        def stages(s):
            return s, s.shift(1), s.shift(2), s.shift(-1)

        block = ctx.enter_context(nc.Block())

        @block.sync
        def _(sp):
            def step(s):
                a, c, e, z = stages(s)
                if e.exists():
                    if z.exists():
                        sp.wait_ge(y_ready, z.number + 1)
                    sp.dma_start(up_w[e.slot][:], dram["up_w"][bass.ds(e.number, 1)].rearrange(
                        "e p c f -> p (e c) f")).then_inc(up_in[e.slot], 16)
                    sp.dma_start(down_w[e.slot][:], dram["down_w"][bass.ds(e.number, 1)].rearrange(
                        "e p c d -> p (e c) d")).then_inc(down_in[e.slot], 16)

            pipeline(sp, step, FIRST, LAST, *STEADY, count=EXPERTS)

        @block.gpsimd
        def _(pool):
            g = nc.gpsimd
            pool.wait_ge(consts, 1)
            g.affine_select(out=ident[:], in_=ident[:], compare_op=ALU.not_equal, fill=1.0, base=0,
                            pattern=[[-1, P]], channel_multiplier=1).then_inc(ident_done, 1)

            def step(s):
                a, c, e, z = stages(s)
                f = s.shift(3)
                if f.exists():
                    if a.exists():
                        pool.wait_ge(x_turned, a.number + 1)
                        pool.wait_ge(weight_done, a.number + 1)
                    pool.sem_inc(passed, 1)
                    g.tensor_copy(gather_now[f.slot][:], gather_rows[:, bass.ds(f.number * HALVES, HALVES)]
                                  ).then_inc(gather_at, 1)
                    pool.wait_ge(gather_at, f.number + 1)
                    pool.sem_inc(passed, 1)
                    for half in range(HALVES):
                        g.indirect_dma_start(rows[f.slot][:, half, :], None, dram["table"],
                                             bass.IndirectOffsetOnAxis(
                                                 gather_now[f.slot][:, half:half + 1], 0)
                                             ).then_inc(gathered[f.slot], 16)
                if a.exists():
                    if s.shift(-3).exists():
                        pool.wait_ge(scattered[a.slot], 32 * a.turns)
                    pool.sem_inc(passed, 1)
                    g.tensor_copy(scatter_now[a.slot][:], scatter_rows[:, bass.ds(a.number * HALVES, HALVES)]
                                  ).then_inc(scatter_at, 1)
                    pool.wait_ge(scatter_at, a.number + 1)
                    pool.wait_ge(y_done, 2 * a.number + 2)
                    if z.exists():
                        pool.wait_ge(scattered[z.slot], 32 * (z.turns + 1))
                    pool.sem_inc(passed, 1)
                    for half in range(HALVES):
                        g.indirect_dma_start(out, bass.IndirectOffsetOnAxis(
                                                 scatter_now[a.slot][:, half:half + 1], 0),
                                             y[a.slot][:, half, :], None, bounds_check=TOKENS - 1,
                                             oob_is_err=False, compute_op=ALU.add
                                             ).then_inc(scattered[a.slot], 16)

            pipeline(pool, step, FIRST - 1, LAST, *STEADY, count=EXPERTS)
            for r in range(3):
                pool.wait_ge(scattered[r], 32 * len(range(r, EXPERTS, 3)))

        @block.vector
        def _(dve):
            v = nc.vector
            v.memset(ident[:], 0.0).then_inc(consts, 1)

            def step(s):
                a, c, e, z = stages(s)
                if c.exists():
                    dve.wait_ge(gathered[c.slot], 32 * (c.turns + 1))
                    if s.shift(-2).exists():
                        dve.wait_ge(y_done, 2 * s.number - 2)
                    v.tensor_copy(weight[c.slot][:], rows[c.slot][:, :, bass.ds(c.number + D, 1)]
                                  ).then_inc(weight_done, 1)
                if a.exists():
                    dve.wait_ge(weight_done, a.number + 1)
                    dve.wait_ge(y_ready, a.number + 1)
                    if s.shift(-3).exists():
                        dve.wait_ge(scattered[a.slot], 32 * a.turns)
                    for half in range(HALVES):
                        v.tensor_scalar(y[a.slot][:, half], ps_y[:, half], weight[a.slot][:, half], None,
                                        ALU.mult).then_inc(y_done, 1)
                if c.exists():
                    dve.wait_ge(silu_done, c.number + 1)
                    dve.wait_ge(up_ready, c.number + 1)
                    if a.exists():
                        dve.wait_ge(y_ready, c.number)
                    v.tensor_tensor(hidden_t[:], silu[:], ps_up[:], ALU.mult).then_inc(hidden_done, 1)

            pipeline(dve, step, FIRST, LAST, *STEADY, count=EXPERTS)

        @block.scalar
        def _(act):
            s_ = nc.scalar

            def step(s):
                a, c, e, z = stages(s)
                if c.exists():
                    act.wait_ge(gate_ready, c.number + 1)
                    if a.exists():
                        act.wait_ge(hidden_done, c.number)
                    s_.activation(silu[:], ps_gate[:], ACT.Silu).then_inc(silu_done, 1)
                if e.exists():
                    act.wait_ge(x_turned, e.number + 1)
                    if z.exists():
                        act.wait_ge(up_ready, z.number + 1)
                    s_.copy(rows_t[e.slot][:], ps_x[:]).then_inc(x_out, 1)

            pipeline(act, step, FIRST, LAST, *STEADY, count=EXPERTS)

        @block.tensor
        def _(pe):
            t_ = nc.tensor
            pe.wait_ge(ident_done, 1)

            def step(s):
                a, c, e, z = stages(s)
                def first(dst, column, ready, used):
                    if c.exists():
                        if a.exists():
                            pe.wait_ge(used, c.number)
                        for m in range(2):
                            for k in range(2):
                                mm = t_.matmul(dst[:, m],
                                               up_w[c.slot][:, k, column + m * FH:column + (m + 1) * FH],
                                               rows_t[c.slot][:, k], start=k == 0, stop=k == 1)
                        mm.then_inc(ready, 1)

                if c.exists():
                    pe.wait_ge(x_out, c.number + 1)
                    pe.wait_ge(up_in[c.slot], 16 * (c.turns + 1))
                first(ps_gate, 0, gate_ready, silu_done)
                if a.exists():
                    pe.wait_ge(hidden_done, a.number + 1)
                    pe.wait_ge(down_in[a.slot], 16 * (a.turns + 1))
                    if z.exists():
                        pe.wait_ge(y_done, 2 * a.number)
                    for half in range(HALVES):
                        for k in range(2):
                            mm = t_.matmul(ps_y[:, half], hidden_t[:, k, half * P:(half + 1) * P],
                                           down_w[a.slot][:, k], start=k == 0, stop=k == 1)
                    mm.then_inc(y_ready, 1)
                if e.exists():
                    pe.wait_ge(gathered[e.slot], 32 * (e.turns + 1))
                    if c.exists():
                        pe.wait_ge(x_out, c.number + 1)
                    for half in range(HALVES):
                        for k in range(2):
                            mm = t_.transpose(ps_x[:, k, half * P:(half + 1) * P],
                                              rows[e.slot][:, half, k * P:(k + 1) * P], ident[:])
                    mm.then_inc(x_turned, 1)
                first(ps_up, FFN, up_ready, hidden_done)

            pipeline(pe, step, FIRST, LAST, *STEADY, count=EXPERTS)


def program(nc, dram, out):
    with ExitStack() as ctx:
        x_res = ctx.enter_context(nc.sbuf_tensor("x_res", [P, BATCHES * ROW], F32))
        gates = ctx.enter_context(nc.sbuf_tensor("gates", [P, 4], F32))
        gates_in = ctx.enter_context(nc.semaphore("gates_in"))
        gates_done = ctx.enter_context(nc.semaphore("gates_done"))
        passed = ctx.enter_context(nc.semaphore("passed"))
        with nc.Block() as block:
            @block.sync
            def _(sp):
                sp.dma_start(gates[:], dram["gates"].partition_broadcast(P)).then_inc(gates_in, 16)

            @block.scalar
            def _(act):
                act.wait_ge(gates_in, 16)
                nc.scalar.activation(gates[:], gates[:], ACT.Tanh).then_inc(gates_done, 1)
                act.wait_ge(gates_done, 1)
        cross_attention(nc, dram, passed, x_res, gates)
        ternary_ffn(nc, dram, passed, x_res, gates)
        logits = ctx.enter_context(nc.sbuf_tensor("logits", [P, EXPERTS, ALL_TILES], F32))
        gather_rows = ctx.enter_context(nc.sbuf_tensor("gather_rows", [P, 2 * EXPERTS], U32))
        scatter_rows = ctx.enter_context(nc.sbuf_tensor("scatter_rows", [P, 2 * EXPERTS], U32))
        causal_attention(nc, dram, passed, x_res, gates, logits, out)
        routing(nc, dram, passed, gates, logits, gather_rows, scatter_rows)
        experts(nc, dram, passed, gather_rows, scatter_rows, out)


def kernel(**inputs):
    import numpy as np
    import concourse.bacc as bacc
    from concourse.bass_utils import run_bass_kernel_spmd

    def arr(name):
        return np.asarray(inputs[name])

    def chunks(w):
        return w.reshape(-1, P, w.shape[1]).transpose(1, 0, 2)

    def by_dim(w):
        return w.reshape(-1, HEADS, DK).transpose(0, 2, 1).reshape(w.shape)

    qk_bias = np.stack([by_dim(arr("L0_xattn_bq")), by_dim(arr("L0_xattn_bk"))])
    arrays = {
        "x": arr("x"),
        "ctx": arr("ctx_1024"),
        "ctx_t": arr("ctx_1024").transpose(0, 2, 1),
        "mask": arr("mask_Bx1xSxS2_if1").reshape(BATCHES, SEQ, SEQ),
        "gates": np.stack([arr("g_xattn"), arr("g_ffn")]).reshape(4),
        "wq": chunks(by_dim(arr("L0_xattn_Wq").T)),
        "wk": chunks(by_dim(arr("L0_xattn_Wk").T)),
        "wv": chunks(arr("L0_xattn_Wv").T),
        "wo": chunks(arr("L0_xattn_Wo").T),
        "qk_bias": qk_bias.reshape(4, P).T,
        "bv": arr("L0_xattn_bv"),
        "w1": chunks(arr("L0_ffn_w1").T),
        "b1": arr("L0_ffn_b1"),
        "w2": chunks(arr("L0_ffn_w2").T),
        "b2": arr("L0_ffn_b2"),
        "gate_w": chunks(arr("L1_ffn_gate_weight").T),
        "up_w": arr("L1_ffn_gate_up_proj").transpose(0, 2, 1).reshape(EXPERTS, 2, P, 2 * FFN)
        .transpose(0, 2, 1, 3),
        "down_w": arr("L1_ffn_down_proj").transpose(0, 2, 1).reshape(EXPERTS, 2, FFN // 2, D)
        .transpose(0, 2, 1, 3),
        "bo": arr("L0_xattn_bo"),
    }
    arrays = {k: np.ascontiguousarray(a) for k, a in arrays.items()}
    nc = bacc.Bacc("TRN2", target_bir_lowering=False, num_devices=1)
    dram = {k: nc.dram_tensor(f"in_{k}", a.shape, mybir.dt.from_np(a.dtype), kind="ExternalInput").ap()
            for k, a in arrays.items()}
    dram["parts"] = nc.dram_tensor("parts_dram", (3, 2, 3, D, SEQ), BF16, kind="Internal").ap()
    dram["table"] = nc.dram_tensor("table", (TOKENS + 1, D + EXPERTS), F32, kind="Internal").ap()
    dram["places"] = nc.dram_tensor("places", (EXPERTS * CAPACITY,), F32, kind="Internal").ap()
    out = nc.dram_tensor("out", (TOKENS, D), F32, kind="ExternalOutput").ap()
    program(nc, dram, out)
    r = run_bass_kernel_spmd(nc, [{f"in_{k}": a for k, a in arrays.items()}], core_ids=[0])
    return r.results[0]["out"].reshape(BATCHES, SEQ, D)
```
